# Optimizing a Trainium2 kernel written in Bass

```python
import numpy as np
import jax
import jax.numpy as jnp

def _softmax(x, axis=-1):
    return jax.nn.softmax(x, axis=axis)

def _gelu(x):
    return jax.nn.gelu(x, approximate=True)

def _silu(x):
    return jax.nn.silu(x)

def _sigmoid(x):
    return jax.nn.sigmoid(x)

def _layernorm(x, axis=-1, eps=1e-05):
    m = jnp.mean(x, axis=axis, keepdims=True)
    v = jnp.var(x, axis=axis, keepdims=True)
    return (x - m) / jnp.sqrt(v + eps)

def _scatter_add(tgt, idx, src, axis=0):
    return tgt.at[idx].add(src)

def _segment_sum(src, seg, n):
    return jax.ops.segment_sum(src, seg, n)
kernel_name = 'mk_gnn_preln_d2_gnn_r64_606619'

def setup_inputs(seed: int=0):
    np.random.seed(seed)
    _w = jnp.asarray

    def _rec_inputs():
        import jax
        import jax.numpy as jnp
        _gk = jax.random.key(seed)
        x = -0.000202 + 1 * jax.random.normal(jax.random.fold_in(_gk, 1), (100000, 64), jnp.float32)
        src = jax.random.randint(jax.random.fold_in(_gk, 2), (25000,), 0, 100000, jnp.int32)
        dst = jax.random.randint(jax.random.fold_in(_gk, 3), (25000,), 0, 100000, jnp.int32)
        _o = jnp.argsort(dst, stable=True)
        src = src[_o]
        dst = dst[_o]
        edge_attr_2 = -0.000622378 + 1.00003 * jax.random.normal(jax.random.fold_in(_gk, 11), (25000, 2), jnp.float32)
        edge_weight = jax.random.uniform(jax.random.fold_in(_gk, 13), (25000,), jnp.float32, 0.0, 1)
        return (x, src, dst, edge_attr_2, edge_weight)
    x, src, dst, edge_attr_2, edge_weight = _rec_inputs()

    def _L0_gnn_setup():
        import jax, jax.numpy as jnp
        import numpy as np
        N_NODES = 100000
        N_EDGES = 50000
        D_IN = 64
        D_OUT = 64
        LN_EPS = 1e-05

        def _layer_norm(h, g, b):
            m = jnp.mean(h, axis=-1, keepdims=True)
            v = jnp.mean(jnp.square(h - m), axis=-1, keepdims=True)
            return (h - m) * jax.lax.rsqrt(v + LN_EPS) * g + b
        key = jax.random.key(seed)
        ks = jax.random.split(key, 12)
        inp = {'x': jax.random.normal(ks[0], (N_NODES, D_IN), dtype=jnp.float32), 'e': jax.random.uniform(ks[1], (N_EDGES,), dtype=jnp.float32), 'edge_index': jax.random.randint(ks[2], (2, N_EDGES), 0, N_NODES, dtype=jnp.int64)}
        dims = [3 * D_IN, D_OUT, D_OUT, D_OUT, D_OUT]
        for i in range(4):
            kW = jax.random.fold_in(ks[3], i)
            scale = 1.0 / np.sqrt(dims[i])
            inp[f'W{i + 1}'] = jax.random.uniform(kW, (dims[i], dims[i + 1]), dtype=jnp.float32, minval=-scale, maxval=scale)
            inp[f'b{i + 1}'] = jnp.zeros((dims[i + 1],), dtype=jnp.float32)
            inp[f'g{i + 1}'] = jnp.ones((dims[i + 1],), dtype=jnp.float32)
            inp[f'be{i + 1}'] = jnp.zeros((dims[i + 1],), dtype=jnp.float32)
        return inp
    _L0_gnn_all = _L0_gnn_setup()
    _L0_gnn_in = {k: v for k, v in _L0_gnn_all.items() if k in ('W1', 'b1', 'g1', 'be1', 'W2', 'b2', 'g2', 'be2', 'W3', 'b3', 'g3', 'be3', 'W4', 'b4', 'g4', 'be4')}
    del _L0_gnn_all

    def _L1_gnn_setup():
        import jax, jax.numpy as jnp
        import numpy as np
        N_NODES = 512
        AGENTS = 32
        N_SAMPLES = N_NODES // AGENTS
        N_EDGES = N_SAMPLES * AGENTS * (AGENTS - 1)
        D = 64
        EDGE_DIM = 2
        Z_DIM = 2 * D + EDGE_DIM
        BN_EPS = 1e-05

        def _build_block_edge_index():
            a = np.arange(AGENTS)
            src, dst = np.meshgrid(a, a, indexing='ij')
            mask = src != dst
            src, dst = (src[mask], dst[mask])
            offs = (np.arange(N_SAMPLES) * AGENTS)[:, None]
            src = (src[None, :] + offs).reshape(-1)
            dst = (dst[None, :] + offs).reshape(-1)
            return jnp.asarray(np.stack([src, dst]), dtype=jnp.int64)

        def _cgconv(x, edge_index, edge_attr, Wf, bf, Ws, bs, gamma, beta):
            src, dst = (edge_index[0], edge_index[1])
            z = jnp.concatenate([x[dst], x[src], edge_attr], axis=-1)
            m = jax.nn.sigmoid(z @ Wf + bf) * jax.nn.softplus(z @ Ws + bs)
            agg = jax.ops.segment_sum(m, dst, num_segments=x.shape[0])
            mu = jnp.mean(agg, axis=0)
            var = jnp.var(agg, axis=0)
            agg = (agg - mu) * jax.lax.rsqrt(var + BN_EPS) * gamma + beta
            return agg + x
        key = jax.random.key(seed)
        ks = jax.random.split(key, 16)
        x = jax.random.normal(ks[0], (N_NODES, D), dtype=jnp.float32)
        edge_index = _build_block_edge_index()
        edge_attr = jax.random.normal(ks[1], (N_EDGES, EDGE_DIM), dtype=jnp.float32)
        s = 1.0 / np.sqrt(Z_DIM)
        params = {}
        for li, base in ((1, 2), (2, 8)):
            params[f'Wf{li}'] = jax.random.uniform(ks[base + 0], (Z_DIM, D), jnp.float32, -s, s)
            params[f'bf{li}'] = jax.random.uniform(ks[base + 1], (D,), jnp.float32, -s, s)
            params[f'Ws{li}'] = jax.random.uniform(ks[base + 2], (Z_DIM, D), jnp.float32, -s, s)
            params[f'bs{li}'] = jax.random.uniform(ks[base + 3], (D,), jnp.float32, -s, s)
            params[f'gamma{li}'] = jnp.ones((D,), jnp.float32)
            params[f'beta{li}'] = jnp.zeros((D,), jnp.float32)
        return {'x': x, 'edge_index': edge_index, 'edge_attr': edge_attr, **params}
    _L1_gnn_all = _L1_gnn_setup()
    _L1_gnn_in = {k: v for k, v in _L1_gnn_all.items() if k in ('Wf1', 'bf1', 'Ws1', 'bs1', 'gamma1', 'beta1', 'Wf2', 'bf2', 'Ws2', 'bs2', 'gamma2', 'beta2')}
    del _L1_gnn_all
    return {'x': x, 'src': src, 'dst': dst, 'edge_attr_2': edge_attr_2, 'edge_weight': edge_weight, 'L0_gnn_W1': _L0_gnn_in['W1'], 'L0_gnn_b1': _L0_gnn_in['b1'], 'L0_gnn_g1': _L0_gnn_in['g1'], 'L0_gnn_be1': _L0_gnn_in['be1'], 'L0_gnn_W2': _L0_gnn_in['W2'], 'L0_gnn_b2': _L0_gnn_in['b2'], 'L0_gnn_g2': _L0_gnn_in['g2'], 'L0_gnn_be2': _L0_gnn_in['be2'], 'L0_gnn_W3': _L0_gnn_in['W3'], 'L0_gnn_b3': _L0_gnn_in['b3'], 'L0_gnn_g3': _L0_gnn_in['g3'], 'L0_gnn_be3': _L0_gnn_in['be3'], 'L0_gnn_W4': _L0_gnn_in['W4'], 'L0_gnn_b4': _L0_gnn_in['b4'], 'L0_gnn_g4': _L0_gnn_in['g4'], 'L0_gnn_be4': _L0_gnn_in['be4'], 'L1_gnn_Wf1': _L1_gnn_in['Wf1'], 'L1_gnn_bf1': _L1_gnn_in['bf1'], 'L1_gnn_Ws1': _L1_gnn_in['Ws1'], 'L1_gnn_bs1': _L1_gnn_in['bs1'], 'L1_gnn_gamma1': _L1_gnn_in['gamma1'], 'L1_gnn_beta1': _L1_gnn_in['beta1'], 'L1_gnn_Wf2': _L1_gnn_in['Wf2'], 'L1_gnn_bf2': _L1_gnn_in['bf2'], 'L1_gnn_Ws2': _L1_gnn_in['Ws2'], 'L1_gnn_bs2': _L1_gnn_in['bs2'], 'L1_gnn_gamma2': _L1_gnn_in['gamma2'], 'L1_gnn_beta2': _L1_gnn_in['beta2']}

def reference(x, src, dst, edge_attr_2, edge_weight, L0_gnn_W1, L0_gnn_b1, L0_gnn_g1, L0_gnn_be1, L0_gnn_W2, L0_gnn_b2, L0_gnn_g2, L0_gnn_be2, L0_gnn_W3, L0_gnn_b3, L0_gnn_g3, L0_gnn_be3, L0_gnn_W4, L0_gnn_b4, L0_gnn_g4, L0_gnn_be4, L1_gnn_Wf1, L1_gnn_bf1, L1_gnn_Ws1, L1_gnn_bs1, L1_gnn_gamma1, L1_gnn_beta1, L1_gnn_Wf2, L1_gnn_bf2, L1_gnn_Ws2, L1_gnn_bs2, L1_gnn_gamma2, L1_gnn_beta2):
    import jax
    import jax.numpy as jnp

    def _L0_gnn_ref(x, e, edge_index, W1, b1, g1, be1, W2, b2, g2, be2, W3, b3, g3, be3, W4, b4, g4, be4):
        import jax, jax.numpy as jnp
        import numpy as np
        N_NODES = 100000
        N_EDGES = 50000
        D_IN = 64
        D_OUT = 64
        LN_EPS = 1e-05

        def _layer_norm(h, g, b):
            m = jnp.mean(h, axis=-1, keepdims=True)
            v = jnp.mean(jnp.square(h - m), axis=-1, keepdims=True)
            return (h - m) * jax.lax.rsqrt(v + LN_EPS) * g + b
        start, end = (edge_index[0], edge_index[1])
        n = x.shape[0]
        ew = e[:, None]
        mi = jax.ops.segment_sum(ew * x[start], end, num_segments=n)
        mo = jax.ops.segment_sum(ew * x[end], start, num_segments=n)
        h = jnp.concatenate([mi, mo, x], axis=1)
        for W, b, g, be in ((W1, b1, g1, be1), (W2, b2, g2, be2), (W3, b3, g3, be3), (W4, b4, g4, be4)):
            h = jnp.tanh(_layer_norm(h @ W + b, g, be))
        return h

    def _L1_gnn_ref(x, edge_index, edge_attr, Wf1, bf1, Ws1, bs1, gamma1, beta1, Wf2, bf2, Ws2, bs2, gamma2, beta2):
        import jax, jax.numpy as jnp
        import numpy as np
        N_NODES = 512
        AGENTS = 32
        N_SAMPLES = N_NODES // AGENTS
        N_EDGES = N_SAMPLES * AGENTS * (AGENTS - 1)
        D = 64
        EDGE_DIM = 2
        Z_DIM = 2 * D + EDGE_DIM
        BN_EPS = 1e-05

        def _build_block_edge_index():
            a = np.arange(AGENTS)
            src, dst = np.meshgrid(a, a, indexing='ij')
            mask = src != dst
            src, dst = (src[mask], dst[mask])
            offs = (np.arange(N_SAMPLES) * AGENTS)[:, None]
            src = (src[None, :] + offs).reshape(-1)
            dst = (dst[None, :] + offs).reshape(-1)
            return jnp.asarray(np.stack([src, dst]), dtype=jnp.int64)

        def _cgconv(x, edge_index, edge_attr, Wf, bf, Ws, bs, gamma, beta):
            src, dst = (edge_index[0], edge_index[1])
            z = jnp.concatenate([x[dst], x[src], edge_attr], axis=-1)
            m = jax.nn.sigmoid(z @ Wf + bf) * jax.nn.softplus(z @ Ws + bs)
            agg = jax.ops.segment_sum(m, dst, num_segments=x.shape[0])
            mu = jnp.mean(agg, axis=0)
            var = jnp.var(agg, axis=0)
            agg = (agg - mu) * jax.lax.rsqrt(var + BN_EPS) * gamma + beta
            return agg + x
        h = jax.nn.relu(_cgconv(x, edge_index, edge_attr, Wf1, bf1, Ws1, bs1, gamma1, beta1))
        out = jax.nn.relu(_cgconv(h, edge_index, edge_attr, Wf2, bf2, Ws2, bs2, gamma2, beta2))
        return out
    edge_index = jnp.stack([src, dst])
    h = jnp.maximum(_layernorm(x, axis=-1), 0.0)
    x = x + _L0_gnn_ref(h, edge_weight, edge_index, L0_gnn_W1, L0_gnn_b1, L0_gnn_g1, L0_gnn_be1, L0_gnn_W2, L0_gnn_b2, L0_gnn_g2, L0_gnn_be2, L0_gnn_W3, L0_gnn_b3, L0_gnn_g3, L0_gnn_be3, L0_gnn_W4, L0_gnn_b4, L0_gnn_g4, L0_gnn_be4)
    h = jnp.maximum(_layernorm(x, axis=-1), 0.0)
    x = x + _L1_gnn_ref(h, edge_index, edge_attr_2, L1_gnn_Wf1, L1_gnn_bf1, L1_gnn_Ws1, L1_gnn_bs1, L1_gnn_gamma1, L1_gnn_beta1, L1_gnn_Wf2, L1_gnn_bf2, L1_gnn_Ws2, L1_gnn_bs2, L1_gnn_gamma2, L1_gnn_beta2)
    return x

_drawn_inputs = setup_inputs


def setup_inputs(seed=0):
    import zlib

    import numpy as np

    out = dict(_drawn_inputs(seed))
    spreads = {'L0_gnn_b1': (0.0, 0.1),
     'L0_gnn_g1': (1.0, 0.2),
     'L0_gnn_be1': (0.0, 0.1),
     'L0_gnn_b2': (0.0, 0.1),
     'L0_gnn_g2': (1.0, 0.2),
     'L0_gnn_be2': (0.0, 0.1),
     'L0_gnn_b3': (0.0, 0.1),
     'L0_gnn_g3': (1.0, 0.2),
     'L0_gnn_be3': (0.0, 0.1),
     'L0_gnn_b4': (0.0, 0.1),
     'L0_gnn_g4': (1.0, 0.2),
     'L0_gnn_be4': (0.0, 0.1),
     'L1_gnn_gamma1': (1.0, 0.2),
     'L1_gnn_beta1': (0.0, 0.29),
     'L1_gnn_gamma2': (1.0, 0.2),
     'L1_gnn_beta2': (0.0, 0.322)}
    factors = {'L1_gnn_bf1': 8.0, 'L1_gnn_bs1': 31.434, 'L1_gnn_bf2': 8.0, 'L1_gnn_bs2': 30.031}
    for name, (base, spread) in spreads.items():
        noise = np.random.default_rng([zlib.crc32(name.encode()), seed]).standard_normal(out[name].shape)
        drawn = base * np.exp(spread * noise) if base else spread * noise
        out[name] = jnp.asarray(drawn.astype(out[name].dtype))
    for name, factor in factors.items():
        out[name] = (out[name] * factor).astype(out[name].dtype)
    return out
```

```python
import concourse.bass as bass
from concourse import mybir
from contextlib import ExitStack

F32 = mybir.dt.float32
BF16 = mybir.dt.bfloat16
I32 = mybir.dt.int32
ALU = mybir.AluOpType
ACT = mybir.ActivationFunctionType
AX = mybir.AxisListType

N, E, D = 100000, 25000, 64
P = 125
NCOL, ECOL = N // P, E // P
GC = 8
W = GC * D
GT = 4
EG = ECOL // GT
Q = 4
NR = NCOL // (GC * Q)
SPARE = 2 * P
ZC = NR
ZR = 32 * ZC
NT = 128 * ZR
EPS = 1e-5
LAYERS = 4
BLK = 32
NB = NCOL // BLK
KA, KB = 112, P - 112
MAGIC = float(0x5F3759DF)


def wait(eng, sem, value):
    if isinstance(value, int) and value <= 0:
        return
    eng.wait_ge(sem, value)


def past(n, k):
    return not isinstance(n, int) or n >= k


class Steps:

    def __init__(self, eng, sem):
        self.eng, self.sem, self.base, self.start, self.count, self.per, self.groups = eng, sem, 0, 0, 0, 0, 0

    def begin(self, n):
        if self.groups == 1:
            self.per = self.count
        self.groups += 1
        if isinstance(n, int) and n == 0:
            self.start = self.base
        else:
            self.start = n * self.per + self.base
        self.count = 0

    def phase(self):
        self.base = self.start + self.count
        self.start, self.count, self.groups = self.base, 0, 0

    def __call__(self, ins):
        self.count += 1
        ins.then_inc(self.sem, 1)
        self.eng.wait_ge(self.sem, self.start + self.count)


def by_pairs(eng, total, body, ahead=1):
    body(0, 0)
    body(1, 1)
    end = 2 * ((total - ahead) // 2)
    with eng.Fori(1, end // 2) as h:
        body(2 * h, 0)
        body(2 * h + 1, 1)
    for g in range(end, total):
        body(g, g % 2)


def one_behind(eng, total, front, back):
    def body(g, parity):
        front(g, parity)
        if past(g, 1):
            back(g - 1, 1 - parity)

    by_pairs(eng, total, body)
    back(total - 1, (total - 1) % 2)


def gnn_kernel(nc, x, src, dst, attr, ew, mlp, conv, out, y_tab, x1_tab, agg_tab):
    ctx = ExitStack()
    with ctx:
        def sb(name, shape, dt=F32):
            return ctx.enter_context(nc.sbuf_tensor(name, shape, dt))

        def sem(name):
            return ctx.enter_context(nc.semaphore(name))

        def nodes(t):
            return t[0:N, :].rearrange("(p c) d -> p (c d)", p=P)

        x_v, out_v, y_v, x1_v = nodes(x), nodes(out), nodes(y_tab), nodes(x1_tab)
        agg_v = [nodes(a) for a in agg_tab]

        ident = sb("ident", [128, 128])
        ones = sb("ones", [128, 128])
        ones3 = sb("ones3", [3, 128], BF16)
        below = sb("below", [P, 2, P])
        spare = sb("spare", [P, 2, GT])
        spare_i = sb("spare_i", [P, 2, GT], I32)
        zeros = sb("zeros", [128, ZR // ZC * D])
        w_raw = sb("w_raw", [128, 5, D])
        w_sum = sb("w_sum", [128, 5])
        w_mean = sb("w_mean", [128, 5])
        w_cen = sb("w_cen", [128, 5, D])
        w_blk = sb("w_blk", [128, LAYERS, 128])
        b_raw = sb("b_raw", [3, LAYERS, D])
        b_sum = sb("b_sum", [3, LAYERS])
        b_mean = sb("b_mean", [3, LAYERS])
        b_cen = sb("b_cen", [3, LAYERS, D])
        b_part = sb("b_part", [3, 3, LAYERS, D], BF16)
        b_rest = sb("b_rest", [3, 2, LAYERS, D])
        b_sel = sb("b_sel", [3, 3, LAYERS, D])
        b_row = sb("b_row", [3, LAYERS, GC, D], BF16)
        gain = sb("gain", [128, LAYERS])
        shift = sb("shift", [128, LAYERS])
        w_fs = sb("w_fs", [128, 2, 128])
        w_at = sb("w_at", [3 * GT, 2, GT * 128])
        bn_gb = sb("bn_gb", [P, 2, 2, D])
        end_i = sb("end_i", [P, 2, ECOL], I32)
        end_f = sb("end_f", [P, 2, ECOL])
        ew_s = sb("ew_s", [P, ECOL])
        at_s = sb("at_s", [P, ECOL, 2])
        to_i = sb("to_i", [P, ECOL], I32)
        g_idx = sb("g_idx", [P, 2, 2, GT], I32)
        s_idx = sb("s_idx", [P, 2, 2, GT], I32)
        e_key = sb("e_key", [P, 2, 2, GT])
        e_at = sb("e_at", [P, 2, GT, 3])
        rows = sb("rows", [P, 2, GT, 2, D])
        xc = sb("xc", [P, 2, W])
        sq = sb("sq", [P, 2, W])
        tiny = sb("tiny", [P, 2, 8, GC])
        hw = sb("hw", [P, 2, GT, 2, D])
        same = sb("same", [P, 2, 2, 2 * P])
        junk = sb("junk", [P, 2 * P])
        repeat = sb("repeat", [P, 2, 2, GT])
        r_tmp = sb("r_tmp", [P, 2, 2, 2, GT])
        s_t = sb("s_t", [128, 2, 2 * P])
        vals = sb("vals", [P, 2, GT, 2, D])
        area = sb("area", [128, EG * W])
        views = {}
        at = [0]

        def carve(name, n, width):
            views[name] = [area[:, at[0] + k * width:at[0] + (k + 1) * width] for k in range(n)]
            at[0] += n * width

        carve("x_in", 2 * Q, W)
        carve("y_in", 2 * Q, W)
        carve("x_cen", Q, W)
        carve("x_sq", Q, W)
        carve("x_nrm", Q, W)
        carve("z_sq", Q, W)
        carve("z_nrm", Q, W)
        carve("h_t", Q, W)
        carve("x_out", Q, W)
        at_m = at[0]
        at[0] = 0
        for name in ("l_x1", "l_a1", "l_a2", "l_xc", "l_sq", "l_a", "l_out"):
            carve(name, 2 if name in ("l_x1", "l_a1", "l_a2", "l_out") else 1, BLK * D)
        assert max(at[0], at_m) <= EG * W
        x_in, y_in, x_cen, x_sq, x_nrm, z_sq, z_nrm, h_t, x_out = (
            views[k] for k in ("x_in", "y_in", "x_cen", "x_sq", "x_nrm", "z_sq", "z_nrm", "h_t", "x_out"))
        l_x1, l_a1, l_a2, l_xc, l_sq, l_a, l_out = (
            views[k] for k in ("l_x1", "l_a1", "l_a2", "l_xc", "l_sq", "l_a", "l_out"))
        h_keep = area
        m_stat = sb("m_stat", [P, 2, Q, 4, GC])
        half = sb("half", [P, GC])
        zt = sb("zt", [128, W])
        at_t = sb("at_t", [3 * GT, 2, P])
        act_e = sb("act_e", [P, 4, GT, D])
        dve_e = sb("dve_e", [P, 3, GT, D])
        bn_w = sb("bn_w", [P, 10, D])
        f_stat = sb("f_stat", [P, 5, BLK])
        blk_s = sb("blk", [128, 2, BLK * D])
        blk = [blk_s[:, k, :] for k in range(2)]
        msg = sb("msg", [P, 2, GT, D])
        bn_x = sb("bn_x", [128, 8, 128])
        bn_s = sb("bn_s", [P, 2, 2, D])
        psum = [ctx.enter_context(nc.psum_tensor(f"bank{k}", [128, 512], F32)) for k in range(8)]

        names = """act_step pool_passed w_zero edges_ready w_ready consts iota_done loads_edges loads_w w_copied setup_done zero_tile y_clear agg_clear dve_step
            idx_ready key_ready a_rows0 a_rows1 a_xc a_sq a_hw a_r a_same a_t a_ts a_v a_vals a_sidx a_scattered
            m_in0 m_in1 m_in2 m_in3 m_in4 m_in5 m_in6 m_in7 m_mean m_xcen m_xsq m_xss m_var m_xrstd m_xnrm m_xt
            m_hin m_z m_zsq m_zss m_zvar m_rstd m_zn m_zt m_h m_back m_out m_stored0 m_stored1 m_stored2 m_stored3
            c_idx c_slots c_rows0 c_rows1 c_xc c_sq c_hw c_keep c_r c_same c_ht c_zt c_att c_atc c_z c_act c_msg
            c_v c_vals c_sidx c_scattered dve_back d_in0 d_in1 d_used d_gram bn_ready bn_sum bn_done
            f_in0 f_in1 f_mean f_xc f_sq f_a f_out f_stored0 f_stored1""".split()
        S = {name: sem(name) for name in names}
        block = ctx.enter_context(nc.Block())

        def halves(eng, dst_ap, src_ap, done):
            eng.dma_start(dst_ap[0:KA], src_ap[0:KA]).then_inc(done, 16)
            eng.dma_start(dst_ap[KA:P], src_ap[KA:P]).then_inc(done, 16)

        def b8(ap):
            return ap.unsqueeze(2).to_broadcast([ap.shape[0], ap.shape[1], D])

        def cols(ap):
            return ap.rearrange("p (c d) -> p c d", d=D)

        N_ZERO = 16 * ZC
        SETUP_POOL = 6
        N_LOADS_W = 1 + LAYERS * 7 + 2 * (2 * (1 + 2 * GT) + 2)
        D_PER = (32 * (NB - NB // 2), 32 * (NB // 2))

        @block.sync
        def _(sp):
            for e, v in ((0, dst), (1, src)):
                halves(sp, end_i[0:P, e, :], v.rearrange("(p t) -> p t", p=P), S["loads_edges"])
            halves(sp, ew_s[0:P, :], ew.rearrange("(p t) -> p t", p=P), S["loads_edges"])
            halves(sp, at_s[0:P, :, :], attr.rearrange("(p t) k -> p t k", p=P), S["loads_edges"])

            def clear(tab, k, done):
                v = tab.rearrange("(p c) d -> p (c d)", p=128)
                w = ZR // ZC * D
                sp.dma_start(v[:, bass.ds(k * w, w)], zeros[:, :]).then_inc(done, 16)

            sp.wait_ge(S["zero_tile"], 1)
            for k in range(ZC):
                clear(y_tab, k, S["y_clear"])

            def load_round(r, v):
                for q in range(Q):
                    wait(sp, S["m_out"], Q * (r - 2) + q + 1 if not isinstance(r, int) or r >= 2 else 0)
                    col = (r * Q + q) * W
                    halves(sp, x_in[v * Q + q], x_v[:, bass.ds(col, W)], S[f"m_in{v * Q + q}"])
                    halves(sp, y_in[v * Q + q], y_v[:, bass.ds(col, W)], S[f"m_in{v * Q + q}"])

            sp.wait_ge(S["a_scattered"], 32 * ECOL)
            load_round(0, 0)

            def mlp_round(r, v):
                if not isinstance(r, int) or r + 1 < NR:
                    load_round(r + 1, 1 - v)
                for q in range(Q):
                    sp.wait_ge(S["m_out"], Q * r + q + 1)
                    halves(sp, x1_v[:, bass.ds((r * Q + q) * W, W)], x_out[q], S[f"m_stored{q}"])
                for tab in agg_tab:
                    clear(tab, r, S["agg_clear"])

            by_pairs(sp, NR, mlp_round)

            for i in range(2):
                sp.wait_ge(S["c_scattered"], 16 * ECOL * (i + 1))

                def agg_block(m, b, i=i):
                    n = i * NB + m
                    if i or not isinstance(m, int) or m >= 2:
                        wait(sp, S["d_used"], n - 1)
                    halves(sp, blk[b], agg_v[i][:, bass.ds(m * BLK * D, BLK * D)], S[f"d_in{b}"])

                by_pairs(sp, NB, agg_block)

            def last_load(m, b):
                if not isinstance(m, int) or m >= 2:
                    sp.wait_ge(S["f_out"], m - 1)
                at_c = m * BLK * D
                halves(sp, l_x1[b], x1_v[:, bass.ds(at_c, BLK * D)], S[f"f_in{b}"])
                halves(sp, l_a1[b], agg_v[0][:, bass.ds(at_c, BLK * D)], S[f"f_in{b}"])
                halves(sp, l_a2[b], agg_v[1][:, bass.ds(at_c, BLK * D)], S[f"f_in{b}"])

            sp.wait_ge(S["bn_done"], 2)
            last_load(0, 0)

            def last_block(m, b):
                if not isinstance(m, int) or m + 1 < NB:
                    last_load(m + 1, 1 - b)
                sp.wait_ge(S["f_out"], m + 1)
                halves(sp, out_v[:, bass.ds(m * BLK * D, BLK * D)], l_out[b], S[f"f_stored{b}"])

            by_pairs(sp, NB, last_block)
            for q in range(Q):
                sp.wait_ge(S[f"m_stored{q}"], 32 * NR)
            sp.wait_ge(S["f_stored0"], 32 * (NB - NB // 2))
            sp.wait_ge(S["f_stored1"], 32 * (NB // 2))

        @block.gpsimd
        def _(pool):
            g = nc.gpsimd
            g.memset(ident[:, :], 0.0).then_inc(S["consts"], 1)
            g.memset(ones[:, :], 1.0).then_inc(S["consts"], 1)
            g.memset(below[:, :, :], 1.0).then_inc(S["consts"], 1)
            g.memset(ones3[:, :], 1.0).then_inc(S["consts"], 1)
            g.memset(half[:, :], -0.5).then_inc(S["consts"], 1)
            g.memset(e_at[:, :, :, :], 1.0).then_inc(S["consts"], 1)
            pool.wait_ge(S["consts"], SETUP_POOL)
            g.affine_select(out=ident[:, :], in_=ident[:, :], compare_op=ALU.not_equal, fill=1.0, base=0,
                            pattern=[[-1, 128]], channel_multiplier=1).then_inc(S["iota_done"], 1)
            g.affine_select(out=below[:, 1, :], in_=below[:, 1, :], compare_op=ALU.is_gt, fill=0.0, base=0,
                            pattern=[[-1, P]], channel_multiplier=1).then_inc(S["iota_done"], 1)
            g.iota(spare_i[:, :, :], pattern=[[P, 2], [0, GT]], base=N, channel_multiplier=1)\
                .then_inc(S["iota_done"], 1)

            def waits(*pairs):
                for sem_, x in pairs:
                    wait(pool, sem_, x)
                pool.sem_inc(S["pool_passed"], 1)

            def gather(tab, b, e, k, done):
                g.indirect_dma_start(
                    out=rows[:, b, k, e, :], out_offset=None, in_=tab[0:N, :],
                    in_offset=bass.IndirectOffsetOnAxis(ap=g_idx[:, b, e, k:k + 1], axis=0),
                    compute_op=ALU.bypass).then_inc(done, 16)

            def scatter(tab, b, e, k, done):
                g.indirect_dma_start(
                    out=tab[:, :], out_offset=bass.IndirectOffsetOnAxis(ap=s_idx[:, b, e, k:k + 1], axis=0),
                    in_=vals[:, b, k, e, :], in_offset=None, compute_op=ALU.add).then_inc(done, 16)

            def a_gathers(n, b, k):
                for e in range(2):
                    gather(x, b, e, k, S[f"a_rows{b}"])

            for n in range(2):
                pool.wait_ge(S["idx_ready"], n + 1)
                for k in range(GT):
                    a_gathers(n, n, k)
            pool.wait_ge(S["y_clear"], N_ZERO)

            def a_scatters(n, b, k):
                waits((S["a_sidx"], n + 1), (S["a_vals"], GT * n + k + 1),
                      (S["a_scattered"], 32 * (GT * n + k)))
                for e in range(2):
                    scatter(y_tab, b, e, k, S["a_scattered"])

            def a_group(n, b):
                more = not isinstance(n, int) or n + 2 < EG
                if more:
                    waits((S["idx_ready"], n + 3), (S["a_xc"], n + 1))
                for k in range(GT):
                    if more:
                        a_gathers(n + 2, b, k)
                    if past(n, 1):
                        a_scatters(n - 1, 1 - b, k)

            by_pairs(pool, EG, a_group)
            for k in range(GT):
                a_scatters(EG - 1, (EG - 1) % 2, k)

            def power(st, k, a):
                g.tensor_scalar(out=st[:, k, :], in0=st[:, k, :], scalar1=1.0 / D, scalar2=EPS,
                                op0=ALU.mult, op1=ALU.add).then_inc(S[a], 1)

            def m_input(r, v):
                for q in range(Q):
                    pool.wait_ge(S["m_mean"], Q * r + q + 1)
                    wait(pool, S["m_xsq"], Q * (r - 1) + q + 1 if not isinstance(r, int) or r else 0)
                    g.tensor_tensor(out=cols(x_cen[q][0:P]), in0=cols(x_in[v * Q + q][0:P]),
                                    in1=b8(m_stat[:, v, q, 0, :]), op=ALU.subtract).then_inc(S["m_xcen"], 1)
                for q in range(Q):
                    waits((S["m_xss"], Q * r + q + 1),)
                    power(m_stat[:, v, q], 1, "m_var")
                    pool.wait_ge(S["m_var"], Q * r + q + 1)
                    g.tensor_tensor(out=m_stat[:, v, q, 1, :], in0=m_stat[:, v, q, 1, :], in1=half[:, :],
                                    op=ALU.pow).then_inc(S["m_xrstd"], 1)
                    pool.wait_ge(S["m_xrstd"], Q * r + q + 1)
                    wait(pool, S["m_xt"], Q * (r - 1) + q + 1 if not isinstance(r, int) or r else 0)
                    g.tensor_tensor(out=cols(x_nrm[q][0:P]), in0=cols(x_cen[q][0:P]),
                                    in1=b8(m_stat[:, v, q, 1, :]), op=ALU.mult).then_inc(S["m_xnrm"], 1)

            def m_round(r, v):
                for l in range(LAYERS):
                    for q in range(Q):
                        n = Q * LAYERS * r + Q * l + q + 1
                        waits((S["m_zss"], n),)
                        power(m_stat[:, v, q], 2, "m_zvar")
                        pool.wait_ge(S["m_zvar"], n)
                        g.tensor_tensor(out=m_stat[:, v, q, 3, :], in0=m_stat[:, v, q, 2, :], in1=half[:, :],
                                        op=ALU.pow).then_inc(S["m_rstd"], 1)
                    if l == 1 and (not isinstance(r, int) or r + 1 < NR):
                        m_input(r + 1, 1 - v)

            m_input(0, 0)
            by_pairs(pool, NR, m_round)

            for q in range(Q):
                pool.wait_ge(S[f"m_stored{q}"], 32 * NR)
            for i in range(2):
                tab = x1_tab if i == 0 else agg_tab[0]

                def c_gathers(n, b, k, tab=tab):
                    for e in range(2):
                        gather(tab, b, e, k, S[f"c_rows{b}"])

                base = i * EG
                if i:
                    pool.wait_ge(S["c_xc"], base)
                    pool.wait_ge(S["c_scattered"], 16 * ECOL)
                for n in range(2):
                    pool.wait_ge(S["c_idx"], base + n + 1)
                    for k in range(GT):
                        c_gathers(n, n, k)
                pool.wait_ge(S["agg_clear"], N_ZERO * 2)

                def c_group(n, b, i=i, base=base, c_gathers=c_gathers):
                    more = not isinstance(n, int) or n + 2 < EG
                    if more:
                        waits((S["c_idx"], base + n + 3), (S["c_xc"], base + n + 1))
                    for k in range(GT):
                        if more:
                            c_gathers(n + 2, b, k)
                        if past(n, 1):
                            c_scatter(n - 1, 1 - b, k)

                def c_scatter(n, b, k, i=i, base=base):
                    if k == 0:
                        waits((S["c_sidx"], base + n + 1), (S["c_vals"], base + n + 1))
                    waits((S["c_scattered"], 16 * (GT * (base + n) + k)),)
                    scatter(agg_tab[i], b, 0, k, S["c_scattered"])

                by_pairs(pool, EG, c_group)
                for k in range(GT):
                    c_scatter(EG - 1, (EG - 1) % 2, k)

            def f_block(m, b):
                pool.wait_ge(S["f_mean"], m + 1)
                wait(pool, S["f_a"], m)
                g.tensor_tensor(out=cols(l_xc[0][0:P]), in0=cols(l_x1[b][0:P]), in1=b8(f_stat[:, 0, :]),
                                op=ALU.subtract).then_inc(S["f_xc"], 1)

            by_pairs(pool, NB, f_block)

        def newton(step, var, y, t):
            v = nc.vector
            step(v.tensor_scalar(out=y.bitcast(I32), in0=var.bitcast(I32), scalar1=-0.5, scalar2=MAGIC,
                                 op0=ALU.mult, op1=ALU.add))
            for _ in range(3):
                step(v.scalar_tensor_tensor(out=t, in0=y, scalar=-0.5, in1=y, op0=ALU.mult, op1=ALU.mult))
                step(v.tensor_tensor(out=t, in0=t, in1=var, op=ALU.mult))
                step(v.scalar_tensor_tensor(out=y, in0=t, scalar=1.5, in1=y, op0=ALU.add, op1=ALU.mult))

        def pair(rows_b):
            return rows_b.rearrange("p k e d -> p (k e) d")

        @block.vector
        def _(dve):
            v = nc.vector
            step, back = Steps(dve, S["dve_step"]), Steps(dve, S["dve_back"])
            step.begin(0)

            v.memset(zeros[:, :], 0.0).then_inc(S["zero_tile"], 1)
            v.memset(w_blk[:, :, :], 0.0).then_inc(S["w_zero"], 1)
            v.memset(w_at[:, :, :], 0.0).then_inc(S["w_zero"], 1)
            dve.wait_ge(S["iota_done"], 3)
            v.tensor_copy(spare[:, :, :], spare_i[:, :, :]).then_inc(S["w_zero"], 1)
            dve.wait_ge(S["loads_edges"], 128)
            v.tensor_copy(end_f[:, :, :], end_i[:, :, :]).then_inc(S["edges_ready"], 1)
            dve.wait_ge(S["loads_w"], 16 * N_LOADS_W)
            step(v.tensor_reduce(out=w_sum[:, :], in_=w_raw[:, :, :], axis=AX.X, op=ALU.add))
            step(v.tensor_scalar(out=w_mean[:, :], in0=w_sum[:, :], scalar1=1.0 / D, scalar2=None, op0=ALU.mult))
            step(v.tensor_tensor(out=w_cen[:, :, :], in0=w_raw[:, :, :], in1=b8(w_mean[:, :]), op=ALU.subtract))
            dve.wait_ge(S["w_zero"], 3)
            step(v.tensor_copy(w_blk[0:D, :, 0:D], w_cen[0:D, 1:5, :]))
            step(v.tensor_copy(w_blk[D:128, :, D:128], w_cen[D:128, 1:5, :]))
            step(v.tensor_reduce(out=b_sum[:, :], in_=b_raw[:, :, :], axis=AX.X, op=ALU.add))
            step(v.tensor_scalar(out=b_mean[:, :], in0=b_sum[:, :], scalar1=1.0 / D, scalar2=None, op0=ALU.mult))
            step(v.tensor_tensor(out=b_cen[:, :, :], in0=b_raw[:, :, :], in1=b8(b_mean[:, :]), op=ALU.subtract))
            step(v.tensor_copy(b_part[:, 0], b_cen[:, :, :]))
            step(v.tensor_tensor(out=b_rest[:, 0], in0=b_cen[:, :, :], in1=b_part[:, 0], op=ALU.subtract))
            step(v.tensor_copy(b_part[:, 1], b_rest[:, 0]))
            step(v.tensor_tensor(out=b_rest[:, 1], in0=b_rest[:, 0], in1=b_part[:, 1], op=ALU.subtract))
            step(v.tensor_copy(b_part[:, 2], b_rest[:, 1]))
            step(v.tensor_scalar(out=b_sel[:, 0], in0=b_part[:, 0], scalar1=ident[0:3, 0:1], scalar2=None,
                                 op0=ALU.mult))
            for k in (1, 2):
                step(v.scalar_tensor_tensor(out=b_sel[:, k], in0=b_part[:, k], scalar=ident[0:3, k:k + 1],
                                            in1=b_sel[:, k - 1], op0=ALU.mult, op1=ALU.add))
            for l in range(LAYERS):
                step(v.tensor_copy(b_row[:, l], b_sel[:, 2, l].unsqueeze(1).to_broadcast([3, GC, D])))
            v.tensor_copy(b_sum[0:1, 0:1], b_mean[0:1, 0:1]).then_inc(S["w_ready"], 1)
            step.phase()

            def a_group(n, b):
                step.begin(n)
                st = tiny[:, b]
                dve.wait_ge(S[f"a_rows{b}"], (n - b) * 64 + 128)
                step(v.tensor_reduce(out=st[:, 0, :], in_=pair(rows[:, b]), axis=AX.X, op=ALU.add))
                step(v.tensor_scalar(out=st[:, 1, :], in0=st[:, 0, :], scalar1=1.0 / D, scalar2=None,
                                     op0=ALU.mult))
                v.tensor_tensor(out=cols(xc[:, b]), in0=pair(rows[:, b]), in1=b8(st[:, 1, :]),
                                op=ALU.subtract).then_inc(S["a_xc"], 1)
                for k in range(GT):
                    t = GT * n + k
                    dve.wait_ge(S["a_r"], t + 1)
                    wait(dve, S["a_t"], t - 1)
                    for e in range(2):
                        v.tensor_scalar(out=same[:, k % 2, e, :], in0=psum[k % 2][0:P, 0:2 * P],
                                        scalar1=e_key[:, b, e, k:k + 1], scalar2=None, op0=ALU.is_equal)\
                            .then_inc(S["a_same"], 1)
                    dve.wait_ge(S["a_same"], 2 * t + 2)
                    step(v.tensor_tensor_reduce(out=junk[:, 0:P], in0=same[:, k % 2, 0, 0:P],
                                                in1=below[:, 1, :], scale=1.0, scalar=0.0, op0=ALU.mult,
                                                op1=ALU.add, accum_out=repeat[:, b, 0, k:k + 1]))
                    step(v.tensor_tensor_reduce(out=junk[:, :], in0=same[:, k % 2, 1, :],
                                                in1=below[:, :, :].rearrange("p a i -> p (a i)"), scale=1.0,
                                                scalar=0.0, op0=ALU.mult, op1=ALU.add,
                                                accum_out=repeat[:, b, 1, k:k + 1]))
                    if k == 0:
                        dve.wait_ge(S["a_sq"], n + 1)
                        step(v.tensor_reduce(out=st[:, 2, :], in_=cols(sq[:, b]), axis=AX.X, op=ALU.add))
                        step(v.tensor_scalar(out=st[:, 3, :], in0=st[:, 2, :], scalar1=1.0 / D, scalar2=EPS,
                                             op0=ALU.mult, op1=ALU.add))
                        newton(step, st[:, 3, :], st[:, 4, :], st[:, 5, :])
                        step(v.tensor_tensor(out=st[:, 6, :].rearrange("p (k e) -> p k e", e=2),
                                             in0=st[:, 4, :].rearrange("p (k e) -> p k e", e=2),
                                             in1=ew_s[:, bass.ds(GT * n, GT)].unsqueeze(2)
                                             .to_broadcast([P, GT, 2]), op=ALU.mult))
                        wait(dve, S["a_t"], GT * (n - 1))
                        v.scalar_tensor_tensor(out=pair(hw[:, b]), in0=cols(xc[:, b]), scalar=0.0,
                                               in1=b8(st[:, 6, :]), op0=ALU.max, op1=ALU.mult)\
                            .then_inc(S["a_hw"], 1)
                tmp = r_tmp[:, b]
                step(v.tensor_tensor(out=tmp[:, 0], in0=spare[:, :, :], in1=e_key[:, b], op=ALU.subtract))
                step(v.scalar_tensor_tensor(out=tmp[:, 1], in0=repeat[:, b], scalar=1.0, in1=tmp[:, 0],
                                            op0=ALU.min, op1=ALU.mult))
                wait(dve, S["a_scattered"], 32 * GT * (n - 1))
                v.tensor_tensor(out=s_idx[:, b], in0=tmp[:, 1], in1=e_key[:, b], op=ALU.add)\
                    .then_inc(S["a_sidx"], 1)
                dve.wait_ge(S["a_sidx"], n + 1)
                step(v.tensor_copy(to_i[:, bass.ds(GT * n, GT)], s_idx[:, b, 0]))

            by_pairs(dve, EG, a_group)
            step.phase()

            dve.wait_ge(S["a_scattered"], 32 * ECOL)

            def m_input(r, u):
                for q in range(Q):
                    dve.wait_ge(S[f"m_in{u * Q + q}"], (r - u) * 32 + 64)
                    step(v.tensor_reduce(out=m_stat[:, u, q, 0, :], in_=cols(x_in[u * Q + q][0:P]), axis=AX.X,
                                         op=ALU.add))
                    v.tensor_scalar(out=m_stat[:, u, q, 0, :], in0=m_stat[:, u, q, 0, :], scalar1=1.0 / D,
                                    scalar2=None, op0=ALU.mult).then_inc(S["m_mean"], 1)
                for q in range(Q):
                    dve.wait_ge(S["m_xsq"], Q * r + q + 1)
                    v.tensor_reduce(out=m_stat[:, u, q, 1, :], in_=cols(x_sq[q][0:P]), axis=AX.X,
                                    op=ALU.add).then_inc(S["m_xss"], 1)

            def m_round(r, u):
                step.begin(r)
                for l in range(LAYERS):
                    n0 = Q * LAYERS * r + Q * l

                    def reduce_sq(q):
                        dve.wait_ge(S["m_zsq"], n0 + q + 1)
                        v.tensor_reduce(out=m_stat[:, u, q, 2, :], in_=cols(z_sq[q][0:P]), axis=AX.X,
                                        op=ALU.add).then_inc(S["m_zss"], 1)

                    def scale(q):
                        dve.wait_ge(S["m_rstd"], n0 + q + 1)
                        wait(dve, S["m_zt"], n0 + q + 1 - Q)
                        v.tensor_tensor(out=cols(z_nrm[q][0:P]), in0=cols(psum[4 + q][0:P, :]),
                                        in1=b8(m_stat[:, u, q, 3, :]), op=ALU.mult).then_inc(S["m_zn"], 1)

                    reduce_sq(0)
                    for q in range(1, Q):
                        reduce_sq(q)
                        scale(q - 1)
                    scale(Q - 1)
                    if l == 1 and (not isinstance(r, int) or r + 1 < NR):
                        m_input(r + 1, 1 - u)
                for q in range(Q):
                    dve.wait_ge(S["m_back"], Q * r + q + 1)
                    wait(dve, S[f"m_stored{q}"], 32 * r)
                    v.tensor_tensor(out=x_out[q][0:P], in0=psum[4 + q][0:P, :], in1=x_in[u * Q + q][0:P],
                                    op=ALU.add).then_inc(S["m_out"], 1)

            step.begin(0)
            m_input(0, 0)
            step.phase()
            by_pairs(dve, NR, m_round)
            step.phase()

            for i in range(2):
                base = i * EG
                if i:
                    dve.wait_ge(S["bn_done"], 1)

                def c_front(n, b, i=i, base=base):
                    step.begin(n)
                    c = n + base
                    st = tiny[:, b]
                    dve.wait_ge(S[f"c_rows{b}"], i * EG * 64 + (n - b) * 64 + 128)
                    if i == 0:
                        step(v.tensor_reduce(out=st[:, 0, :], in_=pair(rows[:, b]), axis=AX.X, op=ALU.add))
                        step(v.tensor_scalar(out=st[:, 1, :], in0=st[:, 0, :], scalar1=1.0 / D, scalar2=None,
                                             op0=ALU.mult))
                        v.tensor_tensor(out=cols(xc[:, b]), in0=pair(rows[:, b]), in1=b8(st[:, 1, :]),
                                        op=ALU.subtract).then_inc(S["c_xc"], 1)
                    else:
                        v.tensor_tensor(out=cols(xc[:, b]), in0=pair(rows[:, b]),
                                        in1=bn_s[:, 0, 0, :].unsqueeze(1).to_broadcast([P, GC, D]),
                                        op=ALU.mult).then_inc(S["c_xc"], 1)
                    for k in range(GT):
                        t = GT * c + k
                        dve.wait_ge(S["c_r"], t + 1)
                        wait(dve, S["c_v"], t + 1 - 2 * GT)
                        v.tensor_scalar(out=same[:, k // 2, k % 2, b * P:(b + 1) * P], in0=psum[k % 2][0:P, 0:P],
                                        scalar1=e_key[:, b, 0, k:k + 1], scalar2=None, op0=ALU.is_equal)\
                            .then_inc(S["c_same"], 1)
                    if i == 0:
                        dve.wait_ge(S["c_sq"], c + 1)
                        step(v.tensor_reduce(out=st[:, 2, :], in_=cols(sq[:, b]), axis=AX.X, op=ALU.add))
                        step(v.tensor_scalar(out=st[:, 3, :], in0=st[:, 2, :], scalar1=1.0 / D, scalar2=EPS,
                                             op0=ALU.mult, op1=ALU.add))
                        newton(step, st[:, 3, :], st[:, 4, :], st[:, 5, :])
                        wait(dve, S["c_ht"], c - 1)
                        wait(dve, S["c_keep"], c - 1)
                        v.scalar_tensor_tensor(out=pair(hw[:, b]), in0=cols(xc[:, b]), scalar=0.0,
                                               in1=b8(st[:, 4, :]), op0=ALU.max, op1=ALU.mult)\
                            .then_inc(S["c_hw"], 1)
                    else:
                        dve.wait_ge(S["c_xc"], c + 1)
                        step(v.tensor_tensor(out=sq[:, b], in0=xc[:, b],
                                             in1=h_keep[0:P, bass.ds(n * W, W)], op=ALU.add))
                        wait(dve, S["c_ht"], c - 1)
                        v.tensor_tensor(out=pair(hw[:, b]), in0=cols(sq[:, b]),
                                        in1=bn_s[:, 0, 1, :].unsqueeze(1).to_broadcast([P, GC, D]),
                                        op=ALU.add).then_inc(S["c_hw"], 1)

                def c_back(n, b, base=base):
                    back.begin(n)
                    c = n + base
                    dve.wait_ge(S["c_act"], c + 1)
                    z = psum[4 + b][0:P, :].rearrange("p (k w) -> p k w", w=128)
                    back(v.tensor_scalar(out=dve_e[:, 0], in0=act_e[:, 0], scalar1=1.0, scalar2=None,
                                         op0=ALU.add))
                    back(v.reciprocal(out=dve_e[:, 1], in_=dve_e[:, 0]))
                    back(v.scalar_tensor_tensor(out=dve_e[:, 2], in0=z[:, :, D:], scalar=0.0, in1=act_e[:, 3],
                                                op0=ALU.max, op1=ALU.add))
                    wait(dve, S["c_v"], GT * (c - 1))
                    v.tensor_tensor(out=msg[:, b], in0=dve_e[:, 2], in1=dve_e[:, 1], op=ALU.mult)\
                        .then_inc(S["c_msg"], 1)

                one_behind(dve, EG, c_front, c_back)
                step.phase()
                back.phase()

                step.begin(0)
                dve.wait_ge(S["d_used"], NB * (i + 1))
                v.tensor_tensor(out=bn_x[:, 0], in0=psum[0][:, 0:128], in1=ident[:, :], op=ALU.mult)\
                    .then_inc(S["bn_ready"], 1)
                v.tensor_scalar(out=bn_x[:, 1], in0=ident[:, :], scalar1=psum[7][:, 0:1], scalar2=None,
                                op0=ALU.mult).then_inc(S["bn_ready"], 1)
                dve.wait_ge(S["bn_sum"], i + 1)
                step(v.tensor_copy(bn_w[:, 0:4, :], psum[1][0:P, 0:256].rearrange("p (a d) -> p a d", d=D)))
                sums = bn_w[:, 0:4, :].rearrange("p (a h) d -> p a h d", h=2)
                step(v.tensor_tensor(out=bn_w[:, 4:6, :], in0=sums[:, :, 0, :], in1=sums[:, :, 1, :], op=ALU.add))
                step(v.tensor_scalar(out=bn_w[:, 4:6, :], in0=bn_w[:, 4:6, :], scalar1=1.0 / N, scalar2=None,
                                     op0=ALU.mult))
                step(v.tensor_tensor(out=bn_w[:, 6, :], in0=bn_w[:, 5, :], in1=bn_w[:, 5, :], op=ALU.mult))
                step(v.tensor_tensor(out=bn_w[:, 7, :], in0=bn_w[:, 4, :], in1=bn_w[:, 6, :], op=ALU.subtract))
                step(v.tensor_scalar(out=bn_w[:, 7, :], in0=bn_w[:, 7, :], scalar1=0.0, scalar2=EPS,
                                     op0=ALU.max, op1=ALU.add))
                newton(step, bn_w[:, 7, :], bn_w[:, 8, :], bn_w[:, 9, :])
                step(v.tensor_tensor(out=bn_s[:, i, 0, :], in0=bn_w[:, 8, :], in1=bn_gb[:, i, 0, :], op=ALU.mult))
                step(v.tensor_tensor(out=bn_w[:, 9, :], in0=bn_w[:, 5, :], in1=bn_s[:, i, 0, :], op=ALU.mult))
                v.tensor_tensor(out=bn_s[:, i, 1, :], in0=bn_gb[:, i, 1, :], in1=bn_w[:, 9, :],
                                op=ALU.subtract).then_inc(S["bn_done"], 1)
                dve.wait_ge(S["bn_done"], i + 1)
                step.phase()

            def spread(i, k):
                return bn_s[:, i, k, :].unsqueeze(1).to_broadcast([P, BLK, D])

            def f_block(m, b):
                step.begin(m)
                dve.wait_ge(S[f"f_in{b}"], (m - b) * 48 + 96)
                wait(dve, S["f_xc"], m)
                step(v.tensor_reduce(out=f_stat[:, 0, :], in_=cols(l_x1[b][0:P]), axis=AX.X, op=ALU.add))
                v.tensor_scalar(out=f_stat[:, 0, :], in0=f_stat[:, 0, :], scalar1=1.0 / D, scalar2=None,
                                op0=ALU.mult).then_inc(S["f_mean"], 1)
                agg1, agg2, a = cols(l_a1[b][0:P]), cols(l_a2[b][0:P]), cols(l_a[0][0:P])
                step(v.tensor_tensor(out=a, in0=agg1, in1=spread(0, 0), op=ALU.mult))
                step(v.tensor_tensor(out=a, in0=a, in1=spread(0, 1), op=ALU.add))
                step(v.tensor_tensor(out=agg2, in0=agg2, in1=spread(1, 0), op=ALU.mult))
                step(v.tensor_tensor(out=agg2, in0=agg2, in1=spread(1, 1), op=ALU.add))
                dve.wait_ge(S["f_sq"], m + 1)
                step(v.tensor_reduce(out=f_stat[:, 1, :], in_=cols(l_sq[0][0:P]), axis=AX.X, op=ALU.add))
                step(v.tensor_scalar(out=f_stat[:, 2, :], in0=f_stat[:, 1, :], scalar1=1.0 / D, scalar2=EPS,
                                     op0=ALU.mult, op1=ALU.add))
                newton(step, f_stat[:, 2, :], f_stat[:, 3, :], f_stat[:, 4, :])
                v.scalar_tensor_tensor(out=agg1, in0=cols(l_xc[0][0:P]), scalar=0.0, in1=b8(f_stat[:, 3, :]),
                                       op0=ALU.max, op1=ALU.mult).then_inc(S["f_a"], 1)
                dve.wait_ge(S["f_a"], m + 1)
                step(v.tensor_tensor(out=a, in0=a, in1=agg1, op=ALU.add))
                step(v.scalar_tensor_tensor(out=agg2, in0=a, scalar=0.0, in1=agg2, op0=ALU.max, op1=ALU.add))
                wait(dve, S[f"f_stored{b}"], (m - b) * 16)
                v.scalar_tensor_tensor(out=cols(l_out[b][0:P]), in0=agg2, scalar=0.0, in1=cols(l_x1[b][0:P]),
                                       op0=ALU.max, op1=ALU.add).then_inc(S["f_out"], 1)

            by_pairs(dve, NB, f_block)

        @block.scalar
        def _(act):
            a = nc.scalar
            step = Steps(act, S["act_step"])

            def load(dst_ap, src_ap):
                act.dma_start(dst_ap, src_ap).then_inc(S["loads_w"], 16)
                n_loads[0] += 1

            n_loads = [0]
            load(w_raw[:, 0, :], mlp["W1"][0:128, :])
            for l in range(LAYERS):
                w = mlp["W1"][128:192, :] if l == 0 else mlp[f"W{l + 1}"]
                for h in range(2):
                    load(w_raw[h * D:(h + 1) * D, 1 + l, :], w)
                    load(gain[h * D:(h + 1) * D, l:l + 1], mlp[f"g{l + 1}"].unsqueeze(1))
                    load(shift[h * D:(h + 1) * D, l:l + 1], mlp[f"be{l + 1}"].unsqueeze(1))
                load(b_raw[:, l, :], mlp[f"b{l + 1}"].unsqueeze(0).to_broadcast([3, D]))
            act.wait_ge(S["w_zero"], 2)
            for i in range(2):
                c = conv[i]
                for h, (wn, bn) in enumerate((("Wf", "bf"), ("Ws", "bs"))):
                    load(w_fs[:, i, h * D:(h + 1) * D], c[wn][0:128, :])
                    for k in range(GT):
                        to = slice(k * 128 + h * D, k * 128 + (h + 1) * D)
                        load(w_at[3 * k:3 * k + 2, i, to], c[wn][128:130, :])
                        load(w_at[3 * k + 2:3 * k + 3, i, to], c[bn].unsqueeze(0))
                for k, name in enumerate(("gamma", "beta")):
                    load(bn_gb[:, i, k, :], c[name].unsqueeze(0).to_broadcast([P, D]))
            assert n_loads[0] == N_LOADS_W

            act.wait_ge(S["edges_ready"], 1)

            def copy(o, i_):
                return a.activation(o, i_, ACT.Copy)

            def group_of(table, n):
                return table[:, :, bass.ds(GT * n, GT)]

            for n in range(2):
                copy(g_idx[:, n], group_of(end_i, n)).then_inc(S["idx_ready"], 1)

            copy(e_key[:, 0], group_of(end_f, 0)).then_inc(S["key_ready"], 1)
            act.wait_ge(S["a_rows0"], 128)
            copy(g_idx[:, 0], group_of(end_i, 2)).then_inc(S["idx_ready"], 1)

            def a_group(n, b):
                act.wait_ge(S["a_xc"], n + 1)
                a.activation(sq[:, b], xc[:, b], ACT.Square).then_inc(S["a_sq"], 1)
                for k in range(GT):
                    t = GT * n + k
                    act.wait_ge(S["a_t"], t + 1)
                    wait(act, S["a_v"], t - 1)
                    copy(s_t[:, k % 2, :], psum[2 + k % 2][:, 0:2 * P]).then_inc(S["a_ts"], 1)
                    act.wait_ge(S["a_v"], t + 1)
                    wait(act, S["a_scattered"], 32 * (t + 1 - 2 * GT))
                    copy(vals[:, b, k].rearrange("p e d -> p (e d)"), psum[4 + k % 2][0:P, 0:2 * D])\
                        .then_inc(S["a_vals"], 1)
                    if k == 0 and (not isinstance(n, int) or n + 1 < EG):
                        wait(act, S["a_sidx"], n)
                        copy(e_key[:, 1 - b], group_of(end_f, n + 1)).then_inc(S["key_ready"], 1)
                    if k == 2 and (not isinstance(n, int) or n + 3 < EG):
                        act.wait_ge(S[f"a_rows{1 - b}"], (n + b) * 64 + 128)
                        copy(g_idx[:, 1 - b], group_of(end_i, n + 3)).then_inc(S["idx_ready"], 1)

            by_pairs(act, EG, a_group, ahead=3)

            def m_input(r, u):
                for q in range(Q):
                    act.wait_ge(S["m_xcen"], Q * r + q + 1)
                    a.activation(x_sq[q][0:P], x_cen[q][0:P], ACT.Square).then_inc(S["m_xsq"], 1)

            def m_round(r, u):
                for q in range(Q):
                    act.wait_ge(S["m_xt"], Q * r + q + 1)
                    wait(act, S["m_back"], Q * (r - 1) + q + 1 if past(r, 1) else 0)
                    a.activation(h_t[q][:, 0:Q * P], psum[q][:, 0:Q * P], ACT.Relu).then_inc(S["m_hin"], 1)
                for l in range(LAYERS):
                    n0 = Q * LAYERS * r + Q * l
                    for q in range(Q):
                        act.wait_ge(S["m_z"], n0 + q + 1)
                        wait(act, S["m_zss"], n0 + q + 1 - Q)
                        a.activation(z_sq[q][0:P], psum[4 + q][0:P, :], ACT.Square).then_inc(S["m_zsq"], 1)
                    for q in range(Q):
                        act.wait_ge(S["m_zt"], n0 + q + 1)
                        a.activation(h_t[q][:, 0:Q * P], psum[q][:, 0:Q * P], ACT.Tanh, bias=shift[:, l:l + 1],
                                     scale=gain[:, l:l + 1]).then_inc(S["m_h"], 1)
                    if l == 1 and (not isinstance(r, int) or r + 1 < NR):
                        m_input(r + 1, 1 - u)

            m_input(0, 0)
            by_pairs(act, NR, m_round)

            for i in range(2):
                base = i * EG
                if i:
                    act.wait_ge(S["c_rows1"], EG * 64)
                    act.wait_ge(S["c_rows0"], EG * 64)
                for n in range(2):
                    copy(g_idx[:, n], group_of(end_i, n)).then_inc(S["c_idx"], 1)

                def c_slots(n, b, base=base):
                    c = n + base
                    wait(act, S["c_same"], GT * (c - 1))
                    copy(e_key[:, b], group_of(end_f, n)).then_inc(S["c_slots"], 1)
                    wait(act, S["c_att"], c - 1)
                    copy(e_at[:, b, :, 0:2], at_s[:, bass.ds(GT * n, GT), :]).then_inc(S["c_slots"], 1)

                c_slots(0, 0)
                act.wait_ge(S["c_rows0"], i * EG * 64 + 128)
                copy(g_idx[:, 0], group_of(end_i, 2)).then_inc(S["c_idx"], 1)

                def c_body(n, b, i=i, base=base, c_slots=c_slots):
                    c = n + base
                    if i == 0:
                        act.wait_ge(S["c_xc"], c + 1)
                        a.activation(sq[:, b], xc[:, b], ACT.Square).then_inc(S["c_sq"], 1)
                    act.wait_ge(S["c_att"], c + 1)
                    copy(at_t[:, b, :], psum[3][0:3 * GT, 0:P]).then_inc(S["c_atc"], 1)
                    if not isinstance(n, int) or n + 1 < EG:
                        c_slots(n + 1, 1 - b)
                    if past(n, 1):
                        c_messages(n - 1, 1 - b)
                    act.wait_ge(S["c_ht"], c + 1)
                    wait(act, S["c_z"], c)
                    a.activation(zt[:, 0:Q * P], psum[2][:, 0:Q * P], ACT.Relu).then_inc(S["c_zt"], 1)
                    if i == 0:
                        act.wait_ge(S["c_hw"], c + 1)
                        copy(h_keep[0:P, bass.ds(n * W, W)], hw[:, b].rearrange("p k e d -> p (k e d)"))\
                            .then_inc(S["c_keep"], 1)
                    if not isinstance(n, int) or n + 3 < EG:
                        act.wait_ge(S[f"c_rows{1 - b}"], i * EG * 64 + (n + b) * 64 + 128)
                        copy(g_idx[:, 1 - b], group_of(end_i, n + 3)).then_inc(S["c_idx"], 1)
                    if past(n, 1):
                        c_results(n - 1, 1 - b)

                def c_messages(n, b, base=base):
                    c = n + base
                    step.begin(n)
                    act.wait_ge(S["c_z"], c + 1)
                    wait(act, S["c_msg"], c)
                    z = psum[4 + b][0:P, :].rearrange("p (k w) -> p k w", w=128)
                    step(a.activation(act_e[:, 1], z[:, :, D:], ACT.Abs))
                    step(a.activation(act_e[:, 2], act_e[:, 1], ACT.Exp, scale=-1.0))
                    a.activation(act_e[:, 3], act_e[:, 2], ACT.Ln, bias=ones[0:P, 0:1])
                    a.activation(act_e[:, 0], z[:, :, 0:D], ACT.Exp, scale=-1.0).then_inc(S["c_act"], 1)

                def c_results(n, b, base=base):
                    c = n + base
                    wait(act, S["c_scattered"], 16 * GT * (c - 1))
                    copy(s_idx[:, b, 0], to_i[:, bass.ds(GT * n, GT)]).then_inc(S["c_sidx"], 1)
                    act.wait_ge(S["c_v"], GT * (c + 1))
                    copy(vals[:, b, :, 0, :], psum[6][0:P, 0:GT * D].rearrange("p (k d) -> p k d", d=D))\
                        .then_inc(S["c_vals"], 1)

                by_pairs(act, EG, c_body, ahead=3)
                c_messages(EG - 1, (EG - 1) % 2)
                c_results(EG - 1, (EG - 1) % 2)
                step.phase()

            def f_block(m, b):
                act.wait_ge(S["f_xc"], m + 1)
                wait(act, S["f_a"], m)
                a.activation(l_sq[0][0:P], l_xc[0][0:P], ACT.Square).then_inc(S["f_sq"], 1)

            by_pairs(act, NB, f_block)

        @block.tensor
        def _(pe):
            t_ = nc.tensor
            pe.wait_ge(S["iota_done"], 3)
            pe.wait_ge(S["w_ready"], 1)
            idp = ident[0:P, 0:P]

            def key_row(b, e, k, bank, at_c):
                return t_.matmul(bank[0:P, at_c:at_c + P], e_key[:, b, e, k:k + 1].to_broadcast([P, P]), idp,
                                 start=True, stop=True)

            def a_keys(n, b, tiles):
                for k in tiles:
                    wait(pe, S["a_same"], 2 * (GT * n + k) - 2)
                    for e in range(2):
                        last = key_row(b, e, k, psum[k % 2], e * P)
                    last.then_inc(S["a_r"], 1)

            pe.wait_ge(S["key_ready"], 1)
            a_keys(0, 0, (0, 1))

            def a_group(n, b):
                a_keys(n, b, (2, 3))
                pe.wait_ge(S["a_hw"], n + 1)
                for k in range(GT):
                    t = GT * n + k
                    pe.wait_ge(S["a_same"], 2 * t + 2)
                    wait(pe, S["a_ts"], t - 1)
                    t_.matmul(psum[2 + k % 2][0:D, 0:2 * P], hw[:, b, k, 1, :], same[:, k % 2, 0, :],
                              start=True, stop=True)
                    t_.matmul(psum[2 + k % 2][D:128, 0:2 * P], hw[:, b, k, 0, :], same[:, k % 2, 1, :],
                              start=True, stop=True).then_inc(S["a_t"], 1)
                    pe.wait_ge(S["a_ts"], t + 1)
                    wait(pe, S["a_vals"], t - 1)
                    for e in range(2):
                        last = t_.matmul(psum[4 + k % 2][0:P, e * D:(e + 1) * D], s_t[:, k % 2, e * P:(e + 1) * P],
                                         w_cen[:, 0, :], start=True, stop=True)
                    last.then_inc(S["a_v"], 1)
                if not isinstance(n, int) or n + 1 < EG:
                    pe.wait_ge(S["key_ready"], n + 2)
                    a_keys(n + 1, 1 - b, (0, 1))

            by_pairs(pe, EG, a_group)

            pe.wait_ge(S["a_scattered"], 32 * ECOL)

            def m_round(r, u):
                for q in range(Q):
                    pe.wait_ge(S["m_xnrm"], Q * r + q + 1)
                    for j in range(Q):
                        last = t_.transpose(psum[q][:, j * P:(j + 1) * P], x_nrm[q][0:P, j * 128:(j + 1) * 128], idp)
                    last.then_inc(S["m_xt"], 1)
                for l in range(LAYERS):
                    n0 = Q * LAYERS * r + Q * l
                    for q in range(Q):
                        if l == 0:
                            wait(pe, S["m_out"], Q * (r - 1) + q + 1 if past(r, 1) else 0)
                            pe.wait_ge(S[f"m_in{u * Q + q}"], (r - u) * 32 + 64)
                        t_.matmul(psum[4 + q][0:P, :], ones3[:, 0:P], b_row[:, l].rearrange("p c d -> p (c d)"),
                                  start=True, stop=False)
                        if l == 0:
                            t_.matmul(psum[4 + q][0:P, :], idp, y_in[u * Q + q][0:P], start=False, stop=False)
                            pe.wait_ge(S["m_hin"], Q * r + q + 1)
                        else:
                            pe.wait_ge(S["m_h"], n0 - Q + q + 1)
                        for j in range(Q):
                            last = t_.matmul(psum[4 + q][0:P, j * 128:(j + 1) * 128],
                                             h_t[q][:, j * P:(j + 1) * P], w_blk[:, l, :], start=False,
                                             stop=(j == Q - 1))
                        last.then_inc(S["m_z"], 1)
                    for q in range(Q):
                        pe.wait_ge(S["m_zn"], n0 + q + 1)
                        for j in range(Q):
                            last = t_.transpose(psum[q][:, j * P:(j + 1) * P],
                                                z_nrm[q][0:P, j * 128:(j + 1) * 128], idp)
                        last.then_inc(S["m_zt"], 1)
                for q in range(Q):
                    pe.wait_ge(S["m_h"], Q * LAYERS * r + Q * (LAYERS - 1) + q + 1)
                    for j in range(Q):
                        last = t_.transpose(psum[4 + q][0:P, j * 128:(j + 1) * 128],
                                            h_t[q][:, j * P:(j + 1) * P], ident[:, :])
                    last.then_inc(S["m_back"], 1)

            by_pairs(pe, NR, m_round)

            for i in range(2):
                base = i * EG
                if i == 0:
                    pe.wait_ge(S["m_out"], NR * Q)
                else:
                    pe.wait_ge(S["bn_done"], 1)

                def c_keys(n, b, tiles, base=base):
                    for k in tiles:
                        wait(pe, S["c_same"], GT * (n + base) + k - 1)
                        key_row(b, 0, k, psum[k % 2], 0).then_inc(S["c_r"], 1)

                pe.wait_ge(S["c_slots"], 2 * base + 2)
                c_keys(0, 0, (0, 1))

                def c_front(n, b, i=i, base=base, c_keys=c_keys):
                    c = n + base
                    c_keys(n, b, (2, 3))
                    wait(pe, S["c_atc"], c)
                    t_.transpose(psum[3][0:3 * GT, 0:P], e_at[:, b].rearrange("p k a -> p (k a)"), idp)\
                        .then_inc(S["c_att"], 1)
                    pe.wait_ge(S["c_hw"], c + 1)
                    wait(pe, S["c_zt"], c)
                    for k in range(GT):
                        last = t_.transpose(psum[2][:, k * P:(k + 1) * P],
                                            hw[:, b, k].rearrange("p e d -> p (e d)"), idp)
                    last.then_inc(S["c_ht"], 1)
                    pe.wait_ge(S["c_atc"], c + 1)
                    wait(pe, S["c_msg"], c - 1)
                    t_.matmul(psum[4 + b][0:P, :], at_t[:, b, :], w_at[:, i, :], start=True, stop=False)
                    pe.wait_ge(S["c_zt"], c + 1)
                    for k in range(GT):
                        last = t_.matmul(psum[4 + b][0:P, k * 128:(k + 1) * 128], zt[:, k * P:(k + 1) * P],
                                         w_fs[:, i, :], start=False, stop=(k == GT - 1))
                    last.then_inc(S["c_z"], 1)
                    if not isinstance(n, int) or n + 1 < EG:
                        pe.wait_ge(S["c_slots"], 2 * c + 4)
                        c_keys(n + 1, 1 - b, (0, 1))

                def c_back(n, b, base=base):
                    c = n + base
                    pe.wait_ge(S["c_msg"], c + 1)
                    flat = msg[:, b].rearrange("p k d -> p (k d)")
                    for h in range(2):
                        t_.matmul(psum[7][:, 0:1], flat[:, h * 128:(h + 1) * 128], ones[0:P, 0:1],
                                  start=not past(n, 1) and h == 0,
                                  stop=isinstance(n, int) and n == EG - 1 and h == 1)
                    wait(pe, S["c_vals"], c)
                    for k in range(GT):
                        pe.wait_ge(S["c_same"], GT * c + k + 1)
                        t_.matmul(psum[6][0:P, k * D:(k + 1) * D], same[:, k // 2, k % 2, b * P:(b + 1) * P], msg[:, b, k, :],
                                  start=True, stop=True).then_inc(S["c_v"], 1)

                one_behind(pe, EG, c_front, c_back)
                pe.wait_ge(S["c_same"], GT * EG * (i + 1))

                def d_block(m, b, i=i):
                    pe.wait_ge(S[f"d_in{b}"], i * D_PER[b] + (m - b) * 16 + 32)
                    for j in range(BLK // 2):
                        pair_ = blk[b][0:P, j * 128:(j + 1) * 128]
                        last = t_.matmul(psum[0][:, 0:128], pair_, pair_, start=not past(m, 1) and j == 0,
                                         stop=isinstance(m, int) and m == NB - 1 and j == BLK // 2 - 1)
                    last.then_inc(S["d_used"], 1)

                by_pairs(pe, NB, d_block)
                pe.wait_ge(S["bn_ready"], 2 * (i + 1))
                for h in range(2):
                    last = t_.matmul(psum[1][0:P, h * 128:(h + 1) * 128], ones[:, 0:P], bn_x[:, h], start=True,
                                     stop=True)
                last.then_inc(S["bn_sum"], 1)


_MLP = [f"{n}{l}" for l in range(1, 5) for n in ("W", "b", "g", "be")]
_CONV = ["Wf", "bf", "Ws", "bs", "gamma", "beta"]


def kernel(**inputs):
    import numpy as np
    import concourse.bacc as bacc
    from concourse.bass_utils import run_bass_kernel_spmd

    nc = bacc.Bacc("TRN2", target_bir_lowering=False, num_devices=1)
    arrays, aps = {}, {}
    for name, value in inputs.items():
        a = np.ascontiguousarray(value)
        arrays[f"in_{name}"] = a
        aps[name] = nc.dram_tensor(f"in_{name}", a.shape, mybir.dt.from_np(a.dtype), kind="ExternalInput").ap()
    out = nc.dram_tensor("out", (N, D), F32, kind="ExternalOutput").ap()
    tables = [nc.dram_tensor(name, (NT, D), F32).ap() for name in ("y_tab", "x1_tab", "agg1_tab", "agg2_tab")]
    gnn_kernel(nc, aps["x"], aps["src"], aps["dst"], aps["edge_attr_2"], aps["edge_weight"],
               {k: aps[f"L0_gnn_{k}"] for k in _MLP},
               [{k: aps[f"L1_gnn_{k}{i}"] for k in _CONV} for i in (1, 2)],
               out, tables[0], tables[1], tables[2:])
    r = run_bass_kernel_spmd(nc, [arrays], core_ids=[0])
    return r.results[0]["out"]
```

```python
import concourse.bass as bass
from concourse import mybir
from contextlib import ExitStack

F32 = mybir.dt.float32
BF16 = mybir.dt.bfloat16
I32 = mybir.dt.int32
ALU = mybir.AluOpType
ACT = mybir.ActivationFunctionType
AX = mybir.AxisListType

N, E, D = 100000, 25000, 64
P = 125
NCOL, ECOL = N // P, E // P
GC = 8
W = GC * D
GT = 4
EG = ECOL // GT
Q = 4
BW = Q * W
NBATCH = NCOL // (GC * Q)
STREAM = [(NBATCH + 1) // 2, NBATCH // 2]
TURNS = STREAM[0] + 1
SPARE = 2 * P
ZC = 2 * (TURNS - 1)
ZR = 31 * ZC
NT = 128 * ZR
EPS = 1e-5
LAYERS = 4
STEPS = 2 * LAYERS
BLK = 32
NB = NCOL // BLK
KA, KB = 112, P - 112
MAGIC = float(0x5F3759DF)


def wait(eng, sem, value):
    if isinstance(value, int) and value <= 0:
        return
    eng.wait_ge(sem, value)


def past(n, k):
    return not isinstance(n, int) or n >= k


def exists(j, u):
    return not isinstance(j, int) or 0 <= j < STREAM[u]


def unit(k, j):
    k, j = (k, j) if k >= 0 else (k + STEPS, j - 1)
    return (k % 2, k // 2, j) if exists(j, k % 2) else None


def nth(l, j, q):
    return Q * LAYERS * j + Q * l + q + 1


class Steps:

    def __init__(self, eng, sem):
        self.eng, self.sem, self.base, self.start, self.count, self.per, self.groups = eng, sem, 0, 0, 0, 0, 0
        self.last = None

    def begin(self, n):
        if self.groups == 1:
            self.per = self.count
        self.groups += 1
        written_out = isinstance(n, int) and isinstance(self.last, int)
        self.last = n
        if isinstance(n, int) and n == 0:
            self.start = self.base
        elif written_out:
            self.start = self.start + self.count
        else:
            self.start = n * self.per + self.base
        self.count = 0

    def phase(self):
        self.base = self.start + self.count
        self.start, self.count, self.groups = self.base, 0, 0

    def __call__(self, ins):
        self.count += 1
        ins.then_inc(self.sem, 1)
        self.eng.wait_ge(self.sem, self.start + self.count)


def by_pairs(eng, total, body, ahead=1):
    body(0, 0)
    body(1, 1)
    end = 2 * ((total - ahead) // 2)
    with eng.Fori(1, end // 2) as h:
        body(2 * h, 0)
        body(2 * h + 1, 1)
    for g in range(end, total):
        body(g, g % 2)


def one_behind(eng, total, front, back):
    def body(g, parity):
        front(g, parity)
        if past(g, 1):
            back(g - 1, 1 - parity)

    by_pairs(eng, total, body)
    back(total - 1, (total - 1) % 2)


def gnn_kernel(nc, x, src, dst, attr, ew, mlp, conv, out, y_tab, x1_tab, agg_tab):
    ctx = ExitStack()
    with ctx:
        def sb(name, shape, dt=F32):
            return ctx.enter_context(nc.sbuf_tensor(name, shape, dt))

        def sem(name):
            return ctx.enter_context(nc.semaphore(name))

        def nodes(t):
            return t[0:N, :].rearrange("(p c) d -> p (c d)", p=P)

        x_v, out_v, y_v, x1_v = nodes(x), nodes(out), nodes(y_tab), nodes(x1_tab)
        agg_v = [nodes(a) for a in agg_tab]

        ident = sb("ident", [128, 128])
        ones = sb("ones", [128, 128])
        ones3 = sb("ones3", [3, 128], BF16)
        below = sb("below", [P, 2, P])
        spare = sb("spare", [P, 2, GT])
        spare_i = sb("spare_i", [P, 2, GT], I32)
        zeros = sb("zeros", [128, ZR // ZC * D])
        w_raw = sb("w_raw", [128, 5, D])
        w_sum = sb("w_sum", [128, 5])
        w_mean = sb("w_mean", [128, 5])
        w_cen = sb("w_cen", [128, 5, D])
        w_blk = sb("w_blk", [128, LAYERS, 128])
        b_raw = sb("b_raw", [3, LAYERS, D])
        b_sum = sb("b_sum", [3, LAYERS])
        b_mean = sb("b_mean", [3, LAYERS])
        b_cen = sb("b_cen", [3, LAYERS, D])
        b_part = sb("b_part", [3, 3, LAYERS, D], BF16)
        b_rest = sb("b_rest", [3, 2, LAYERS, D])
        b_sel = sb("b_sel", [3, 3, LAYERS, D])
        b_row = sb("b_row", [3, LAYERS, GC, D], BF16)
        gain = sb("gain", [128, LAYERS])
        shift = sb("shift", [128, LAYERS])
        w_fs = sb("w_fs", [128, 2, 128])
        w_at = sb("w_at", [3 * GT, 2, GT * 128])
        bn_gb = sb("bn_gb", [P, 2, 2, D])
        end_i = sb("end_i", [P, 2, ECOL], I32)
        end_f = sb("end_f", [P, 2, ECOL])
        ew_s = sb("ew_s", [P, ECOL])
        at_s = sb("at_s", [P, ECOL, 2])
        to_i = sb("to_i", [P, ECOL], I32)
        g_idx = sb("g_idx", [P, 2, 2, GT], I32)
        s_idx = sb("s_idx", [P, 2, 2, GT], I32)
        e_key = sb("e_key", [P, 2, 2, GT])
        e_at = sb("e_at", [P, 2, GT, 3])
        e_buf = sb("e_buf", [128, 4, 2 * W])
        rows = e_buf[0:P, 0, :].rearrange("p (b k e d) -> p b k e d", b=2, k=GT, e=2)
        xc = e_buf[0:P, 1, :].rearrange("p (b w) -> p b w", b=2)
        sq = e_buf[0:P, 2, :].rearrange("p (b w) -> p b w", b=2)
        hw = e_buf[0:P, 3, :].rearrange("p (b k e d) -> p b k e d", b=2, k=GT, e=2)
        tiny = sb("tiny", [P, 2, 8, GC])
        same = sb("same", [P, 2, 2, 2 * P])
        junk = sb("junk", [P, 2 * P])
        repeat = sb("repeat", [P, 2, 2, GT])
        r_tmp = sb("r_tmp", [P, 2, 2, 2, GT])
        s_t = sb("s_t", [128, 2, 2 * P])
        v_buf = sb("v_buf", [128, 2, 2 * W])
        vals = v_buf[0:P, 0, :].rearrange("p (b k e d) -> p b k e d", b=2, k=GT, e=2)
        act_e = v_buf[0:P, 1, :].rearrange("p (a k d) -> p a k d", a=4, k=GT)
        area = sb("area", [128, EG * W])
        views = {}
        at = [0]

        def carve(name, n, width):
            views[name] = [area[:, at[0] + k * width:at[0] + (k + 1) * width] for k in range(n)]
            at[0] += n * width

        for name in ("x_even", "y_in", "z_sq", "z_nrm", "h_t", "x_out"):
            carve(name, 2, BW)
        at_m = at[0]
        at[0] = 0
        for name in ("l_x1", "l_a1", "l_a2", "l_xc", "l_sq", "l_a", "l_out"):
            carve(name, 2 if name in ("l_x1", "l_a1", "l_a2", "l_out") else 1, BLK * D)
        assert max(at[0], at_m) <= EG * W
        x_even, y_in, z_sq, z_nrm, h_t, x_out = (
            views[k] for k in ("x_even", "y_in", "z_sq", "z_nrm", "h_t", "x_out"))
        l_x1, l_a1, l_a2, l_xc, l_sq, l_a, l_out = (
            views[k] for k in ("l_x1", "l_a1", "l_a2", "l_xc", "l_sq", "l_a", "l_out"))
        h_keep = area
        blk_s = sb("blk", [128, 2, BLK * D])
        blk = [blk_s[:, k, :] for k in range(2)]
        x_in = [[x_even[u][0:P], e_buf[0:P, 2 * u:2 * u + 2, :].rearrange("p a w -> p (a w)")]
                for u in range(2)]
        x_sq = v_buf[0:P, :, :].rearrange("p a w -> p (a w)")
        x_nrm = [blk[u][0:P] for u in range(2)]
        m_stat = sb("m_stat", [P, 2, 9, Q * GC])
        zt = sb("zt", [128, W])
        at_t = sb("at_t", [3 * GT, 2, P])
        dve_e = sb("dve_e", [P, 3, GT, D])
        bn_w = sb("bn_w", [P, 10, D])
        f_stat = sb("f_stat", [P, 5, BLK])
        msg = sb("msg", [P, 2, GT, D])
        bn_x = sb("bn_x", [128, 8, 128])
        bn_s = sb("bn_s", [P, 2, 2, D])
        psum = [ctx.enter_context(nc.psum_tensor(f"bank{k}", [128, 512], F32)) for k in range(8)]

        names = """act_step pool_passed w_zero edges_ready w_ready consts iota_done loads_edges loads_w w_copied setup_done zero_tile y_clear agg_clear dve_step
            idx_ready key_ready a_rows0 a_rows1 a_xc a_sq a_hw a_r a_same a_t a_ts a_v a_vals a_sidx a_scattered
            m_x00 m_x01 m_x10 m_x11 m_y0 m_y1 m_mean0 m_mean1 m_xcen0 m_xcen1 m_xsq0 m_xsq1 m_xss0 m_xss1
            m_xrstd0 m_xrstd1 m_xnrm0 m_xnrm1 m_xt0 m_xt1 m_hin0 m_hin1 m_z0 m_z1 m_zsq0 m_zsq1 m_zss0 m_zss1
            m_rstd0 m_rstd1 m_zn0 m_zn1 m_zt0 m_zt1 m_h0 m_h1 m_back0 m_back1 m_out0 m_out1 m_stored0
            m_stored1 pool_step
            c_idx c_slots c_rows0 c_rows1 c_xc c_sq c_hw c_keep c_r c_same c_ht c_zt c_att c_atc c_z c_act c_msg
            c_v c_vals c_sidx c_scattered dve_back d_in0 d_in1 d_used d_gram bn_ready bn_sum bn_done
            f_in0 f_in1 f_mean f_xc f_sq f_a f_out f_stored0 f_stored1""".split()
        S = {name: sem(name) for name in names}
        block = ctx.enter_context(nc.Block())

        def halves(eng, dst_ap, src_ap, done):
            eng.dma_start(dst_ap[0:KA], src_ap[0:KA]).then_inc(done, 16)
            eng.dma_start(dst_ap[KA:P], src_ap[KA:P]).then_inc(done, 16)

        def b8(ap):
            return ap.unsqueeze(2).to_broadcast([ap.shape[0], ap.shape[1], D])

        def cols(ap):
            return ap.rearrange("p (c d) -> p c d", d=D)

        N_ZERO = 16 * ZC
        SETUP_POOL = 5
        N_LOADS_W = 1 + LAYERS * 7 + 2 * (2 * (1 + 2 * GT) + 2)
        D_PER = (32 * (NB - NB // 2), 32 * (NB // 2))

        @block.sync
        def _(sp):
            for e, v in ((0, dst), (1, src)):
                halves(sp, end_i[0:P, e, :], v.rearrange("(p t) -> p t", p=P), S["loads_edges"])
            halves(sp, ew_s[0:P, :], ew.rearrange("(p t) -> p t", p=P), S["loads_edges"])
            halves(sp, at_s[0:P, :, :], attr.rearrange("(p t) k -> p t k", p=P), S["loads_edges"])

            def clear(tab, k, done):
                v = tab.rearrange("(p c) d -> p (c d)", p=128)
                w = ZR // ZC * D
                sp.dma_start(v[:, bass.ds(k * w, w)], zeros[:, :]).then_inc(done, 16)

            sp.wait_ge(S["zero_tile"], 1)
            for k in range(ZC):
                clear(y_tab, k, S["y_clear"])

            sp.wait_ge(S["a_scattered"], 32 * ECOL)

            def batch_cols(j, u):
                return bass.ds((2 * j + u) * BW, BW)

            def load_batch(j, u, jp):
                if past(j, 2):
                    sp.wait_ge(S[f"m_out{u}"], Q * (j - 1))
                halves(sp, x_in[u][jp], x_v[:, batch_cols(j, u)], S[f"m_x{u}{jp}"])
                if past(j, 1):
                    sp.wait_ge(S[f"m_z{u}"], nth(0, j - 1, Q - 1))
                halves(sp, y_in[u], y_v[:, batch_cols(j, u)], S[f"m_y{u}"])

            for u in range(2):
                load_batch(0, u, 0)

            def mlp_turn(j, jp):
                for u in range(2):
                    if exists(j - 1, u):
                        sp.wait_ge(S[f"m_out{u}"], Q * j)
                        halves(sp, x1_v[:, batch_cols(j - 1, u)], x_out[u], S[f"m_stored{u}"])
                    if exists(j + 1, u):
                        load_batch(j + 1, u, 1 - jp)
                if not isinstance(j, int) or j < TURNS - 1:
                    for tab in agg_tab:
                        for k in range(2):
                            clear(tab, 2 * j + k, S["agg_clear"])

            by_pairs(sp, TURNS, mlp_turn, ahead=3)

            for i in range(2):
                sp.wait_ge(S["c_scattered"], 16 * ECOL * (i + 1))

                def agg_block(m, b, i=i):
                    n = i * NB + m
                    if i or not isinstance(m, int) or m >= 2:
                        wait(sp, S["d_used"], n - 1)
                    halves(sp, blk[b], agg_v[i][:, bass.ds(m * BLK * D, BLK * D)], S[f"d_in{b}"])

                by_pairs(sp, NB, agg_block)

            def last_load(m, b):
                if not isinstance(m, int) or m >= 2:
                    sp.wait_ge(S["f_out"], m - 1)
                at_c = m * BLK * D
                halves(sp, l_x1[b], x1_v[:, bass.ds(at_c, BLK * D)], S[f"f_in{b}"])
                halves(sp, l_a1[b], agg_v[0][:, bass.ds(at_c, BLK * D)], S[f"f_in{b}"])
                halves(sp, l_a2[b], agg_v[1][:, bass.ds(at_c, BLK * D)], S[f"f_in{b}"])

            sp.wait_ge(S["bn_done"], 2)
            last_load(0, 0)

            def last_block(m, b):
                if not isinstance(m, int) or m + 1 < NB:
                    last_load(m + 1, 1 - b)
                sp.wait_ge(S["f_out"], m + 1)
                halves(sp, out_v[:, bass.ds(m * BLK * D, BLK * D)], l_out[b], S[f"f_stored{b}"])

            by_pairs(sp, NB, last_block)
            for u in range(2):
                sp.wait_ge(S[f"m_stored{u}"], 32 * STREAM[u])
            sp.wait_ge(S["f_stored0"], 32 * (NB - NB // 2))
            sp.wait_ge(S["f_stored1"], 32 * (NB // 2))

        @block.gpsimd
        def _(pool):
            g = nc.gpsimd
            g.memset(ident[:, :], 0.0).then_inc(S["consts"], 1)
            g.memset(ones[:, :], 1.0).then_inc(S["consts"], 1)
            g.memset(below[:, :, :], 1.0).then_inc(S["consts"], 1)
            g.memset(ones3[:, :], 1.0).then_inc(S["consts"], 1)
            g.memset(e_at[:, :, :, :], 1.0).then_inc(S["consts"], 1)
            pool.wait_ge(S["consts"], SETUP_POOL)
            g.affine_select(out=ident[:, :], in_=ident[:, :], compare_op=ALU.not_equal, fill=1.0, base=0,
                            pattern=[[-1, 128]], channel_multiplier=1).then_inc(S["iota_done"], 1)
            g.affine_select(out=below[:, 1, :], in_=below[:, 1, :], compare_op=ALU.is_gt, fill=0.0, base=0,
                            pattern=[[-1, P]], channel_multiplier=1).then_inc(S["iota_done"], 1)
            g.iota(spare_i[:, :, :], pattern=[[P, 2], [0, GT]], base=N, channel_multiplier=1)\
                .then_inc(S["iota_done"], 1)

            def waits(*pairs):
                for sem_, x in pairs:
                    wait(pool, sem_, x)
                pool.sem_inc(S["pool_passed"], 1)

            def gather(tab, b, e, k, done):
                g.indirect_dma_start(
                    out=rows[:, b, k, e, :], out_offset=None, in_=tab[0:N, :],
                    in_offset=bass.IndirectOffsetOnAxis(ap=g_idx[:, b, e, k:k + 1], axis=0),
                    compute_op=ALU.bypass).then_inc(done, 16)

            def scatter(tab, b, e, k, done):
                g.indirect_dma_start(
                    out=tab[:, :], out_offset=bass.IndirectOffsetOnAxis(ap=s_idx[:, b, e, k:k + 1], axis=0),
                    in_=vals[:, b, k, e, :], in_offset=None, compute_op=ALU.add).then_inc(done, 16)

            def a_gathers(n, b, k):
                for e in range(2):
                    gather(x, b, e, k, S[f"a_rows{b}"])

            for n in range(2):
                pool.wait_ge(S["idx_ready"], n + 1)
                for k in range(GT):
                    a_gathers(n, n, k)
            pool.wait_ge(S["y_clear"], N_ZERO)

            def a_scatters(n, b, k):
                waits((S["a_sidx"], n + 1), (S["a_vals"], GT * n + k + 1),
                      (S["a_scattered"], 32 * (GT * n + k)))
                for e in range(2):
                    scatter(y_tab, b, e, k, S["a_scattered"])

            def a_group(n, b):
                more = not isinstance(n, int) or n + 2 < EG
                if more:
                    waits((S["idx_ready"], n + 3), (S["a_xc"], n + 1))
                for k in range(GT):
                    if more:
                        a_gathers(n + 2, b, k)
                    if past(n, 1):
                        a_scatters(n - 1, 1 - b, k)

            by_pairs(pool, EG, a_group)
            for k in range(GT):
                a_scatters(EG - 1, (EG - 1) % 2, k)

            step = Steps(pool, S["pool_step"])

            def inv_std(st, done):
                total, var, t, y = (st[:, k, :] for k in range(4))

                def scaled(o, i_, m, c):
                    return g.tensor_scalar(out=o, in0=i_, scalar1=m, scalar2=c, op0=ALU.mult, op1=ALU.add)

                def times(o, x_, y_):
                    return g.tensor_tensor(out=o, in0=x_, in1=y_, op=ALU.mult)

                def held(ins):
                    step(ins)
                    pool.sem_inc(S["pool_passed"], 1)

                held(scaled(var, total, 1.0 / D, EPS))
                step(scaled(y.bitcast(I32), var.bitcast(I32), -0.5, MAGIC))
                step(times(t, y, y))
                held(times(t, t, var))
                step(scaled(total, t, 0.375, -1.25))
                held(times(total, total, t))
                step(g.tensor_scalar(out=total, in0=total, scalar1=1.875, scalar2=1.0, op0=ALU.add, op1=ALU.mult))
                step(times(y, y, total))
                step(times(t, y, y))
                held(times(t, t, var))
                step(scaled(t, t, -0.5, 1.5))
                times(y, y, t).then_inc(done, 1)

            def center(u, j, par):
                pool.wait_ge(S[f"m_mean{u}"], j + 1)
                wait(pool, S[f"m_xt{u}"], Q * j)
                for q in range(Q):
                    c = slice(q * W, (q + 1) * W)
                    g.tensor_tensor(out=cols(x_nrm[u][:, c]), in0=cols(x_in[u][par][:, c]),
                                    in1=b8(m_stat[:, u, 0, q * GC:(q + 1) * GC]), op=ALU.subtract)\
                        .then_inc(S[f"m_xcen{u}"], 1)

            def x_std(u, j):
                waits((S[f"m_xss{u}"], j + 1),)
                inv_std(m_stat[:, u, 1:5], S[f"m_xrstd{u}"])

            def x_scale(u, j, groups):
                pool.wait_ge(S[f"m_xrstd{u}"], j + 1)
                for q in groups:
                    c = slice(q * W, (q + 1) * W)
                    g.tensor_tensor(out=cols(x_nrm[u][:, c]), in0=cols(x_nrm[u][:, c]),
                                    in1=b8(m_stat[:, u, 4, q * GC:(q + 1) * GC]), op=ALU.mult)\
                        .then_inc(S[f"m_xnrm{u}"], 1)

            step.begin(0)
            for u in range(2):
                center(u, 0, 0)
            for u in range(2):
                x_std(u, 0)
                x_scale(u, 0, range(Q))
            step.phase()

            def m_turn(j, jp):
                step.begin(j)
                for k in range(STEPS):
                    if unit(k, j):
                        u, l, _ = unit(k, j)
                        waits((S[f"m_zss{u}"], nth(l, j, Q - 1)),)
                        inv_std(m_stat[:, u, 5:9], S[f"m_rstd{u}"])
                    more = [exists(j + 1, u) for u in range(2)]
                    if k in (2, 3) and more[k - 2]:
                        center(k - 2, j + 1, 1 - jp)
                    if k in (4, 5) and more[k - 4]:
                        x_std(k - 4, j + 1)
                    if k in (5, 6) and more[0]:
                        x_scale(0, j + 1, (0, 1) if k == 5 else (2, 3))
                    if k in (6, 7) and more[1]:
                        x_scale(1, j + 1, (0, 1) if k == 6 else (2, 3))

            by_pairs(pool, TURNS, m_turn, ahead=3)
            step.phase()

            for u in range(2):
                pool.wait_ge(S[f"m_stored{u}"], 32 * STREAM[u])
            for i in range(2):
                tab = x1_tab if i == 0 else agg_tab[0]

                def c_gathers(n, b, k, tab=tab):
                    for e in range(2):
                        gather(tab, b, e, k, S[f"c_rows{b}"])

                base = i * EG
                if i:
                    pool.wait_ge(S["c_xc"], base)
                    pool.wait_ge(S["c_scattered"], 16 * ECOL)
                for n in range(2):
                    pool.wait_ge(S["c_idx"], base + n + 1)
                    for k in range(GT):
                        c_gathers(n, n, k)
                pool.wait_ge(S["agg_clear"], N_ZERO * 2)

                def c_group(n, b, i=i, base=base, c_gathers=c_gathers):
                    more = not isinstance(n, int) or n + 2 < EG
                    if more:
                        waits((S["c_idx"], base + n + 3), (S["c_xc"], base + n + 1))
                    for k in range(GT):
                        if more:
                            c_gathers(n + 2, b, k)
                        if past(n, 1):
                            c_scatter(n - 1, 1 - b, k)

                def c_scatter(n, b, k, i=i, base=base):
                    if k == 0:
                        waits((S["c_sidx"], base + n + 1), (S["c_vals"], base + n + 1))
                    waits((S["c_scattered"], 16 * (GT * (base + n) + k)),)
                    scatter(agg_tab[i], b, 0, k, S["c_scattered"])

                by_pairs(pool, EG, c_group)
                for k in range(GT):
                    c_scatter(EG - 1, (EG - 1) % 2, k)

            def f_block(m, b):
                pool.wait_ge(S["f_mean"], m + 1)
                wait(pool, S["f_a"], m)
                g.tensor_tensor(out=cols(l_xc[0][0:P]), in0=cols(l_x1[b][0:P]), in1=b8(f_stat[:, 0, :]),
                                op=ALU.subtract).then_inc(S["f_xc"], 1)

            by_pairs(pool, NB, f_block)

        def newton(step, var, y, t):
            v = nc.vector
            step(v.tensor_scalar(out=y.bitcast(I32), in0=var.bitcast(I32), scalar1=-0.5, scalar2=MAGIC,
                                 op0=ALU.mult, op1=ALU.add))
            for _ in range(3):
                step(v.scalar_tensor_tensor(out=t, in0=y, scalar=-0.5, in1=y, op0=ALU.mult, op1=ALU.mult))
                step(v.tensor_tensor(out=t, in0=t, in1=var, op=ALU.mult))
                step(v.scalar_tensor_tensor(out=y, in0=t, scalar=1.5, in1=y, op0=ALU.add, op1=ALU.mult))

        def pair(rows_b):
            return rows_b.rearrange("p k e d -> p (k e) d")

        @block.vector
        def _(dve):
            v = nc.vector
            step, back = Steps(dve, S["dve_step"]), Steps(dve, S["dve_back"])
            step.begin(0)

            v.memset(zeros[:, :], 0.0).then_inc(S["zero_tile"], 1)
            v.memset(w_blk[:, :, :], 0.0).then_inc(S["w_zero"], 1)
            v.memset(w_at[:, :, :], 0.0).then_inc(S["w_zero"], 1)
            dve.wait_ge(S["iota_done"], 3)
            v.tensor_copy(spare[:, :, :], spare_i[:, :, :]).then_inc(S["w_zero"], 1)
            dve.wait_ge(S["loads_edges"], 128)
            v.tensor_copy(end_f[:, :, :], end_i[:, :, :]).then_inc(S["edges_ready"], 1)
            dve.wait_ge(S["loads_w"], 16 * N_LOADS_W)
            step(v.tensor_reduce(out=w_sum[:, :], in_=w_raw[:, :, :], axis=AX.X, op=ALU.add))
            step(v.tensor_scalar(out=w_mean[:, :], in0=w_sum[:, :], scalar1=1.0 / D, scalar2=None, op0=ALU.mult))
            step(v.tensor_tensor(out=w_cen[:, :, :], in0=w_raw[:, :, :], in1=b8(w_mean[:, :]), op=ALU.subtract))
            dve.wait_ge(S["w_zero"], 3)
            step(v.tensor_copy(w_blk[0:D, :, 0:D], w_cen[0:D, 1:5, :]))
            step(v.tensor_copy(w_blk[D:128, :, D:128], w_cen[D:128, 1:5, :]))
            step(v.tensor_reduce(out=b_sum[:, :], in_=b_raw[:, :, :], axis=AX.X, op=ALU.add))
            step(v.tensor_scalar(out=b_mean[:, :], in0=b_sum[:, :], scalar1=1.0 / D, scalar2=None, op0=ALU.mult))
            step(v.tensor_tensor(out=b_cen[:, :, :], in0=b_raw[:, :, :], in1=b8(b_mean[:, :]), op=ALU.subtract))
            step(v.tensor_copy(b_part[:, 0], b_cen[:, :, :]))
            step(v.tensor_tensor(out=b_rest[:, 0], in0=b_cen[:, :, :], in1=b_part[:, 0], op=ALU.subtract))
            step(v.tensor_copy(b_part[:, 1], b_rest[:, 0]))
            step(v.tensor_tensor(out=b_rest[:, 1], in0=b_rest[:, 0], in1=b_part[:, 1], op=ALU.subtract))
            step(v.tensor_copy(b_part[:, 2], b_rest[:, 1]))
            step(v.tensor_scalar(out=b_sel[:, 0], in0=b_part[:, 0], scalar1=ident[0:3, 0:1], scalar2=None,
                                 op0=ALU.mult))
            for k in (1, 2):
                step(v.scalar_tensor_tensor(out=b_sel[:, k], in0=b_part[:, k], scalar=ident[0:3, k:k + 1],
                                            in1=b_sel[:, k - 1], op0=ALU.mult, op1=ALU.add))
            for l in range(LAYERS):
                step(v.tensor_copy(b_row[:, l], b_sel[:, 2, l].unsqueeze(1).to_broadcast([3, GC, D])))
            v.tensor_copy(b_sum[0:1, 0:1], b_mean[0:1, 0:1]).then_inc(S["w_ready"], 1)
            step.phase()

            def a_group(n, b):
                step.begin(n)
                st = tiny[:, b]
                dve.wait_ge(S[f"a_rows{b}"], (n - b) * 64 + 128)
                step(v.tensor_reduce(out=st[:, 0, :], in_=pair(rows[:, b]), axis=AX.X, op=ALU.add))
                step(v.tensor_scalar(out=st[:, 1, :], in0=st[:, 0, :], scalar1=1.0 / D, scalar2=None,
                                     op0=ALU.mult))
                v.tensor_tensor(out=cols(xc[:, b]), in0=pair(rows[:, b]), in1=b8(st[:, 1, :]),
                                op=ALU.subtract).then_inc(S["a_xc"], 1)
                for k in range(GT):
                    t = GT * n + k
                    dve.wait_ge(S["a_r"], t + 1)
                    wait(dve, S["a_t"], t - 1)
                    for e in range(2):
                        v.tensor_scalar(out=same[:, k % 2, e, :], in0=psum[k % 2][0:P, 0:2 * P],
                                        scalar1=e_key[:, b, e, k:k + 1], scalar2=None, op0=ALU.is_equal)\
                            .then_inc(S["a_same"], 1)
                    dve.wait_ge(S["a_same"], 2 * t + 2)
                    step(v.tensor_tensor_reduce(out=junk[:, 0:P], in0=same[:, k % 2, 0, 0:P],
                                                in1=below[:, 1, :], scale=1.0, scalar=0.0, op0=ALU.mult,
                                                op1=ALU.add, accum_out=repeat[:, b, 0, k:k + 1]))
                    step(v.tensor_tensor_reduce(out=junk[:, :], in0=same[:, k % 2, 1, :],
                                                in1=below[:, :, :].rearrange("p a i -> p (a i)"), scale=1.0,
                                                scalar=0.0, op0=ALU.mult, op1=ALU.add,
                                                accum_out=repeat[:, b, 1, k:k + 1]))
                    if k == 0:
                        dve.wait_ge(S["a_sq"], n + 1)
                        step(v.tensor_reduce(out=st[:, 2, :], in_=cols(sq[:, b]), axis=AX.X, op=ALU.add))
                        step(v.tensor_scalar(out=st[:, 3, :], in0=st[:, 2, :], scalar1=1.0 / D, scalar2=EPS,
                                             op0=ALU.mult, op1=ALU.add))
                        newton(step, st[:, 3, :], st[:, 4, :], st[:, 5, :])
                        step(v.tensor_tensor(out=st[:, 6, :].rearrange("p (k e) -> p k e", e=2),
                                             in0=st[:, 4, :].rearrange("p (k e) -> p k e", e=2),
                                             in1=ew_s[:, bass.ds(GT * n, GT)].unsqueeze(2)
                                             .to_broadcast([P, GT, 2]), op=ALU.mult))
                        wait(dve, S["a_t"], GT * (n - 1))
                        v.scalar_tensor_tensor(out=pair(hw[:, b]), in0=cols(xc[:, b]), scalar=0.0,
                                               in1=b8(st[:, 6, :]), op0=ALU.max, op1=ALU.mult)\
                            .then_inc(S["a_hw"], 1)
                tmp = r_tmp[:, b]
                step(v.tensor_tensor(out=tmp[:, 0], in0=spare[:, :, :], in1=e_key[:, b], op=ALU.subtract))
                step(v.scalar_tensor_tensor(out=tmp[:, 1], in0=repeat[:, b], scalar=1.0, in1=tmp[:, 0],
                                            op0=ALU.min, op1=ALU.mult))
                wait(dve, S["a_scattered"], 32 * GT * (n - 1))
                v.tensor_tensor(out=s_idx[:, b], in0=tmp[:, 1], in1=e_key[:, b], op=ALU.add)\
                    .then_inc(S["a_sidx"], 1)
                dve.wait_ge(S["a_sidx"], n + 1)
                step(v.tensor_copy(to_i[:, bass.ds(GT * n, GT)], s_idx[:, b, 0]))

            by_pairs(dve, EG, a_group)
            step.phase()

            dve.wait_ge(S["a_scattered"], 32 * ECOL)

            def x_mean(u, j, par):
                dve.wait_ge(S[f"m_x{u}{par}"], (j - par) * 16 + 32)
                step(v.tensor_reduce(out=m_stat[:, u, 0, :], in_=cols(x_in[u][par]), axis=AX.X, op=ALU.add))
                v.tensor_scalar(out=m_stat[:, u, 0, :], in0=m_stat[:, u, 0, :], scalar1=1.0 / D, scalar2=None,
                                op0=ALU.mult).then_inc(S[f"m_mean{u}"], 1)

            def x_squares(u, j):
                dve.wait_ge(S[f"m_xsq{u}"], j + 1)
                v.tensor_reduce(out=m_stat[:, u, 1, :], in_=cols(x_sq), axis=AX.X, op=ALU.add)\
                    .then_inc(S[f"m_xss{u}"], 1)

            step.begin(0)
            for u in range(2):
                x_mean(u, 0, 0)
            for u in range(2):
                x_squares(u, 0)
            step.phase()

            def reduce_sq(u, l, j, q):
                dve.wait_ge(S[f"m_zsq{u}"], nth(l, j, q))
                v.tensor_reduce(out=m_stat[:, u, 5, q * GC:(q + 1) * GC], in_=cols(z_sq[u][0:P, q * W:(q + 1) * W]),
                                axis=AX.X, op=ALU.add).then_inc(S[f"m_zss{u}"], 1)

            def scale(u, l, j, q):
                dve.wait_ge(S[f"m_rstd{u}"], LAYERS * j + l + 1)
                wait(dve, S[f"m_zt{u}"], nth(l, j, q) - Q)
                v.tensor_tensor(out=cols(z_nrm[u][0:P, q * W:(q + 1) * W]), in0=cols(psum[4 * u + q][0:P, :]),
                                in1=b8(m_stat[:, u, 8, q * GC:(q + 1) * GC]), op=ALU.mult)\
                    .then_inc(S[f"m_zn{u}"], 1)

            def m_turn(j, jp):
                step.begin(j)
                for k in range(STEPS):
                    u, l = k % 2, k // 2
                    if l == 0 and exists(j - 1, u):
                        for q in range(Q):
                            c = slice(q * W, (q + 1) * W)
                            dve.wait_ge(S[f"m_back{u}"], Q * (j - 1) + q + 1)
                            if past(j, 2):
                                dve.wait_ge(S[f"m_stored{u}"], 32 * (j - 1))
                            v.tensor_tensor(out=x_out[u][0:P, c], in0=psum[4 * u + q][0:P, :],
                                            in1=x_in[u][1 - jp][:, c], op=ALU.add).then_inc(S[f"m_out{u}"], 1)
                    this, before = unit(k, j), unit(k - 1, j)
                    for reduced, scaled in ((0, 0), (1, 1), (2, 2), (None, 3), (3, None)):
                        if this and reduced is not None:
                            reduce_sq(*this, reduced)
                        if before and scaled is not None:
                            scale(*before, scaled)
                    if k in (1, 2) and exists(j + 1, k - 1):
                        x_mean(k - 1, j + 1, 1 - jp)
                    if k in (3, 4) and exists(j + 1, k - 3):
                        x_squares(k - 3, j + 1)

            by_pairs(dve, TURNS, m_turn, ahead=3)
            step.phase()

            for i in range(2):
                base = i * EG
                if i:
                    dve.wait_ge(S["bn_done"], 1)

                def c_front(n, b, i=i, base=base):
                    step.begin(n)
                    c = n + base
                    st = tiny[:, b]
                    dve.wait_ge(S[f"c_rows{b}"], i * EG * 64 + (n - b) * 64 + 128)
                    if i == 0:
                        step(v.tensor_reduce(out=st[:, 0, :], in_=pair(rows[:, b]), axis=AX.X, op=ALU.add))
                        step(v.tensor_scalar(out=st[:, 1, :], in0=st[:, 0, :], scalar1=1.0 / D, scalar2=None,
                                             op0=ALU.mult))
                        v.tensor_tensor(out=cols(xc[:, b]), in0=pair(rows[:, b]), in1=b8(st[:, 1, :]),
                                        op=ALU.subtract).then_inc(S["c_xc"], 1)
                    else:
                        v.tensor_tensor(out=cols(xc[:, b]), in0=pair(rows[:, b]),
                                        in1=bn_s[:, 0, 0, :].unsqueeze(1).to_broadcast([P, GC, D]),
                                        op=ALU.mult).then_inc(S["c_xc"], 1)
                    for k in range(GT):
                        t = GT * c + k
                        dve.wait_ge(S["c_r"], t + 1)
                        wait(dve, S["c_v"], t + 1 - 2 * GT)
                        v.tensor_scalar(out=same[:, k // 2, k % 2, b * P:(b + 1) * P], in0=psum[k % 2][0:P, 0:P],
                                        scalar1=e_key[:, b, 0, k:k + 1], scalar2=None, op0=ALU.is_equal)\
                            .then_inc(S["c_same"], 1)
                    if i == 0:
                        dve.wait_ge(S["c_sq"], c + 1)
                        step(v.tensor_reduce(out=st[:, 2, :], in_=cols(sq[:, b]), axis=AX.X, op=ALU.add))
                        step(v.tensor_scalar(out=st[:, 3, :], in0=st[:, 2, :], scalar1=1.0 / D, scalar2=EPS,
                                             op0=ALU.mult, op1=ALU.add))
                        newton(step, st[:, 3, :], st[:, 4, :], st[:, 5, :])
                        wait(dve, S["c_ht"], c - 1)
                        wait(dve, S["c_keep"], c - 1)
                        v.scalar_tensor_tensor(out=pair(hw[:, b]), in0=cols(xc[:, b]), scalar=0.0,
                                               in1=b8(st[:, 4, :]), op0=ALU.max, op1=ALU.mult)\
                            .then_inc(S["c_hw"], 1)
                    else:
                        dve.wait_ge(S["c_xc"], c + 1)
                        step(v.tensor_tensor(out=sq[:, b], in0=xc[:, b],
                                             in1=h_keep[0:P, bass.ds(n * W, W)], op=ALU.add))
                        wait(dve, S["c_ht"], c - 1)
                        v.tensor_tensor(out=pair(hw[:, b]), in0=cols(sq[:, b]),
                                        in1=bn_s[:, 0, 1, :].unsqueeze(1).to_broadcast([P, GC, D]),
                                        op=ALU.add).then_inc(S["c_hw"], 1)

                def c_back(n, b, base=base):
                    back.begin(n)
                    c = n + base
                    dve.wait_ge(S["c_act"], c + 1)
                    z = psum[4 + b][0:P, :].rearrange("p (k w) -> p k w", w=128)
                    back(v.tensor_scalar(out=dve_e[:, 0], in0=act_e[:, 0], scalar1=1.0, scalar2=None,
                                         op0=ALU.add))
                    back(v.reciprocal(out=dve_e[:, 1], in_=dve_e[:, 0]))
                    back(v.scalar_tensor_tensor(out=dve_e[:, 2], in0=z[:, :, D:], scalar=0.0, in1=act_e[:, 3],
                                                op0=ALU.max, op1=ALU.add))
                    wait(dve, S["c_v"], GT * (c - 1))
                    v.tensor_tensor(out=msg[:, b], in0=dve_e[:, 2], in1=dve_e[:, 1], op=ALU.mult)\
                        .then_inc(S["c_msg"], 1)

                one_behind(dve, EG, c_front, c_back)
                step.phase()
                back.phase()

                step.begin(0)
                dve.wait_ge(S["d_used"], NB * (i + 1))
                v.tensor_tensor(out=bn_x[:, 0], in0=psum[0][:, 0:128], in1=ident[:, :], op=ALU.mult)\
                    .then_inc(S["bn_ready"], 1)
                v.tensor_scalar(out=bn_x[:, 1], in0=ident[:, :], scalar1=psum[7][:, 0:1], scalar2=None,
                                op0=ALU.mult).then_inc(S["bn_ready"], 1)
                dve.wait_ge(S["bn_sum"], i + 1)
                step(v.tensor_copy(bn_w[:, 0:4, :], psum[1][0:P, 0:256].rearrange("p (a d) -> p a d", d=D)))
                sums = bn_w[:, 0:4, :].rearrange("p (a h) d -> p a h d", h=2)
                step(v.tensor_tensor(out=bn_w[:, 4:6, :], in0=sums[:, :, 0, :], in1=sums[:, :, 1, :], op=ALU.add))
                step(v.tensor_scalar(out=bn_w[:, 4:6, :], in0=bn_w[:, 4:6, :], scalar1=1.0 / N, scalar2=None,
                                     op0=ALU.mult))
                step(v.tensor_tensor(out=bn_w[:, 6, :], in0=bn_w[:, 5, :], in1=bn_w[:, 5, :], op=ALU.mult))
                step(v.tensor_tensor(out=bn_w[:, 7, :], in0=bn_w[:, 4, :], in1=bn_w[:, 6, :], op=ALU.subtract))
                step(v.tensor_scalar(out=bn_w[:, 7, :], in0=bn_w[:, 7, :], scalar1=0.0, scalar2=EPS,
                                     op0=ALU.max, op1=ALU.add))
                newton(step, bn_w[:, 7, :], bn_w[:, 8, :], bn_w[:, 9, :])
                step(v.tensor_tensor(out=bn_s[:, i, 0, :], in0=bn_w[:, 8, :], in1=bn_gb[:, i, 0, :], op=ALU.mult))
                step(v.tensor_tensor(out=bn_w[:, 9, :], in0=bn_w[:, 5, :], in1=bn_s[:, i, 0, :], op=ALU.mult))
                v.tensor_tensor(out=bn_s[:, i, 1, :], in0=bn_gb[:, i, 1, :], in1=bn_w[:, 9, :],
                                op=ALU.subtract).then_inc(S["bn_done"], 1)
                dve.wait_ge(S["bn_done"], i + 1)
                step.phase()

            def spread(i, k):
                return bn_s[:, i, k, :].unsqueeze(1).to_broadcast([P, BLK, D])

            def f_block(m, b):
                step.begin(m)
                dve.wait_ge(S[f"f_in{b}"], (m - b) * 48 + 96)
                wait(dve, S["f_xc"], m)
                step(v.tensor_reduce(out=f_stat[:, 0, :], in_=cols(l_x1[b][0:P]), axis=AX.X, op=ALU.add))
                v.tensor_scalar(out=f_stat[:, 0, :], in0=f_stat[:, 0, :], scalar1=1.0 / D, scalar2=None,
                                op0=ALU.mult).then_inc(S["f_mean"], 1)
                agg1, agg2, a = cols(l_a1[b][0:P]), cols(l_a2[b][0:P]), cols(l_a[0][0:P])
                step(v.tensor_tensor(out=a, in0=agg1, in1=spread(0, 0), op=ALU.mult))
                step(v.tensor_tensor(out=a, in0=a, in1=spread(0, 1), op=ALU.add))
                step(v.tensor_tensor(out=agg2, in0=agg2, in1=spread(1, 0), op=ALU.mult))
                step(v.tensor_tensor(out=agg2, in0=agg2, in1=spread(1, 1), op=ALU.add))
                dve.wait_ge(S["f_sq"], m + 1)
                step(v.tensor_reduce(out=f_stat[:, 1, :], in_=cols(l_sq[0][0:P]), axis=AX.X, op=ALU.add))
                step(v.tensor_scalar(out=f_stat[:, 2, :], in0=f_stat[:, 1, :], scalar1=1.0 / D, scalar2=EPS,
                                     op0=ALU.mult, op1=ALU.add))
                newton(step, f_stat[:, 2, :], f_stat[:, 3, :], f_stat[:, 4, :])
                v.scalar_tensor_tensor(out=agg1, in0=cols(l_xc[0][0:P]), scalar=0.0, in1=b8(f_stat[:, 3, :]),
                                       op0=ALU.max, op1=ALU.mult).then_inc(S["f_a"], 1)
                dve.wait_ge(S["f_a"], m + 1)
                step(v.tensor_tensor(out=a, in0=a, in1=agg1, op=ALU.add))
                step(v.scalar_tensor_tensor(out=agg2, in0=a, scalar=0.0, in1=agg2, op0=ALU.max, op1=ALU.add))
                wait(dve, S[f"f_stored{b}"], (m - b) * 16)
                v.scalar_tensor_tensor(out=cols(l_out[b][0:P]), in0=agg2, scalar=0.0, in1=cols(l_x1[b][0:P]),
                                       op0=ALU.max, op1=ALU.add).then_inc(S["f_out"], 1)

            by_pairs(dve, NB, f_block)

        @block.scalar
        def _(act):
            a = nc.scalar
            step = Steps(act, S["act_step"])

            def load(dst_ap, src_ap):
                act.dma_start(dst_ap, src_ap).then_inc(S["loads_w"], 16)
                n_loads[0] += 1

            n_loads = [0]
            load(w_raw[:, 0, :], mlp["W1"][0:128, :])
            for l in range(LAYERS):
                w = mlp["W1"][128:192, :] if l == 0 else mlp[f"W{l + 1}"]
                for h in range(2):
                    load(w_raw[h * D:(h + 1) * D, 1 + l, :], w)
                    load(gain[h * D:(h + 1) * D, l:l + 1], mlp[f"g{l + 1}"].unsqueeze(1))
                    load(shift[h * D:(h + 1) * D, l:l + 1], mlp[f"be{l + 1}"].unsqueeze(1))
                load(b_raw[:, l, :], mlp[f"b{l + 1}"].unsqueeze(0).to_broadcast([3, D]))
            act.wait_ge(S["w_zero"], 2)
            for i in range(2):
                c = conv[i]
                for h, (wn, bn) in enumerate((("Wf", "bf"), ("Ws", "bs"))):
                    load(w_fs[:, i, h * D:(h + 1) * D], c[wn][0:128, :])
                    for k in range(GT):
                        to = slice(k * 128 + h * D, k * 128 + (h + 1) * D)
                        load(w_at[3 * k:3 * k + 2, i, to], c[wn][128:130, :])
                        load(w_at[3 * k + 2:3 * k + 3, i, to], c[bn].unsqueeze(0))
                for k, name in enumerate(("gamma", "beta")):
                    load(bn_gb[:, i, k, :], c[name].unsqueeze(0).to_broadcast([P, D]))
            assert n_loads[0] == N_LOADS_W

            act.wait_ge(S["edges_ready"], 1)

            def copy(o, i_):
                return a.activation(o, i_, ACT.Copy)

            def group_of(table, n):
                return table[:, :, bass.ds(GT * n, GT)]

            for n in range(2):
                copy(g_idx[:, n], group_of(end_i, n)).then_inc(S["idx_ready"], 1)

            copy(e_key[:, 0], group_of(end_f, 0)).then_inc(S["key_ready"], 1)
            act.wait_ge(S["a_rows0"], 128)
            copy(g_idx[:, 0], group_of(end_i, 2)).then_inc(S["idx_ready"], 1)

            def a_group(n, b):
                act.wait_ge(S["a_xc"], n + 1)
                a.activation(sq[:, b], xc[:, b], ACT.Square).then_inc(S["a_sq"], 1)
                for k in range(GT):
                    t = GT * n + k
                    act.wait_ge(S["a_t"], t + 1)
                    wait(act, S["a_v"], t - 1)
                    copy(s_t[:, k % 2, :], psum[2 + k % 2][:, 0:2 * P]).then_inc(S["a_ts"], 1)
                    act.wait_ge(S["a_v"], t + 1)
                    wait(act, S["a_scattered"], 32 * (t + 1 - 2 * GT))
                    copy(vals[:, b, k].rearrange("p e d -> p (e d)"), psum[4 + k % 2][0:P, 0:2 * D])\
                        .then_inc(S["a_vals"], 1)
                    if k == 0 and (not isinstance(n, int) or n + 1 < EG):
                        wait(act, S["a_sidx"], n)
                        copy(e_key[:, 1 - b], group_of(end_f, n + 1)).then_inc(S["key_ready"], 1)
                    if k == 2 and (not isinstance(n, int) or n + 3 < EG):
                        act.wait_ge(S[f"a_rows{1 - b}"], (n + b) * 64 + 128)
                        copy(g_idx[:, 1 - b], group_of(end_i, n + 3)).then_inc(S["idx_ready"], 1)

            by_pairs(act, EG, a_group, ahead=3)

            def x_squares(u, j):
                act.wait_ge(S[f"m_xcen{u}"], Q * (j + 1))
                wait(act, S["m_xss0"], j + u)
                wait(act, S["m_xss1"], j)
                a.activation(x_sq, x_nrm[u], ACT.Square).then_inc(S[f"m_xsq{u}"], 1)

            for u in range(2):
                x_squares(u, 0)

            def m_turn(j, jp):
                for k in range(STEPS):
                    this, before = unit(k, j), unit(k - 1, j)
                    if this:
                        u, l, _ = this
                        if l == 0:
                            for q in range(Q):
                                act.wait_ge(S[f"m_xt{u}"], Q * j + q + 1)
                                a.activation(h_t[u][:, q * W:q * W + Q * P], psum[4 * u + q][:, 0:Q * P], ACT.Relu)\
                                    .then_inc(S[f"m_hin{u}"], 1)
                        for q in range(Q):
                            act.wait_ge(S[f"m_z{u}"], nth(l, j, q))
                            wait(act, S[f"m_zss{u}"], nth(l, j, q) - Q)
                            a.activation(z_sq[u][0:P, q * W:(q + 1) * W], psum[4 * u + q][0:P, :], ACT.Square)\
                                .then_inc(S[f"m_zsq{u}"], 1)
                    if before:
                        u, l, jb = before
                        for q in range(Q):
                            act.wait_ge(S[f"m_zt{u}"], nth(l, jb, q))
                            a.activation(h_t[u][:, q * W:q * W + Q * P], psum[4 * u + q][:, 0:Q * P], ACT.Tanh,
                                         bias=shift[:, l:l + 1], scale=gain[:, l:l + 1]).then_inc(S[f"m_h{u}"], 1)
                    if k in (3, 4) and exists(j + 1, k - 3):
                        x_squares(k - 3, j + 1)

            by_pairs(act, TURNS, m_turn, ahead=3)

            for i in range(2):
                base = i * EG
                if i:
                    act.wait_ge(S["c_rows1"], EG * 64)
                    act.wait_ge(S["c_rows0"], EG * 64)
                for n in range(2):
                    copy(g_idx[:, n], group_of(end_i, n)).then_inc(S["c_idx"], 1)

                def c_slots(n, b, base=base):
                    c = n + base
                    wait(act, S["c_same"], GT * (c - 1))
                    copy(e_key[:, b], group_of(end_f, n)).then_inc(S["c_slots"], 1)
                    wait(act, S["c_att"], c - 1)
                    copy(e_at[:, b, :, 0:2], at_s[:, bass.ds(GT * n, GT), :]).then_inc(S["c_slots"], 1)

                c_slots(0, 0)
                act.wait_ge(S["c_rows0"], i * EG * 64 + 128)
                copy(g_idx[:, 0], group_of(end_i, 2)).then_inc(S["c_idx"], 1)

                def c_body(n, b, i=i, base=base, c_slots=c_slots):
                    c = n + base
                    if i == 0:
                        act.wait_ge(S["c_xc"], c + 1)
                        a.activation(sq[:, b], xc[:, b], ACT.Square).then_inc(S["c_sq"], 1)
                    act.wait_ge(S["c_att"], c + 1)
                    copy(at_t[:, b, :], psum[3][0:3 * GT, 0:P]).then_inc(S["c_atc"], 1)
                    if not isinstance(n, int) or n + 1 < EG:
                        c_slots(n + 1, 1 - b)
                    if past(n, 1):
                        c_messages(n - 1, 1 - b)
                    act.wait_ge(S["c_ht"], c + 1)
                    wait(act, S["c_z"], c)
                    a.activation(zt[:, 0:Q * P], psum[2][:, 0:Q * P], ACT.Relu).then_inc(S["c_zt"], 1)
                    if i == 0:
                        act.wait_ge(S["c_hw"], c + 1)
                        copy(h_keep[0:P, bass.ds(n * W, W)], hw[:, b].rearrange("p k e d -> p (k e d)"))\
                            .then_inc(S["c_keep"], 1)
                    if not isinstance(n, int) or n + 3 < EG:
                        act.wait_ge(S[f"c_rows{1 - b}"], i * EG * 64 + (n + b) * 64 + 128)
                        copy(g_idx[:, 1 - b], group_of(end_i, n + 3)).then_inc(S["c_idx"], 1)
                    if past(n, 1):
                        c_results(n - 1, 1 - b)

                def c_messages(n, b, base=base):
                    c = n + base
                    step.begin(n)
                    act.wait_ge(S["c_z"], c + 1)
                    wait(act, S["c_msg"], c)
                    z = psum[4 + b][0:P, :].rearrange("p (k w) -> p k w", w=128)
                    step(a.activation(act_e[:, 1], z[:, :, D:], ACT.Abs))
                    step(a.activation(act_e[:, 2], act_e[:, 1], ACT.Exp, scale=-1.0))
                    a.activation(act_e[:, 3], act_e[:, 2], ACT.Ln, bias=ones[0:P, 0:1])
                    a.activation(act_e[:, 0], z[:, :, 0:D], ACT.Exp, scale=-1.0).then_inc(S["c_act"], 1)

                def c_results(n, b, base=base):
                    c = n + base
                    wait(act, S["c_scattered"], 16 * GT * (c - 1))
                    copy(s_idx[:, b, 0], to_i[:, bass.ds(GT * n, GT)]).then_inc(S["c_sidx"], 1)
                    act.wait_ge(S["c_v"], GT * (c + 1))
                    copy(vals[:, b, :, 0, :], psum[6][0:P, 0:GT * D].rearrange("p (k d) -> p k d", d=D))\
                        .then_inc(S["c_vals"], 1)

                by_pairs(act, EG, c_body, ahead=3)
                c_messages(EG - 1, (EG - 1) % 2)
                c_results(EG - 1, (EG - 1) % 2)
                step.phase()

            def f_block(m, b):
                act.wait_ge(S["f_xc"], m + 1)
                wait(act, S["f_a"], m)
                a.activation(l_sq[0][0:P], l_xc[0][0:P], ACT.Square).then_inc(S["f_sq"], 1)

            by_pairs(act, NB, f_block)

        @block.tensor
        def _(pe):
            t_ = nc.tensor
            pe.wait_ge(S["iota_done"], 3)
            pe.wait_ge(S["w_ready"], 1)
            idp = ident[0:P, 0:P]

            def key_row(b, e, k, bank, at_c):
                return t_.matmul(bank[0:P, at_c:at_c + P], e_key[:, b, e, k:k + 1].to_broadcast([P, P]), idp,
                                 start=True, stop=True)

            def a_keys(n, b, tiles):
                for k in tiles:
                    wait(pe, S["a_same"], 2 * (GT * n + k) - 2)
                    for e in range(2):
                        last = key_row(b, e, k, psum[k % 2], e * P)
                    last.then_inc(S["a_r"], 1)

            pe.wait_ge(S["key_ready"], 1)
            a_keys(0, 0, (0, 1))

            def a_group(n, b):
                a_keys(n, b, (2, 3))
                pe.wait_ge(S["a_hw"], n + 1)
                for k in range(GT):
                    t = GT * n + k
                    pe.wait_ge(S["a_same"], 2 * t + 2)
                    wait(pe, S["a_ts"], t - 1)
                    t_.matmul(psum[2 + k % 2][0:D, 0:2 * P], hw[:, b, k, 1, :], same[:, k % 2, 0, :],
                              start=True, stop=True)
                    t_.matmul(psum[2 + k % 2][D:128, 0:2 * P], hw[:, b, k, 0, :], same[:, k % 2, 1, :],
                              start=True, stop=True).then_inc(S["a_t"], 1)
                    pe.wait_ge(S["a_ts"], t + 1)
                    wait(pe, S["a_vals"], t - 1)
                    for e in range(2):
                        last = t_.matmul(psum[4 + k % 2][0:P, e * D:(e + 1) * D], s_t[:, k % 2, e * P:(e + 1) * P],
                                         w_cen[:, 0, :], start=True, stop=True)
                    last.then_inc(S["a_v"], 1)
                if not isinstance(n, int) or n + 1 < EG:
                    pe.wait_ge(S["key_ready"], n + 2)
                    a_keys(n + 1, 1 - b, (0, 1))

            by_pairs(pe, EG, a_group)

            pe.wait_ge(S["a_scattered"], 32 * ECOL)

            def four(bank, source, q, n):
                for a in range(Q):
                    if n == P:
                        last = t_.transpose(bank[:, a * P:(a + 1) * P],
                                            source[0:P, q * W + a * 128:q * W + (a + 1) * 128], idp)
                    else:
                        last = t_.transpose(bank[0:P, a * 128:(a + 1) * 128],
                                            source[:, q * W + a * P:q * W + (a + 1) * P], ident[:, :])
                return last

            def m_turn(j, jp):
                for k in range(STEPS):
                    u, l = k % 2, k // 2
                    bank = psum[4 * u:4 * u + 4]
                    if l == 0 and exists(j - 1, u):
                        for q in range(Q):
                            pe.wait_ge(S[f"m_h{u}"], nth(LAYERS - 1, j - 1, q))
                            four(bank[q], h_t[u], q, 128).then_inc(S[f"m_back{u}"], 1)
                    if exists(j, u):
                        if l == 0:
                            for q in range(Q):
                                pe.wait_ge(S[f"m_xnrm{u}"], Q * j + q + 1)
                                wait(pe, S[f"m_out{u}"], Q * (j - 1) + q + 1 if past(j, 1) else 0)
                                four(bank[q], x_nrm[u], q, P).then_inc(S[f"m_xt{u}"], 1)
                            pe.wait_ge(S[f"m_y{u}"], 32 * (j + 1))
                        for q in range(Q):
                            if l == 0:
                                pe.wait_ge(S[f"m_hin{u}"], Q * j + q + 1)
                            else:
                                pe.wait_ge(S[f"m_h{u}"], nth(l - 1, j, q))
                            t_.matmul(bank[q][0:P, :], ones3[:, 0:P], b_row[:, l].rearrange("p c d -> p (c d)"),
                                      start=True, stop=False)
                            if l == 0:
                                t_.matmul(bank[q][0:P, :], idp, y_in[u][0:P, q * W:(q + 1) * W], start=False,
                                          stop=False)
                            for a in range(Q):
                                last = t_.matmul(bank[q][0:P, a * 128:(a + 1) * 128],
                                                 h_t[u][:, q * W + a * P:q * W + (a + 1) * P], w_blk[:, l, :],
                                                 start=False, stop=(a == Q - 1))
                            last.then_inc(S[f"m_z{u}"], 1)
                    before = unit(k - 1, j)
                    if before:
                        ub, lb, jb = before
                        for q in range(Q):
                            pe.wait_ge(S[f"m_zn{ub}"], nth(lb, jb, q))
                            four(psum[4 * ub + q], z_nrm[ub], q, P).then_inc(S[f"m_zt{ub}"], 1)

            by_pairs(pe, TURNS, m_turn, ahead=3)

            for i in range(2):
                base = i * EG
                if i == 0:
                    for u in range(2):
                        pe.wait_ge(S[f"m_out{u}"], STREAM[u] * Q)
                else:
                    pe.wait_ge(S["bn_done"], 1)

                def c_keys(n, b, tiles, base=base):
                    for k in tiles:
                        wait(pe, S["c_same"], GT * (n + base) + k - 1)
                        key_row(b, 0, k, psum[k % 2], 0).then_inc(S["c_r"], 1)

                pe.wait_ge(S["c_slots"], 2 * base + 2)
                c_keys(0, 0, (0, 1))

                def c_front(n, b, i=i, base=base, c_keys=c_keys):
                    c = n + base
                    c_keys(n, b, (2, 3))
                    wait(pe, S["c_atc"], c)
                    t_.transpose(psum[3][0:3 * GT, 0:P], e_at[:, b].rearrange("p k a -> p (k a)"), idp)\
                        .then_inc(S["c_att"], 1)
                    pe.wait_ge(S["c_hw"], c + 1)
                    wait(pe, S["c_zt"], c)
                    for k in range(GT):
                        last = t_.transpose(psum[2][:, k * P:(k + 1) * P],
                                            hw[:, b, k].rearrange("p e d -> p (e d)"), idp)
                    last.then_inc(S["c_ht"], 1)
                    pe.wait_ge(S["c_atc"], c + 1)
                    wait(pe, S["c_msg"], c - 1)
                    t_.matmul(psum[4 + b][0:P, :], at_t[:, b, :], w_at[:, i, :], start=True, stop=False)
                    pe.wait_ge(S["c_zt"], c + 1)
                    for k in range(GT):
                        last = t_.matmul(psum[4 + b][0:P, k * 128:(k + 1) * 128], zt[:, k * P:(k + 1) * P],
                                         w_fs[:, i, :], start=False, stop=(k == GT - 1))
                    last.then_inc(S["c_z"], 1)
                    if not isinstance(n, int) or n + 1 < EG:
                        pe.wait_ge(S["c_slots"], 2 * c + 4)
                        c_keys(n + 1, 1 - b, (0, 1))

                def c_back(n, b, base=base):
                    c = n + base
                    pe.wait_ge(S["c_msg"], c + 1)
                    flat = msg[:, b].rearrange("p k d -> p (k d)")
                    for h in range(2):
                        t_.matmul(psum[7][:, 0:1], flat[:, h * 128:(h + 1) * 128], ones[0:P, 0:1],
                                  start=not past(n, 1) and h == 0,
                                  stop=isinstance(n, int) and n == EG - 1 and h == 1)
                    wait(pe, S["c_vals"], c)
                    for k in range(GT):
                        pe.wait_ge(S["c_same"], GT * c + k + 1)
                        t_.matmul(psum[6][0:P, k * D:(k + 1) * D], same[:, k // 2, k % 2, b * P:(b + 1) * P], msg[:, b, k, :],
                                  start=True, stop=True).then_inc(S["c_v"], 1)

                one_behind(pe, EG, c_front, c_back)
                pe.wait_ge(S["c_same"], GT * EG * (i + 1))

                def d_block(m, b, i=i):
                    pe.wait_ge(S[f"d_in{b}"], i * D_PER[b] + (m - b) * 16 + 32)
                    for j in range(BLK // 2):
                        pair_ = blk[b][0:P, j * 128:(j + 1) * 128]
                        last = t_.matmul(psum[0][:, 0:128], pair_, pair_, start=not past(m, 1) and j == 0,
                                         stop=isinstance(m, int) and m == NB - 1 and j == BLK // 2 - 1)
                    last.then_inc(S["d_used"], 1)

                by_pairs(pe, NB, d_block)
                pe.wait_ge(S["bn_ready"], 2 * (i + 1))
                for h in range(2):
                    last = t_.matmul(psum[1][0:P, h * 128:(h + 1) * 128], ones[:, 0:P], bn_x[:, h], start=True,
                                     stop=True)
                last.then_inc(S["bn_sum"], 1)


_MLP = [f"{n}{l}" for l in range(1, 5) for n in ("W", "b", "g", "be")]
_CONV = ["Wf", "bf", "Ws", "bs", "gamma", "beta"]


def kernel(**inputs):
    import numpy as np
    import concourse.bacc as bacc
    from concourse.bass_utils import run_bass_kernel_spmd

    nc = bacc.Bacc("TRN2", target_bir_lowering=False, num_devices=1)
    arrays, aps = {}, {}
    for name, value in inputs.items():
        a = np.ascontiguousarray(value)
        arrays[f"in_{name}"] = a
        aps[name] = nc.dram_tensor(f"in_{name}", a.shape, mybir.dt.from_np(a.dtype), kind="ExternalInput").ap()
    out = nc.dram_tensor("out", (N, D), F32, kind="ExternalOutput").ap()
    tables = [nc.dram_tensor(name, (NT, D), F32).ap() for name in ("y_tab", "x1_tab", "agg1_tab", "agg2_tab")]
    gnn_kernel(nc, aps["x"], aps["src"], aps["dst"], aps["edge_attr_2"], aps["edge_weight"],
               {k: aps[f"L0_gnn_{k}"] for k in _MLP},
               [{k: aps[f"L1_gnn_{k}{i}"] for k in _CONV} for i in (1, 2)],
               out, tables[0], tables[1], tables[2:])
    r = run_bass_kernel_spmd(nc, [arrays], core_ids=[0])
    return r.results[0]["out"]
```

```python
import concourse.bass as bass
from concourse import mybir
from contextlib import ExitStack

F32 = mybir.dt.float32
BF16 = mybir.dt.bfloat16
I32 = mybir.dt.int32
ALU = mybir.AluOpType
ACT = mybir.ActivationFunctionType
AX = mybir.AxisListType

N, E, D = 100000, 25000, 64
P = 125
NCOL, ECOL = N // P, E // P
GC = 8
W = GC * D
GT = 4
EG = ECOL // GT
Q = 4
BW = Q * W
NBATCH = NCOL // (GC * Q)
STREAM = [(NBATCH + 1) // 2, NBATCH // 2]
TURNS = STREAM[0] + 1
SPARE = 2 * P
ZC = 2 * (TURNS - 1)
ZR = 31 * ZC
NT = 128 * ZR
EPS = 1e-5
LAYERS = 4
STEPS = 2 * LAYERS
BLK = 32
HB = BLK * D // 2
NB = NCOL // BLK
KA, KB = 112, P - 112
MAGIC = float(0x5F3759DF)


def wait(eng, sem, value):
    if isinstance(value, int) and value <= 0:
        return
    eng.wait_ge(sem, value)


def past(n, k):
    return not isinstance(n, int) or n >= k


def exists(j, u):
    return not isinstance(j, int) or 0 <= j < STREAM[u]


def unit(k, j):
    k, j = (k, j) if k >= 0 else (k + STEPS, j - 1)
    return (k % 2, k // 2, j) if exists(j, k % 2) else None


def nth(l, j, q):
    return Q * LAYERS * j + Q * l + q + 1


class Steps:

    def __init__(self, eng, sem):
        self.eng, self.sem, self.base, self.start, self.count, self.per, self.groups = eng, sem, 0, 0, 0, 0, 0
        self.last = None

    def begin(self, n):
        if self.groups == 1:
            self.per = self.count
        self.groups += 1
        written_out = isinstance(n, int) and isinstance(self.last, int)
        self.last = n
        if isinstance(n, int) and n == 0:
            self.start = self.base
        elif written_out:
            self.start = self.start + self.count
        else:
            self.start = n * self.per + self.base
        self.count = 0

    def phase(self):
        self.base = self.start + self.count
        self.start, self.count, self.groups = self.base, 0, 0

    def __call__(self, ins):
        self.count += 1
        ins.then_inc(self.sem, 1)
        self.eng.wait_ge(self.sem, self.start + self.count)


def by_pairs(eng, total, body, ahead=1):
    body(0, 0)
    body(1, 1)
    end = 2 * ((total - ahead) // 2)
    with eng.Fori(1, end // 2) as h:
        body(2 * h, 0)
        body(2 * h + 1, 1)
    for g in range(end, total):
        body(g, g % 2)


def one_behind(eng, total, front, back):
    def body(g, parity):
        front(g, parity)
        if past(g, 1):
            back(g - 1, 1 - parity)

    by_pairs(eng, total, body)
    back(total - 1, (total - 1) % 2)


def gnn_kernel(nc, x, src, dst, attr, ew, mlp, conv, out, y_tab, x1_tab, agg_tab):
    ctx = ExitStack()
    with ctx:
        def sb(name, shape, dt=F32):
            return ctx.enter_context(nc.sbuf_tensor(name, shape, dt))

        def sem(name):
            return ctx.enter_context(nc.semaphore(name))

        def nodes(t):
            return t[0:N, :].rearrange("(p c) d -> p (c d)", p=P)

        x_v, out_v, y_v, x1_v = nodes(x), nodes(out), nodes(y_tab), nodes(x1_tab)
        agg_v = [nodes(a) for a in agg_tab]

        ident = sb("ident", [128, 128])
        ones = sb("ones", [128, 128])
        ones3 = sb("ones3", [3, 128], BF16)
        below = sb("below", [P, 2, P])
        spare = sb("spare", [P, 2, GT])
        spare_i = sb("spare_i", [P, 2, GT], I32)
        zeros = sb("zeros", [128, ZR // ZC * D])
        w_raw = sb("w_raw", [128, 5, D])
        w_sum = sb("w_sum", [128, 5])
        w_mean = sb("w_mean", [128, 5])
        w_cen = sb("w_cen", [128, 5, D])
        w_blk = sb("w_blk", [128, LAYERS, 128])
        b_raw = sb("b_raw", [3, LAYERS, D])
        b_sum = sb("b_sum", [3, LAYERS])
        b_mean = sb("b_mean", [3, LAYERS])
        b_cen = sb("b_cen", [3, LAYERS, D])
        b_part = sb("b_part", [3, 3, LAYERS, D], BF16)
        b_rest = sb("b_rest", [3, 2, LAYERS, D])
        b_sel = sb("b_sel", [3, 3, LAYERS, D])
        b_row = sb("b_row", [3, LAYERS, GC, D], BF16)
        gain = sb("gain", [128, LAYERS])
        shift = sb("shift", [128, LAYERS])
        w_fs = sb("w_fs", [128, 2, 128])
        w_at = sb("w_at", [3 * GT, 2, GT * 128])
        bn_gb = sb("bn_gb", [P, 2, 2, D])
        end_i = sb("end_i", [P, 2, ECOL], I32)
        end_f = sb("end_f", [P, 2, ECOL])
        ew_s = sb("ew_s", [P, ECOL])
        at_s = sb("at_s", [P, ECOL, 2])
        to_i = sb("to_i", [P, ECOL], I32)
        g_idx = sb("g_idx", [P, 2, 2, GT], I32)
        s_idx = sb("s_idx", [P, 2, 2, GT], I32)
        e_key = sb("e_key", [P, 2, 2, GT])
        e_at = sb("e_at", [P, 2, GT, 3])
        e_buf = sb("e_buf", [128, 4, 2 * W])
        rows = e_buf[0:P, 0, :].rearrange("p (b k e d) -> p b k e d", b=2, k=GT, e=2)
        xc = e_buf[0:P, 1, :].rearrange("p (b w) -> p b w", b=2)
        sq = e_buf[0:P, 2, :].rearrange("p (b w) -> p b w", b=2)
        hw = e_buf[0:P, 3, :].rearrange("p (b k e d) -> p b k e d", b=2, k=GT, e=2)
        tiny = sb("tiny", [P, 2, 8, GC])
        same = sb("same", [P, 2, 2, 2 * P])
        junk = sb("junk", [P, 2 * P])
        repeat = sb("repeat", [P, 2, 2, GT])
        r_tmp = sb("r_tmp", [P, 2, 2, 2, GT])
        s_t = sb("s_t", [128, 2, 2 * P])
        v_buf = sb("v_buf", [128, 2, 2 * W])
        vals = v_buf[0:P, 0, :].rearrange("p (b k e d) -> p b k e d", b=2, k=GT, e=2)
        act_e = v_buf[0:P, 1, :].rearrange("p (a k d) -> p a k d", a=4, k=GT)
        area = sb("area", [128, EG * W])
        views = {}
        at = [0]

        def carve(name, n, width):
            views[name] = [area[:, at[0] + k * width:at[0] + (k + 1) * width] for k in range(n)]
            at[0] += n * width

        for name in ("x_even", "y_in", "z_sq", "z_nrm", "h_t", "x_out"):
            carve(name, 2, BW)
        at_m = at[0]
        at[0] = 0
        for name in ("l_x1", "l_keep", "l_a1", "l_a2", "l_xc", "l_sq"):
            carve(name, 1 if name == "l_sq" else 2, BLK * D)
        assert max(at[0], at_m) <= EG * W
        x_even, y_in, z_sq, z_nrm, h_t, x_out = (
            views[k] for k in ("x_even", "y_in", "z_sq", "z_nrm", "h_t", "x_out"))
        l_x1, l_keep, l_a1, l_a2, l_xc, l_sq = (
            views[k] for k in ("l_x1", "l_keep", "l_a1", "l_a2", "l_xc", "l_sq"))
        h_keep = area
        blk_s = sb("blk", [128, 2, BLK * D])
        blk = [blk_s[:, k, :] for k in range(2)]
        x_in = [[x_even[u][0:P], e_buf[0:P, 2 * u:2 * u + 2, :].rearrange("p a w -> p (a w)")]
                for u in range(2)]
        x_sq = v_buf[0:P, :, :].rearrange("p a w -> p (a w)")
        x_nrm = [blk[u][0:P] for u in range(2)]
        m_stat = sb("m_stat", [P, 2, 5, 2 * Q * GC])
        OF_LAYER, OF_X = slice(0, Q * GC), slice(Q * GC, 2 * Q * GC)
        zt = sb("zt", [128, W])
        at_t = sb("at_t", [3 * GT, 2, P])
        dve_e = sb("dve_e", [P, 3, GT, D])
        bn_w = sb("bn_w", [P, 10, D])
        f_stat = sb("f_stat", [P, 6, BLK])
        t_part, t_rest, t_sel, t_row = b_part[:, :, 0:2], b_rest[:, :, 0:2], b_sel[:, :, 0:2], b_row[:, 0:2]
        msg = sb("msg", [P, 2, GT, D])
        bn_x = sb("bn_x", [128, 2, 128])
        bn_s = sb("bn_s", [P, 2, 2, D])
        psum = [ctx.enter_context(nc.psum_tensor(f"bank{k}", [128, 512], F32)) for k in range(8)]

        names = """act_step pool_passed w_zero edges_ready w_ready consts iota_done loads_edges loads_w zero_tile
            y_clear agg_clear dve_step
            idx_ready key_ready a_rows0 a_rows1 a_xc a_sq a_hw a_r a_same a_t a_ts a_v a_vals a_sidx a_scattered
            m_x00 m_x01 m_x10 m_x11 m_y0 m_y1 m_mean0 m_mean1 m_xcen0 m_xcen1 m_xsq0 m_xsq1 m_xss0 m_xss1
            m_xrstd0 m_xrstd1 m_xnrm0 m_xnrm1 m_xt0 m_xt1 m_hin0 m_hin1 m_z0 m_z1 m_zsq0 m_zsq1 m_zss0 m_zss1
            m_rstd0 m_rstd1 m_zn0 m_zn1 m_zt0 m_zt1 m_h0 m_h1 m_zy0 m_zy1 m_back0 m_back1 m_out0 m_out1 m_stored0
            m_stored1 pool_step
            c_idx c_slots c_rows0 c_rows1 c_xc c_sq c_hw c_keep c_r c_same c_ht c_zt c_att c_atc c_z c_act c_msg
            c_v c_vals c_sidx c_scattered dve_back d_in00 d_in01 d_in10 d_in11 loads_conv d_used
            bn_ready bn_sum bn_done
            f_x0 f_x1 f_agg0 f_agg1 f_mean f_xc f_sq f_ss f_keep f_p f_h f_sum f_h2 f_added f_out f_rows f_stored0
            f_stored1""".split()
        S = {name: sem(name) for name in names}
        block = ctx.enter_context(nc.Block())

        def halves(eng, dst_ap, src_ap, done):
            eng.dma_start(dst_ap[0:KA], src_ap[0:KA]).then_inc(done, 16)
            eng.dma_start(dst_ap[KA:P], src_ap[KA:P]).then_inc(done, 16)

        def b8(ap):
            return ap.unsqueeze(2).to_broadcast([ap.shape[0], ap.shape[1], D])

        def cols(ap):
            return ap.rearrange("p (c d) -> p c d", d=D)

        N_ZERO = 16 * ZC
        SETUP_POOL = 5
        N_LOADS_W = 1 + LAYERS * 7
        N_LOADS_CONV = 2 * (2 * (1 + 2 * GT) + 2)
        D_PER = (32 * (NB - NB // 2), 32 * (NB // 2))

        @block.sync
        def _(sp):
            for e, v in ((0, dst), (1, src)):
                halves(sp, end_i[0:P, e, :], v.rearrange("(p t) -> p t", p=P), S["loads_edges"])
            halves(sp, ew_s[0:P, :], ew.rearrange("(p t) -> p t", p=P), S["loads_edges"])
            halves(sp, at_s[0:P, :, :], attr.rearrange("(p t) k -> p t k", p=P), S["loads_edges"])

            def clear(tab, k, done):
                v = tab.rearrange("(p c) d -> p (c d)", p=128)
                w = ZR // ZC * D
                sp.dma_start(v[:, bass.ds(k * w, w)], zeros[:, :]).then_inc(done, 16)

            sp.wait_ge(S["zero_tile"], 1)
            for k in range(ZC):
                clear(y_tab, k, S["y_clear"])

            def load_conv(dst_ap, src_ap):
                sp.dma_start(dst_ap, src_ap).then_inc(S["loads_conv"], 16)

            sp.wait_ge(S["w_zero"], 2)
            for i in range(2):
                c = conv[i]
                for h, (wn, bn) in enumerate((("Wf", "bf"), ("Ws", "bs"))):
                    load_conv(w_fs[:, i, h * D:(h + 1) * D], c[wn][0:128, :])
                    for k in range(GT):
                        to = slice(k * 128 + h * D, k * 128 + (h + 1) * D)
                        load_conv(w_at[3 * k:3 * k + 2, i, to], c[wn][128:130, :])
                        load_conv(w_at[3 * k + 2:3 * k + 3, i, to], c[bn].unsqueeze(0))
                for k, name in enumerate(("gamma", "beta")):
                    load_conv(bn_gb[:, i, k, :], c[name].unsqueeze(0).to_broadcast([P, D]))

            def batch_cols(j, u):
                return bass.ds((2 * j + u) * BW, BW)

            def load_batch(j, u, jp):
                if past(j, 2):
                    sp.wait_ge(S[f"m_out{u}"], Q * (j - 1))
                halves(sp, x_in[u][jp], x_v[:, batch_cols(j, u)], S[f"m_x{u}{jp}"])
                if past(j, 1):
                    sp.wait_ge(S[f"m_zn{u}"], nth(0, j - 1, Q - 1))
                else:
                    sp.wait_ge(S["a_scattered"], 32 * ECOL)
                halves(sp, y_in[u], y_v[:, batch_cols(j, u)], S[f"m_y{u}"])

            for u in range(2):
                load_batch(0, u, 0)

            def mlp_turn(j, jp):
                for u in range(2):
                    if exists(j - 1, u):
                        sp.wait_ge(S[f"m_out{u}"], Q * j)
                        halves(sp, x1_v[:, batch_cols(j - 1, u)], x_out[u], S[f"m_stored{u}"])
                    if exists(j + 1, u):
                        load_batch(j + 1, u, 1 - jp)
                if not isinstance(j, int) or j < TURNS - 1:
                    for tab in agg_tab:
                        for k in range(2):
                            clear(tab, 2 * j + k, S["agg_clear"])

            by_pairs(sp, TURNS, mlp_turn, ahead=3)

            for i in range(2):
                sp.wait_ge(S["c_scattered"], 16 * ECOL * (i + 1))

                def agg_block(m, b, i=i):
                    n = i * NB + m
                    for h in range(2):
                        if i or past(m, 2):
                            sp.wait_ge(S["d_used"], 2 * (n - 2) + h + 1)
                        halves(sp, blk[b][:, h * HB:(h + 1) * HB], agg_v[i][:, bass.ds(m * BLK * D + h * HB, HB)],
                               S[f"d_in{b}{h}"])

                by_pairs(sp, NB, agg_block)

            def block_cols(m):
                return bass.ds(m * BLK * D, BLK * D)

            def load_x(m, b):
                if past(m, 2):
                    sp.wait_ge(S["f_xc"], m - 1)
                    sp.wait_ge(S["f_keep"], m - 1)
                halves(sp, l_x1[b], x1_v[:, block_cols(m)], S[f"f_x{b}"])

            def load_agg(m, b):
                if past(m, 2):
                    sp.wait_ge(S["f_sum"], Q * (m - 1))
                halves(sp, l_a1[b], agg_v[0][:, block_cols(m)], S[f"f_agg{b}"])
                halves(sp, l_a2[b], agg_v[1][:, block_cols(m)], S[f"f_agg{b}"])

            def store_block(m, b):
                sp.wait_ge(S["f_out"], m + 1)
                halves(sp, out_v[:, block_cols(m)], blk[b], S[f"f_stored{b}"])

            sp.wait_ge(S["bn_done"], 2)
            load_x(0, 0)
            load_agg(0, 0)
            load_x(1, 1)

            def last_block(m, b):
                if not isinstance(m, int) or m + 2 < NB:
                    load_x(m + 2, b)
                if not isinstance(m, int) or m + 1 < NB:
                    load_agg(m + 1, 1 - b)
                if past(m, 1):
                    store_block(m - 1, 1 - b)

            by_pairs(sp, NB, last_block, ahead=2)
            store_block(NB - 1, (NB - 1) % 2)
            for u in range(2):
                sp.wait_ge(S[f"m_stored{u}"], 32 * STREAM[u])
            sp.wait_ge(S["f_stored0"], 32 * (NB - NB // 2))
            sp.wait_ge(S["f_stored1"], 32 * (NB // 2))

        @block.gpsimd
        def _(pool):
            g = nc.gpsimd
            g.memset(ident[:, :], 0.0).then_inc(S["consts"], 1)
            g.memset(ones[:, :], 1.0).then_inc(S["consts"], 1)
            g.memset(below[:, :, :], 1.0).then_inc(S["consts"], 1)
            g.memset(ones3[:, :], 1.0).then_inc(S["consts"], 1)
            g.memset(e_at[:, :, :, :], 1.0).then_inc(S["consts"], 1)
            pool.wait_ge(S["consts"], SETUP_POOL)
            g.affine_select(out=ident[:, :], in_=ident[:, :], compare_op=ALU.not_equal, fill=1.0, base=0,
                            pattern=[[-1, 128]], channel_multiplier=1).then_inc(S["iota_done"], 1)
            g.affine_select(out=below[:, 1, :], in_=below[:, 1, :], compare_op=ALU.is_gt, fill=0.0, base=0,
                            pattern=[[-1, P]], channel_multiplier=1).then_inc(S["iota_done"], 1)
            g.iota(spare_i[:, :, :], pattern=[[P, 2], [0, GT]], base=N, channel_multiplier=1)\
                .then_inc(S["iota_done"], 1)

            def waits(*pairs):
                for sem_, x in pairs:
                    wait(pool, sem_, x)
                pool.sem_inc(S["pool_passed"], 1)

            def gather(tab, b, e, k, done):
                g.indirect_dma_start(
                    out=rows[:, b, k, e, :], out_offset=None, in_=tab[0:N, :],
                    in_offset=bass.IndirectOffsetOnAxis(ap=g_idx[:, b, e, k:k + 1], axis=0),
                    compute_op=ALU.bypass).then_inc(done, 16)

            def scatter(tab, b, e, k, done):
                g.indirect_dma_start(
                    out=tab[:, :], out_offset=bass.IndirectOffsetOnAxis(ap=s_idx[:, b, e, k:k + 1], axis=0),
                    in_=vals[:, b, k, e, :], in_offset=None, compute_op=ALU.add).then_inc(done, 16)

            def a_gathers(n, b, k):
                for e in range(2):
                    gather(x, b, e, k, S[f"a_rows{b}"])

            for n in range(2):
                pool.wait_ge(S["idx_ready"], n + 1)
                for k in range(GT):
                    a_gathers(n, n, k)
            pool.wait_ge(S["y_clear"], N_ZERO)

            def a_scatters(n, b, k):
                waits((S["a_sidx"], n + 1), (S["a_vals"], GT * n + k + 1),
                      (S["a_scattered"], 32 * (GT * n + k)))
                for e in range(2):
                    scatter(y_tab, b, e, k, S["a_scattered"])

            def a_group(n, b):
                more = not isinstance(n, int) or n + 2 < EG
                if more:
                    waits((S["idx_ready"], n + 3), (S["a_xc"], n + 1))
                for k in range(GT):
                    if more:
                        a_gathers(n + 2, b, k)
                    if past(n, 1):
                        a_scatters(n - 1, 1 - b, k)

            by_pairs(pool, EG, a_group)
            for k in range(GT):
                a_scatters(EG - 1, (EG - 1) % 2, k)

            step = Steps(pool, S["pool_step"])

            def inv_std(st, done):
                total, var, t, y = (st[:, k, :] for k in range(4))

                def scaled(o, i_, m, c):
                    return g.tensor_scalar(out=o, in0=i_, scalar1=m, scalar2=c, op0=ALU.mult, op1=ALU.add)

                def times(o, x_, y_):
                    return g.tensor_tensor(out=o, in0=x_, in1=y_, op=ALU.mult)

                def held(ins):
                    step(ins)
                    pool.sem_inc(S["pool_passed"], 1)

                held(scaled(var, total, 1.0 / D, EPS))
                step(scaled(y.bitcast(I32), var.bitcast(I32), -0.5, MAGIC))
                step(times(t, y, y))
                held(times(t, t, var))
                step(scaled(total, t, 0.375, -1.25))
                held(times(total, total, t))
                step(g.tensor_scalar(out=total, in0=total, scalar1=1.875, scalar2=1.0, op0=ALU.add, op1=ALU.mult))
                step(times(y, y, total))
                step(times(t, y, y))
                held(times(t, t, var))
                step(scaled(t, t, -0.5, 1.5))
                times(y, y, t).then_inc(done, 1)

            def center(u, j, par):
                pool.wait_ge(S[f"m_mean{u}"], j + 1)
                wait(pool, S[f"m_xt{u}"], Q * j)
                for q in range(Q):
                    c = slice(q * W, (q + 1) * W)
                    g.tensor_tensor(out=cols(x_nrm[u][:, c]), in0=cols(x_in[u][par][:, c]),
                                    in1=b8(m_stat[:, u, 0, q * GC:(q + 1) * GC]), op=ALU.subtract)\
                        .then_inc(S[f"m_xcen{u}"], 1)

            def x_scale(u):
                for q in range(Q):
                    c = slice(q * W, (q + 1) * W)
                    g.tensor_tensor(out=cols(x_nrm[u][:, c]), in0=cols(x_nrm[u][:, c]),
                                    in1=b8(m_stat[:, u, 4, (Q + q) * GC:(Q + q + 1) * GC]), op=ALU.mult)\
                        .then_inc(S[f"m_xnrm{u}"], 1)

            step.begin(0)
            for u in range(2):
                center(u, 0, 0)
            for u in range(2):
                pool.wait_ge(S[f"m_xss{u}"], 1)
                inv_std(m_stat[:, u, 1:5, OF_X], S[f"m_xrstd{u}"])
                pool.wait_ge(S[f"m_xrstd{u}"], 1)
                x_scale(u)
            step.phase()

            def m_turn(j, jp):
                step.begin(j)
                for k in range(STEPS):
                    if unit(k, j):
                        u, l, _ = unit(k, j)
                        more = exists(j + 1, u)
                        if l == LAYERS - 1 and more:
                            waits((S[f"m_zss{u}"], nth(l, j, Q - 1)), (S[f"m_xss{u}"], j + 2))
                            inv_std(m_stat[:, u, 1:5, :], S[f"m_rstd{u}"])
                            pool.wait_ge(S[f"m_rstd{u}"], LAYERS * (j + 1))
                            x_scale(u)
                        else:
                            waits((S[f"m_zss{u}"], nth(l, j, Q - 1)),)
                            inv_std(m_stat[:, u, 1:5, OF_LAYER], S[f"m_rstd{u}"])
                        if l == 1 and more:
                            center(u, j + 1, 1 - jp)

            by_pairs(pool, TURNS, m_turn, ahead=3)
            step.phase()

            for u in range(2):
                pool.wait_ge(S[f"m_stored{u}"], 32 * STREAM[u])
            for i in range(2):
                tab = x1_tab if i == 0 else agg_tab[0]

                def c_gathers(n, b, k, tab=tab):
                    for e in range(2):
                        gather(tab, b, e, k, S[f"c_rows{b}"])

                base = i * EG
                if i:
                    pool.wait_ge(S["c_xc"], base)
                    pool.wait_ge(S["c_scattered"], 16 * ECOL)
                for n in range(2):
                    pool.wait_ge(S["c_idx"], base + n + 1)
                    for k in range(GT):
                        c_gathers(n, n, k)
                pool.wait_ge(S["agg_clear"], N_ZERO * 2)

                def c_group(n, b, i=i, base=base, c_gathers=c_gathers):
                    more = not isinstance(n, int) or n + 2 < EG
                    if more:
                        waits((S["c_idx"], base + n + 3), (S["c_xc"], base + n + 1))
                    for k in range(GT):
                        if more:
                            c_gathers(n + 2, b, k)
                        if past(n, 2):
                            c_scatter(n - 2, b, k)

                def c_scatter(n, b, k, i=i, base=base):
                    if k == 0:
                        waits((S["c_sidx"], base + n + 1), (S["c_vals"], base + n + 1))
                    waits((S["c_scattered"], 16 * (GT * (base + n) + k)),)
                    scatter(agg_tab[i], b, 0, k, S["c_scattered"])

                by_pairs(pool, EG, c_group)
                for n in (EG - 2, EG - 1):
                    for k in range(GT):
                        c_scatter(n, n % 2, k)

            def f_center(m, b):
                pool.wait_ge(S["f_mean"], m + 1)
                if past(m, 2):
                    pool.wait_ge(S["f_sum"], Q * (m - 1))
                g.tensor_tensor(out=cols(l_xc[b][0:P]), in0=cols(l_x1[b][0:P]), in1=b8(f_stat[:, b, :]),
                                op=ALU.subtract).then_inc(S["f_xc"], 1)

            def f_scale(m, b):
                for i, part in enumerate((l_a1, l_a2)):
                    pool.wait_ge(S[f"f_agg{b}"], (m - b) * 32 + 64)
                    g.tensor_tensor(out=cols(part[b][0:P]), in0=cols(part[b][0:P]),
                                    in1=bn_s[:, i, 0, :].unsqueeze(1).to_broadcast([P, BLK, D]),
                                    op=ALU.mult).then_inc(S["f_p"], 1)

            f_center(0, 0)
            f_scale(0, 0)

            def f_block(m, b):
                if not isinstance(m, int) or m + 1 < NB:
                    f_center(m + 1, 1 - b)
                    f_scale(m + 1, 1 - b)

            by_pairs(pool, NB, f_block)

        def newton(step, var, y, t):
            v = nc.vector
            step(v.tensor_scalar(out=y.bitcast(I32), in0=var.bitcast(I32), scalar1=-0.5, scalar2=MAGIC,
                                 op0=ALU.mult, op1=ALU.add))
            for _ in range(3):
                step(v.scalar_tensor_tensor(out=t, in0=y, scalar=-0.5, in1=y, op0=ALU.mult, op1=ALU.mult))
                step(v.tensor_tensor(out=t, in0=t, in1=var, op=ALU.mult))
                step(v.scalar_tensor_tensor(out=y, in0=t, scalar=1.5, in1=y, op0=ALU.add, op1=ALU.mult))

        def pair(rows_b):
            return rows_b.rearrange("p k e d -> p (k e) d")

        @block.vector
        def _(dve):
            v = nc.vector
            step, back = Steps(dve, S["dve_step"]), Steps(dve, S["dve_back"])
            step.begin(0)

            v.memset(zeros[:, :], 0.0).then_inc(S["zero_tile"], 1)
            v.memset(w_blk[:, :, :], 0.0).then_inc(S["w_zero"], 1)
            v.memset(w_at[:, :, :], 0.0).then_inc(S["w_zero"], 1)
            dve.wait_ge(S["iota_done"], 3)
            v.tensor_copy(spare[:, :, :], spare_i[:, :, :]).then_inc(S["w_zero"], 1)
            dve.wait_ge(S["loads_edges"], 128)
            v.tensor_copy(end_f[:, :, :], end_i[:, :, :]).then_inc(S["edges_ready"], 1)
            dve.wait_ge(S["loads_w"], 16 * N_LOADS_W)
            step(v.tensor_reduce(out=w_sum[:, :], in_=w_raw[:, :, :], axis=AX.X, op=ALU.add))
            step(v.tensor_scalar(out=w_mean[:, :], in0=w_sum[:, :], scalar1=1.0 / D, scalar2=None, op0=ALU.mult))
            step(v.tensor_tensor(out=w_cen[:, :, :], in0=w_raw[:, :, :], in1=b8(w_mean[:, :]), op=ALU.subtract))
            dve.wait_ge(S["w_zero"], 3)
            step(v.tensor_copy(w_blk[0:D, :, 0:D], w_cen[0:D, 1:5, :]))
            step(v.tensor_copy(w_blk[D:128, :, D:128], w_cen[D:128, 1:5, :]))
            step(v.tensor_reduce(out=b_sum[:, :], in_=b_raw[:, :, :], axis=AX.X, op=ALU.add))
            step(v.tensor_scalar(out=b_mean[:, :], in0=b_sum[:, :], scalar1=1.0 / D, scalar2=None, op0=ALU.mult))
            step(v.tensor_tensor(out=b_cen[:, :, :], in0=b_raw[:, :, :], in1=b8(b_mean[:, :]), op=ALU.subtract))
            step(v.tensor_copy(b_part[:, 0], b_cen[:, :, :]))
            step(v.tensor_tensor(out=b_rest[:, 0], in0=b_cen[:, :, :], in1=b_part[:, 0], op=ALU.subtract))
            step(v.tensor_copy(b_part[:, 1], b_rest[:, 0]))
            step(v.tensor_tensor(out=b_rest[:, 1], in0=b_rest[:, 0], in1=b_part[:, 1], op=ALU.subtract))
            step(v.tensor_copy(b_part[:, 2], b_rest[:, 1]))
            step(v.tensor_scalar(out=b_sel[:, 0], in0=b_part[:, 0], scalar1=ident[0:3, 0:1], scalar2=None,
                                 op0=ALU.mult))
            for k in (1, 2):
                step(v.scalar_tensor_tensor(out=b_sel[:, k], in0=b_part[:, k], scalar=ident[0:3, k:k + 1],
                                            in1=b_sel[:, k - 1], op0=ALU.mult, op1=ALU.add))
            for l in range(LAYERS):
                step(v.tensor_copy(b_row[:, l], b_sel[:, 2, l].unsqueeze(1).to_broadcast([3, GC, D])))
            v.tensor_copy(b_sum[0:1, 0:1], b_mean[0:1, 0:1]).then_inc(S["w_ready"], 1)
            step.phase()

            def a_group(n, b):
                step.begin(n)
                st = tiny[:, b]
                dve.wait_ge(S[f"a_rows{b}"], (n - b) * 64 + 128)
                step(v.tensor_reduce(out=st[:, 0, :], in_=pair(rows[:, b]), axis=AX.X, op=ALU.add))
                step(v.tensor_scalar(out=st[:, 1, :], in0=st[:, 0, :], scalar1=1.0 / D, scalar2=None,
                                     op0=ALU.mult))
                v.tensor_tensor(out=cols(xc[:, b]), in0=pair(rows[:, b]), in1=b8(st[:, 1, :]),
                                op=ALU.subtract).then_inc(S["a_xc"], 1)
                for k in range(GT):
                    t = GT * n + k
                    dve.wait_ge(S["a_r"], t + 1)
                    wait(dve, S["a_t"], t - 1)
                    for e in range(2):
                        v.tensor_scalar(out=same[:, k % 2, e, :], in0=psum[k % 2][0:P, 0:2 * P],
                                        scalar1=e_key[:, b, e, k:k + 1], scalar2=None, op0=ALU.is_equal)\
                            .then_inc(S["a_same"], 1)
                    dve.wait_ge(S["a_same"], 2 * t + 2)
                    step(v.tensor_tensor_reduce(out=junk[:, 0:P], in0=same[:, k % 2, 0, 0:P],
                                                in1=below[:, 1, :], scale=1.0, scalar=0.0, op0=ALU.mult,
                                                op1=ALU.add, accum_out=repeat[:, b, 0, k:k + 1]))
                    step(v.tensor_tensor_reduce(out=junk[:, :], in0=same[:, k % 2, 1, :],
                                                in1=below[:, :, :].rearrange("p a i -> p (a i)"), scale=1.0,
                                                scalar=0.0, op0=ALU.mult, op1=ALU.add,
                                                accum_out=repeat[:, b, 1, k:k + 1]))
                    if k == 0:
                        dve.wait_ge(S["a_sq"], n + 1)
                        step(v.tensor_reduce(out=st[:, 2, :], in_=cols(sq[:, b]), axis=AX.X, op=ALU.add))
                        step(v.tensor_scalar(out=st[:, 3, :], in0=st[:, 2, :], scalar1=1.0 / D, scalar2=EPS,
                                             op0=ALU.mult, op1=ALU.add))
                        newton(step, st[:, 3, :], st[:, 4, :], st[:, 5, :])
                        step(v.tensor_tensor(out=st[:, 6, :].rearrange("p (k e) -> p k e", e=2),
                                             in0=st[:, 4, :].rearrange("p (k e) -> p k e", e=2),
                                             in1=ew_s[:, bass.ds(GT * n, GT)].unsqueeze(2)
                                             .to_broadcast([P, GT, 2]), op=ALU.mult))
                        wait(dve, S["a_t"], GT * (n - 1))
                        v.scalar_tensor_tensor(out=pair(hw[:, b]), in0=cols(xc[:, b]), scalar=0.0,
                                               in1=b8(st[:, 6, :]), op0=ALU.max, op1=ALU.mult)\
                            .then_inc(S["a_hw"], 1)
                tmp = r_tmp[:, b]
                step(v.tensor_tensor(out=tmp[:, 0], in0=spare[:, :, :], in1=e_key[:, b], op=ALU.subtract))
                step(v.scalar_tensor_tensor(out=tmp[:, 1], in0=repeat[:, b], scalar=1.0, in1=tmp[:, 0],
                                            op0=ALU.min, op1=ALU.mult))
                wait(dve, S["a_scattered"], 32 * GT * (n - 1))
                v.tensor_tensor(out=s_idx[:, b], in0=tmp[:, 1], in1=e_key[:, b], op=ALU.add)\
                    .then_inc(S["a_sidx"], 1)
                dve.wait_ge(S["a_sidx"], n + 1)
                step(v.tensor_copy(to_i[:, bass.ds(GT * n, GT)], s_idx[:, b, 0]))

            by_pairs(dve, EG, a_group)
            step.phase()


            def x_mean(u, j, par):
                dve.wait_ge(S[f"m_x{u}{par}"], (j - par) * 16 + 32)
                step(v.tensor_reduce(out=m_stat[:, u, 0, OF_LAYER], in_=cols(x_in[u][par]), axis=AX.X, op=ALU.add))
                v.tensor_scalar(out=m_stat[:, u, 0, OF_LAYER], in0=m_stat[:, u, 0, OF_LAYER], scalar1=1.0 / D, scalar2=None,
                                op0=ALU.mult).then_inc(S[f"m_mean{u}"], 1)

            def x_squares(u, j):
                dve.wait_ge(S[f"m_xsq{u}"], Q * (j + 1))
                v.tensor_reduce(out=m_stat[:, u, 1, OF_X], in_=cols(x_sq), axis=AX.X, op=ALU.add)\
                    .then_inc(S[f"m_xss{u}"], 1)

            step.begin(0)
            for u in range(2):
                x_mean(u, 0, 0)
            for u in range(2):
                x_squares(u, 0)
            step.phase()

            def reduce_sq(u, l, j, q):
                dve.wait_ge(S[f"m_zsq{u}"], nth(l, j, q))
                v.tensor_reduce(out=m_stat[:, u, 1, q * GC:(q + 1) * GC], in_=cols(z_sq[u][0:P, q * W:(q + 1) * W]),
                                axis=AX.X, op=ALU.add).then_inc(S[f"m_zss{u}"], 1)

            def add_messages(u, j, q):
                c = slice(q * W, (q + 1) * W)
                dve.wait_ge(S[f"m_z{u}"], nth(0, j, q))
                dve.wait_ge(S[f"m_y{u}"], 32 * (j + 1))
                v.tensor_tensor(out=y_in[u][0:P, c], in0=psum[4 * u + q][0:P, :], in1=y_in[u][0:P, c],
                                op=ALU.add).then_inc(S[f"m_zy{u}"], 1)

            def scale(u, l, j, q):
                dve.wait_ge(S[f"m_rstd{u}"], LAYERS * j + l + 1)
                wait(dve, S[f"m_zt{u}"], nth(l, j, q) - Q)
                z = y_in[u][0:P, q * W:(q + 1) * W] if l == 0 else psum[4 * u + q][0:P, :]
                v.tensor_tensor(out=cols(z_nrm[u][0:P, q * W:(q + 1) * W]), in0=cols(z),
                                in1=b8(m_stat[:, u, 4, q * GC:(q + 1) * GC]), op=ALU.mult)\
                    .then_inc(S[f"m_zn{u}"], 1)

            def m_turn(j, jp):
                step.begin(j)
                for k in range(STEPS):
                    u, l = k % 2, k // 2
                    if l == 0 and exists(j - 1, u):
                        for q in range(Q):
                            c = slice(q * W, (q + 1) * W)
                            dve.wait_ge(S[f"m_back{u}"], Q * (j - 1) + q + 1)
                            if past(j, 2):
                                dve.wait_ge(S[f"m_stored{u}"], 32 * (j - 1))
                            v.tensor_tensor(out=x_out[u][0:P, c], in0=psum[4 * u + q][0:P, :],
                                            in1=x_in[u][1 - jp][:, c], op=ALU.add).then_inc(S[f"m_out{u}"], 1)
                    this, before = unit(k, j), unit(k - 1, j)
                    for q in range(Q):
                        if this and l == 0:
                            add_messages(u, j, q)
                        elif this:
                            reduce_sq(*this, q)
                        if this and l == 0 and q:
                            reduce_sq(*this, q - 1)
                        if before:
                            scale(*before, q)
                    if this and l == 0:
                        reduce_sq(*this, Q - 1)
                    if k in (1, 2) and exists(j + 1, k - 1):
                        x_mean(k - 1, j + 1, 1 - jp)
                    if k in (4, 5) and exists(j + 1, k - 4):
                        x_squares(k - 4, j + 1)

            by_pairs(dve, TURNS, m_turn, ahead=3)
            step.phase()

            for i in range(2):
                base = i * EG
                if i:
                    dve.wait_ge(S["bn_done"], 1)

                def c_front(n, b, i=i, base=base):
                    step.begin(n)
                    c = n + base
                    st = tiny[:, b]
                    dve.wait_ge(S[f"c_rows{b}"], i * EG * 64 + (n - b) * 64 + 128)
                    if i == 0:
                        step(v.tensor_reduce(out=st[:, 0, :], in_=pair(rows[:, b]), axis=AX.X, op=ALU.add))
                        step(v.tensor_scalar(out=st[:, 1, :], in0=st[:, 0, :], scalar1=1.0 / D, scalar2=None,
                                             op0=ALU.mult))
                        v.tensor_tensor(out=cols(xc[:, b]), in0=pair(rows[:, b]), in1=b8(st[:, 1, :]),
                                        op=ALU.subtract).then_inc(S["c_xc"], 1)
                    else:
                        v.tensor_tensor(out=cols(xc[:, b]), in0=pair(rows[:, b]),
                                        in1=bn_s[:, 0, 0, :].unsqueeze(1).to_broadcast([P, GC, D]),
                                        op=ALU.mult).then_inc(S["c_xc"], 1)
                    for k in range(GT):
                        t = GT * c + k
                        dve.wait_ge(S["c_r"], t + 1)
                        wait(dve, S["c_v"], t + 1 - 2 * GT)
                        v.tensor_scalar(out=same[:, k // 2, k % 2, b * P:(b + 1) * P], in0=psum[k % 2][0:P, 0:P],
                                        scalar1=e_key[:, b, 0, k:k + 1], scalar2=None, op0=ALU.is_equal)\
                            .then_inc(S["c_same"], 1)
                    if i == 0:
                        dve.wait_ge(S["c_sq"], c + 1)
                        step(v.tensor_reduce(out=st[:, 2, :], in_=cols(sq[:, b]), axis=AX.X, op=ALU.add))
                        step(v.tensor_scalar(out=st[:, 3, :], in0=st[:, 2, :], scalar1=1.0 / D, scalar2=EPS,
                                             op0=ALU.mult, op1=ALU.add))
                        newton(step, st[:, 3, :], st[:, 4, :], st[:, 5, :])
                        wait(dve, S["c_ht"], c - 1)
                        wait(dve, S["c_keep"], c - 1)
                        v.scalar_tensor_tensor(out=pair(hw[:, b]), in0=cols(xc[:, b]), scalar=0.0,
                                               in1=b8(st[:, 4, :]), op0=ALU.max, op1=ALU.mult)\
                            .then_inc(S["c_hw"], 1)
                    else:
                        dve.wait_ge(S["c_xc"], c + 1)
                        step(v.tensor_tensor(out=sq[:, b], in0=xc[:, b],
                                             in1=h_keep[0:P, bass.ds(n * W, W)], op=ALU.add))
                        wait(dve, S["c_ht"], c - 1)
                        v.tensor_tensor(out=pair(hw[:, b]), in0=cols(sq[:, b]),
                                        in1=bn_s[:, 0, 1, :].unsqueeze(1).to_broadcast([P, GC, D]),
                                        op=ALU.add).then_inc(S["c_hw"], 1)

                def c_back(n, b, base=base):
                    back.begin(n)
                    c = n + base
                    dve.wait_ge(S["c_act"], c + 1)
                    z = psum[4 + b][0:P, :].rearrange("p (k w) -> p k w", w=128)
                    back(v.tensor_scalar(out=dve_e[:, 0], in0=act_e[:, 0], scalar1=1.0, scalar2=None,
                                         op0=ALU.add))
                    back(v.reciprocal(out=dve_e[:, 1], in_=dve_e[:, 0]))
                    back(v.scalar_tensor_tensor(out=dve_e[:, 2], in0=z[:, :, D:], scalar=0.0, in1=act_e[:, 3],
                                                op0=ALU.max, op1=ALU.add))
                    wait(dve, S["c_v"], GT * (c - 1))
                    v.tensor_tensor(out=msg[:, b], in0=dve_e[:, 2], in1=dve_e[:, 1], op=ALU.mult)\
                        .then_inc(S["c_msg"], 1)

                one_behind(dve, EG, c_front, c_back)
                step.phase()
                back.phase()

                dve.wait_ge(S["loads_conv"], 16 * N_LOADS_CONV)
                step.begin(0)
                dve.wait_ge(S["d_used"], 2 * NB * (i + 1))
                v.tensor_tensor(out=bn_x[:, 0], in0=psum[0][:, 0:128], in1=ident[:, :], op=ALU.mult)\
                    .then_inc(S["bn_ready"], 1)
                v.tensor_scalar(out=bn_x[:, 1], in0=ident[:, :], scalar1=psum[7][:, 0:1], scalar2=None,
                                op0=ALU.mult).then_inc(S["bn_ready"], 1)
                dve.wait_ge(S["bn_sum"], i + 1)
                step(v.tensor_copy(bn_w[:, 0:4, :], psum[1][0:P, 0:256].rearrange("p (a d) -> p a d", d=D)))
                sums = bn_w[:, 0:4, :].rearrange("p (a h) d -> p a h d", h=2)
                step(v.tensor_tensor(out=bn_w[:, 4:6, :], in0=sums[:, :, 0, :], in1=sums[:, :, 1, :], op=ALU.add))
                step(v.tensor_scalar(out=bn_w[:, 4:6, :], in0=bn_w[:, 4:6, :], scalar1=1.0 / N, scalar2=None,
                                     op0=ALU.mult))
                step(v.tensor_tensor(out=bn_w[:, 6, :], in0=bn_w[:, 5, :], in1=bn_w[:, 5, :], op=ALU.mult))
                step(v.tensor_tensor(out=bn_w[:, 7, :], in0=bn_w[:, 4, :], in1=bn_w[:, 6, :], op=ALU.subtract))
                step(v.tensor_scalar(out=bn_w[:, 7, :], in0=bn_w[:, 7, :], scalar1=0.0, scalar2=EPS,
                                     op0=ALU.max, op1=ALU.add))
                newton(step, bn_w[:, 7, :], bn_w[:, 8, :], bn_w[:, 9, :])
                step(v.tensor_tensor(out=bn_s[:, i, 0, :], in0=bn_w[:, 8, :], in1=bn_gb[:, i, 0, :], op=ALU.mult))
                step(v.tensor_tensor(out=bn_w[:, 9, :], in0=bn_w[:, 5, :], in1=bn_s[:, i, 0, :], op=ALU.mult))
                v.tensor_tensor(out=bn_s[:, i, 1, :], in0=bn_gb[:, i, 1, :], in1=bn_w[:, 9, :],
                                op=ALU.subtract).then_inc(S["bn_done"], 1)
                dve.wait_ge(S["bn_done"], i + 1)
                step.phase()

            offs = bn_s[0:3, :, 1, :]
            step(v.tensor_copy(t_part[:, 0], offs))
            step(v.tensor_tensor(out=t_rest[:, 0], in0=offs, in1=t_part[:, 0], op=ALU.subtract))
            step(v.tensor_copy(t_part[:, 1], t_rest[:, 0]))
            step(v.tensor_tensor(out=t_rest[:, 1], in0=t_rest[:, 0], in1=t_part[:, 1], op=ALU.subtract))
            step(v.tensor_copy(t_part[:, 2], t_rest[:, 1]))
            step(v.tensor_scalar(out=t_sel[:, 0], in0=t_part[:, 0], scalar1=ident[0:3, 0:1], scalar2=None,
                                 op0=ALU.mult))
            for k in (1, 2):
                step(v.scalar_tensor_tensor(out=t_sel[:, k], in0=t_part[:, k], scalar=ident[0:3, k:k + 1],
                                            in1=t_sel[:, k - 1], op0=ALU.mult, op1=ALU.add))
            for i in range(2):
                v.tensor_copy(t_row[:, i], t_sel[:, 2, i].unsqueeze(1).to_broadcast([3, GC, D]))\
                    .then_inc(S["f_rows"], 1)

            def f_mean(m, b):
                dve.wait_ge(S[f"f_x{b}"], (m - b) * 16 + 32)
                if past(m, 2):
                    dve.wait_ge(S["f_xc"], m - 1)
                step(v.tensor_reduce(out=f_stat[:, b, :], in_=cols(l_x1[b][0:P]), axis=AX.X, op=ALU.add))
                v.tensor_scalar(out=f_stat[:, b, :], in0=f_stat[:, b, :], scalar1=1.0 / D,
                                scalar2=None, op0=ALU.mult).then_inc(S["f_mean"], 1)

            def f_result(m, b):
                for q in range(Q):
                    c = slice(q * W, (q + 1) * W)
                    dve.wait_ge(S["f_h2"], Q * m + q + 1)
                    if past(m, 2):
                        dve.wait_ge(S[f"f_stored{b}"], (m - b) * 16)
                    v.tensor_tensor(out=blk[b][0:P, c], in0=x_sq[:, c], in1=psum[4 + q][0:P, :], op=ALU.add)\
                        .then_inc(S["f_added"], 1)
                dve.wait_ge(S["f_added"], Q * (m + 1))
                dve.wait_ge(S["f_keep"], m + 1)
                v.scalar_tensor_tensor(out=blk[b][0:P], in0=blk[b][0:P], scalar=0.0, in1=l_keep[b][0:P],
                                       op0=ALU.max, op1=ALU.add).then_inc(S["f_out"], 1)

            f_mean(0, 0)
            step.phase()

            def f_block(m, b):
                step.begin(m)
                if not isinstance(m, int) or m + 1 < NB:
                    f_mean(m + 1, 1 - b)
                dve.wait_ge(S["f_sq"], m + 1)
                v.tensor_reduce(out=f_stat[:, 2, :], in_=cols(l_sq[0][0:P]), axis=AX.X, op=ALU.add)\
                    .then_inc(S["f_ss"], 1)
                dve.wait_ge(S["f_ss"], m + 1)
                step(v.tensor_scalar(out=f_stat[:, 3, :], in0=f_stat[:, 2, :], scalar1=1.0 / D, scalar2=EPS,
                                     op0=ALU.mult, op1=ALU.add))
                newton(step, f_stat[:, 3, :], f_stat[:, 4, :], f_stat[:, 5, :])
                v.scalar_tensor_tensor(out=cols(l_xc[b][0:P]), in0=cols(l_xc[b][0:P]), scalar=0.0,
                                       in1=b8(f_stat[:, 4, :]), op0=ALU.max, op1=ALU.mult).then_inc(S["f_h"], 1)
                if past(m, 1):
                    f_result(m - 1, 1 - b)

            by_pairs(dve, NB, f_block)
            f_result(NB - 1, (NB - 1) % 2)

        @block.scalar
        def _(act):
            a = nc.scalar
            step = Steps(act, S["act_step"])

            def load(dst_ap, src_ap):
                act.dma_start(dst_ap, src_ap).then_inc(S["loads_w"], 16)
                n_loads[0] += 1

            n_loads = [0]
            load(w_raw[:, 0, :], mlp["W1"][0:128, :])
            for l in range(LAYERS):
                w = mlp["W1"][128:192, :] if l == 0 else mlp[f"W{l + 1}"]
                for h in range(2):
                    load(w_raw[h * D:(h + 1) * D, 1 + l, :], w)
                    load(gain[h * D:(h + 1) * D, l:l + 1], mlp[f"g{l + 1}"].unsqueeze(1))
                    load(shift[h * D:(h + 1) * D, l:l + 1], mlp[f"be{l + 1}"].unsqueeze(1))
                load(b_raw[:, l, :], mlp[f"b{l + 1}"].unsqueeze(0).to_broadcast([3, D]))
            assert n_loads[0] == N_LOADS_W

            act.wait_ge(S["edges_ready"], 1)

            def copy(o, i_):
                return a.activation(o, i_, ACT.Copy)

            def group_of(table, n):
                return table[:, :, bass.ds(GT * n, GT)]

            for n in range(2):
                copy(g_idx[:, n], group_of(end_i, n)).then_inc(S["idx_ready"], 1)

            copy(e_key[:, 0], group_of(end_f, 0)).then_inc(S["key_ready"], 1)
            act.wait_ge(S["a_rows0"], 128)
            copy(g_idx[:, 0], group_of(end_i, 2)).then_inc(S["idx_ready"], 1)

            def a_group(n, b):
                act.wait_ge(S["a_xc"], n + 1)
                a.activation(sq[:, b], xc[:, b], ACT.Square).then_inc(S["a_sq"], 1)

                def keep_sums(k):
                    t = GT * n + k
                    act.wait_ge(S["a_t"], t + 1)
                    wait(act, S["a_v"], t - 1)
                    copy(s_t[:, k % 2, :], psum[2 + k % 2][:, 0:2 * P]).then_inc(S["a_ts"], 1)

                def keep_values(k):
                    t = GT * n + k
                    act.wait_ge(S["a_v"], t + 1)
                    wait(act, S["a_scattered"], 32 * (t + 1 - 2 * GT))
                    copy(vals[:, b, k].rearrange("p e d -> p (e d)"), psum[4 + k % 2][0:P, 0:2 * D])\
                        .then_inc(S["a_vals"], 1)

                for k in range(GT + 1):
                    if k < GT:
                        keep_sums(k)
                    if k:
                        keep_values(k - 1)
                    if k == 0 and (not isinstance(n, int) or n + 1 < EG):
                        wait(act, S["a_sidx"], n)
                        copy(e_key[:, 1 - b], group_of(end_f, n + 1)).then_inc(S["key_ready"], 1)
                    if k == 2 and (not isinstance(n, int) or n + 3 < EG):
                        act.wait_ge(S[f"a_rows{1 - b}"], (n + b) * 64 + 128)
                        copy(g_idx[:, 1 - b], group_of(end_i, n + 3)).then_inc(S["idx_ready"], 1)

            by_pairs(act, EG, a_group, ahead=3)

            def x_squares(u, j, q):
                act.wait_ge(S[f"m_xcen{u}"], Q * j + q + 1)
                wait(act, S["m_xss0"], j + u)
                wait(act, S["m_xss1"], j)
                c = slice(q * W, (q + 1) * W)
                a.activation(x_sq[:, c], x_nrm[u][:, c], ACT.Square).then_inc(S[f"m_xsq{u}"], 1)

            act.wait_ge(S["a_scattered"], 32 * ECOL)
            for u in range(2):
                for q in range(Q):
                    x_squares(u, 0, q)

            def m_turn(j, jp):
                for k in range(STEPS):
                    this, before = unit(k, j), unit(k - 1, j)
                    if this:
                        u, l, _ = this
                        if l == 0:
                            for q in range(Q):
                                act.wait_ge(S[f"m_xt{u}"], Q * j + q + 1)
                                a.activation(h_t[u][:, q * W:q * W + Q * P], psum[4 * u + q][:, 0:Q * P], ACT.Relu)\
                                    .then_inc(S[f"m_hin{u}"], 1)
                        for q in range(Q):
                            if l == 0:
                                act.wait_ge(S[f"m_zy{u}"], Q * j + q + 1)
                                z = y_in[u][0:P, q * W:(q + 1) * W]
                            else:
                                act.wait_ge(S[f"m_z{u}"], nth(l, j, q))
                                z = psum[4 * u + q][0:P, :]
                            wait(act, S[f"m_zss{u}"], nth(l, j, q) - Q)
                            a.activation(z_sq[u][0:P, q * W:(q + 1) * W], z, ACT.Square)\
                                .then_inc(S[f"m_zsq{u}"], 1)
                            if l == 2 and exists(j + 1, u):
                                x_squares(u, j + 1, q)
                    if before:
                        u, l, jb = before
                        for q in range(Q):
                            act.wait_ge(S[f"m_zt{u}"], nth(l, jb, q))
                            a.activation(h_t[u][:, q * W:q * W + Q * P], psum[4 * u + q][:, 0:Q * P], ACT.Tanh,
                                         bias=shift[:, l:l + 1], scale=gain[:, l:l + 1]).then_inc(S[f"m_h{u}"], 1)

            by_pairs(act, TURNS, m_turn, ahead=3)

            for i in range(2):
                base = i * EG
                if i:
                    act.wait_ge(S["c_rows1"], EG * 64)
                    act.wait_ge(S["c_rows0"], EG * 64)
                for n in range(2):
                    copy(g_idx[:, n], group_of(end_i, n)).then_inc(S["c_idx"], 1)

                def c_slots(n, b, base=base):
                    c = n + base
                    wait(act, S["c_same"], GT * (c - 1))
                    copy(e_key[:, b], group_of(end_f, n)).then_inc(S["c_slots"], 1)
                    wait(act, S["c_att"], c - 1)
                    copy(e_at[:, b, :, 0:2], at_s[:, bass.ds(GT * n, GT), :]).then_inc(S["c_slots"], 1)

                c_slots(0, 0)
                act.wait_ge(S["c_rows0"], i * EG * 64 + 128)
                copy(g_idx[:, 0], group_of(end_i, 2)).then_inc(S["c_idx"], 1)

                def c_body(n, b, i=i, base=base, c_slots=c_slots):
                    c = n + base
                    if i == 0:
                        act.wait_ge(S["c_xc"], c + 1)
                        a.activation(sq[:, b], xc[:, b], ACT.Square).then_inc(S["c_sq"], 1)
                    act.wait_ge(S["c_att"], c + 1)
                    copy(at_t[:, b, :], psum[3][0:3 * GT, 0:P]).then_inc(S["c_atc"], 1)
                    if not isinstance(n, int) or n + 1 < EG:
                        c_slots(n + 1, 1 - b)
                    if past(n, 1):
                        c_messages(n - 1, 1 - b)
                    act.wait_ge(S["c_ht"], c + 1)
                    wait(act, S["c_z"], c)
                    a.activation(zt[:, 0:Q * P], psum[2][:, 0:Q * P], ACT.Relu).then_inc(S["c_zt"], 1)
                    if i == 0:
                        act.wait_ge(S["c_hw"], c + 1)
                        copy(h_keep[0:P, bass.ds(n * W, W)], hw[:, b].rearrange("p k e d -> p (k e d)"))\
                            .then_inc(S["c_keep"], 1)
                    if not isinstance(n, int) or n + 3 < EG:
                        act.wait_ge(S[f"c_rows{1 - b}"], i * EG * 64 + (n + b) * 64 + 128)
                        copy(g_idx[:, 1 - b], group_of(end_i, n + 3)).then_inc(S["c_idx"], 1)
                    if past(n, 1):
                        c_results(n - 1, 1 - b)

                def c_messages(n, b, base=base):
                    c = n + base
                    step.begin(n)
                    act.wait_ge(S["c_z"], c + 1)
                    wait(act, S["c_msg"], c)
                    z = psum[4 + b][0:P, :].rearrange("p (k w) -> p k w", w=128)
                    step(a.activation(act_e[:, 1], z[:, :, D:], ACT.Abs))
                    step(a.activation(act_e[:, 2], act_e[:, 1], ACT.Exp, scale=-1.0))
                    a.activation(act_e[:, 3], act_e[:, 2], ACT.Ln, bias=ones[0:P, 0:1])
                    a.activation(act_e[:, 0], z[:, :, 0:D], ACT.Exp, scale=-1.0).then_inc(S["c_act"], 1)

                def c_results(n, b, base=base):
                    c = n + base
                    wait(act, S["c_scattered"], 16 * GT * (c - 1))
                    copy(s_idx[:, b, 0], to_i[:, bass.ds(GT * n, GT)]).then_inc(S["c_sidx"], 1)
                    act.wait_ge(S["c_v"], GT * (c + 1))
                    copy(vals[:, b, :, 0, :], psum[6][0:P, 0:GT * D].rearrange("p (k d) -> p k d", d=D))\
                        .then_inc(S["c_vals"], 1)

                by_pairs(act, EG, c_body, ahead=3)
                c_messages(EG - 1, (EG - 1) % 2)
                c_results(EG - 1, (EG - 1) % 2)
                step.phase()

            def f_square(m, b):
                act.wait_ge(S["f_xc"], m + 1)
                wait(act, S["f_ss"], m)
                a.activation(l_sq[0][0:P], l_xc[b][0:P], ACT.Square).then_inc(S["f_sq"], 1)

            def f_keep(m, b):
                if past(m, 2):
                    act.wait_ge(S["f_out"], m - 1)
                copy(l_keep[b][0:P], l_x1[b][0:P]).then_inc(S["f_keep"], 1)

            f_square(0, 0)
            f_keep(0, 0)

            def f_second(m):
                for q in range(Q):
                    act.wait_ge(S["f_sum"], Q * m + q + 1)
                    if past(m, 1):
                        act.wait_ge(S["f_added"], Q * (m - 1) + q + 1)
                    a.activation(x_sq[:, q * W:(q + 1) * W], psum[q][0:P, :], ACT.Relu).then_inc(S["f_h2"], 1)

            def f_block(m, b):
                if past(m, 1):
                    f_second(m - 1)
                if not isinstance(m, int) or m + 1 < NB:
                    f_square(m + 1, 1 - b)
                    f_keep(m + 1, 1 - b)

            by_pairs(act, NB, f_block)
            f_second(NB - 1)

        @block.tensor
        def _(pe):
            t_ = nc.tensor
            pe.wait_ge(S["iota_done"], 3)
            pe.wait_ge(S["w_ready"], 1)
            idp = ident[0:P, 0:P]

            def key_row(b, e, k, bank, at_c):
                return t_.matmul(bank[0:P, at_c:at_c + P], e_key[:, b, e, k:k + 1].to_broadcast([P, P]), idp,
                                 start=True, stop=True)

            def a_keys(n, b, tiles):
                for k in tiles:
                    wait(pe, S["a_same"], 2 * (GT * n + k) - 2)
                    for e in range(2):
                        last = key_row(b, e, k, psum[k % 2], e * P)
                    last.then_inc(S["a_r"], 1)

            pe.wait_ge(S["key_ready"], 1)
            a_keys(0, 0, (0, 1))

            def a_group(n, b):
                a_keys(n, b, (2, 3))
                pe.wait_ge(S["a_hw"], n + 1)

                def target_sums(k):
                    t = GT * n + k
                    pe.wait_ge(S["a_same"], 2 * t + 2)
                    wait(pe, S["a_ts"], t - 1)
                    t_.matmul(psum[2 + k % 2][0:D, 0:2 * P], hw[:, b, k, 1, :], same[:, k % 2, 0, :],
                              start=True, stop=True)
                    t_.matmul(psum[2 + k % 2][D:128, 0:2 * P], hw[:, b, k, 0, :], same[:, k % 2, 1, :],
                              start=True, stop=True).then_inc(S["a_t"], 1)

                def times_w1(k):
                    t = GT * n + k
                    pe.wait_ge(S["a_ts"], t + 1)
                    wait(pe, S["a_vals"], t - 1)
                    for e in range(2):
                        last = t_.matmul(psum[4 + k % 2][0:P, e * D:(e + 1) * D], s_t[:, k % 2, e * P:(e + 1) * P],
                                         w_cen[:, 0, :], start=True, stop=True)
                    last.then_inc(S["a_v"], 1)

                for k in range(GT + 1):
                    if k < GT:
                        target_sums(k)
                    if k:
                        times_w1(k - 1)
                if not isinstance(n, int) or n + 1 < EG:
                    pe.wait_ge(S["key_ready"], n + 2)
                    a_keys(n + 1, 1 - b, (0, 1))

            by_pairs(pe, EG, a_group)

            pe.wait_ge(S["a_scattered"], 32 * ECOL)

            def four(bank, source, q, n):
                for a in range(Q):
                    if n == P:
                        last = t_.transpose(bank[:, a * P:(a + 1) * P],
                                            source[0:P, q * W + a * 128:q * W + (a + 1) * 128], idp)
                    else:
                        last = t_.transpose(bank[0:P, a * 128:(a + 1) * 128],
                                            source[:, q * W + a * P:q * W + (a + 1) * P], ident[:, :])
                return last

            def m_turn(j, jp):
                for k in range(STEPS):
                    u, l = k % 2, k // 2
                    bank = psum[4 * u:4 * u + 4]
                    if l == 0 and exists(j - 1, u):
                        for q in range(Q):
                            pe.wait_ge(S[f"m_h{u}"], nth(LAYERS - 1, j - 1, q))
                            four(bank[q], h_t[u], q, 128).then_inc(S[f"m_back{u}"], 1)
                    if exists(j, u):
                        if l == 0:
                            for q in range(Q):
                                pe.wait_ge(S[f"m_xnrm{u}"], Q * j + q + 1)
                                wait(pe, S[f"m_out{u}"], Q * (j - 1) + q + 1 if past(j, 1) else 0)
                                four(bank[q], x_nrm[u], q, P).then_inc(S[f"m_xt{u}"], 1)
                        for q in range(Q):
                            if l == 0:
                                pe.wait_ge(S[f"m_hin{u}"], Q * j + q + 1)
                            else:
                                pe.wait_ge(S[f"m_h{u}"], nth(l - 1, j, q))
                            t_.matmul(bank[q][0:P, :], ones3[:, 0:P], b_row[:, l].rearrange("p c d -> p (c d)"),
                                      start=True, stop=False)
                            for a in range(Q):
                                last = t_.matmul(bank[q][0:P, a * 128:(a + 1) * 128],
                                                 h_t[u][:, q * W + a * P:q * W + (a + 1) * P], w_blk[:, l, :],
                                                 start=False, stop=(a == Q - 1))
                            last.then_inc(S[f"m_z{u}"], 1)
                    before = unit(k - 1, j)
                    if before:
                        ub, lb, jb = before
                        for q in range(Q):
                            pe.wait_ge(S[f"m_zn{ub}"], nth(lb, jb, q))
                            four(psum[4 * ub + q], z_nrm[ub], q, P).then_inc(S[f"m_zt{ub}"], 1)

            by_pairs(pe, TURNS, m_turn, ahead=3)

            for i in range(2):
                base = i * EG
                if i == 0:
                    pe.wait_ge(S["loads_conv"], 16 * N_LOADS_CONV)
                    for u in range(2):
                        pe.wait_ge(S[f"m_out{u}"], STREAM[u] * Q)
                else:
                    pe.wait_ge(S["bn_done"], 1)

                def c_keys(n, b, tiles, base=base):
                    for k in tiles:
                        wait(pe, S["c_same"], GT * (n + base) + k - 1)
                        key_row(b, 0, k, psum[k % 2], 0).then_inc(S["c_r"], 1)

                pe.wait_ge(S["c_slots"], 2 * base + 2)
                c_keys(0, 0, (0, 1))

                def c_front(n, b, i=i, base=base, c_keys=c_keys):
                    c = n + base
                    c_keys(n, b, (2, 3))
                    wait(pe, S["c_atc"], c)
                    t_.transpose(psum[3][0:3 * GT, 0:P], e_at[:, b].rearrange("p k a -> p (k a)"), idp)\
                        .then_inc(S["c_att"], 1)
                    pe.wait_ge(S["c_hw"], c + 1)
                    wait(pe, S["c_zt"], c)
                    for k in range(GT):
                        last = t_.transpose(psum[2][:, k * P:(k + 1) * P],
                                            hw[:, b, k].rearrange("p e d -> p (e d)"), idp)
                    last.then_inc(S["c_ht"], 1)
                    pe.wait_ge(S["c_atc"], c + 1)
                    wait(pe, S["c_msg"], c - 1)
                    t_.matmul(psum[4 + b][0:P, :], at_t[:, b, :], w_at[:, i, :], start=True, stop=False)
                    pe.wait_ge(S["c_zt"], c + 1)
                    for k in range(GT):
                        last = t_.matmul(psum[4 + b][0:P, k * 128:(k + 1) * 128], zt[:, k * P:(k + 1) * P],
                                         w_fs[:, i, :], start=False, stop=(k == GT - 1))
                    last.then_inc(S["c_z"], 1)
                    if not isinstance(n, int) or n + 1 < EG:
                        pe.wait_ge(S["c_slots"], 2 * c + 4)
                        c_keys(n + 1, 1 - b, (0, 1))

                def c_back(n, b, base=base):
                    c = n + base
                    pe.wait_ge(S["c_msg"], c + 1)
                    flat = msg[:, b].rearrange("p k d -> p (k d)")
                    for h in range(2):
                        t_.matmul(psum[7][:, 0:1], flat[:, h * 128:(h + 1) * 128], ones[0:P, 0:1],
                                  start=not past(n, 1) and h == 0,
                                  stop=isinstance(n, int) and n == EG - 1 and h == 1)
                    wait(pe, S["c_vals"], c)
                    for k in range(GT):
                        pe.wait_ge(S["c_same"], GT * c + k + 1)
                        t_.matmul(psum[6][0:P, k * D:(k + 1) * D], same[:, k // 2, k % 2, b * P:(b + 1) * P], msg[:, b, k, :],
                                  start=True, stop=True).then_inc(S["c_v"], 1)

                one_behind(pe, EG, c_front, c_back)
                pe.wait_ge(S["c_same"], GT * EG * (i + 1))

                def d_block(m, b, i=i):
                    for j in range(BLK // 2):
                        if j % (BLK // 4) == 0:
                            pe.wait_ge(S[f"d_in{b}{j * 4 // BLK}"], i * D_PER[b] + (m - b) * 16 + 32)
                        pair_ = blk[b][0:P, j * 128:(j + 1) * 128]
                        last = t_.matmul(psum[0][:, 0:128], pair_, pair_, start=not past(m, 1) and j == 0,
                                         stop=isinstance(m, int) and m == NB - 1 and j == BLK // 2 - 1)
                        if j % (BLK // 4) == BLK // 4 - 1:
                            last.then_inc(S["d_used"], 1)

                by_pairs(pe, NB, d_block)
                pe.wait_ge(S["bn_ready"], 2 * (i + 1))
                for h in range(2):
                    last = t_.matmul(psum[1][0:P, h * 128:(h + 1) * 128], ones[:, 0:P], bn_x[:, h], start=True,
                                     stop=True)
                last.then_inc(S["bn_sum"], 1)

            pe.wait_ge(S["f_rows"], 2)

            def f_block(m, b):
                for q in range(Q):
                    c = slice(q * W, (q + 1) * W)
                    if past(m, 1):
                        pe.wait_ge(S["f_added"], Q * (m - 1) + q + 1)
                    pe.wait_ge(S["f_p"], 2 * m + 1)
                    for i in range(2):
                        t_.matmul(psum[4 * i + q][0:P, :], ones3[:, 0:P], t_row[:, i].rearrange("p c d -> p (c d)"),
                                  start=True, stop=False)
                    t_.matmul(psum[q][0:P, :], idp, l_a1[b][0:P, c], start=False, stop=False)
                    pe.wait_ge(S["f_h"], m + 1)
                    t_.matmul(psum[q][0:P, :], idp, l_xc[b][0:P, c], start=False, stop=True)
                    pe.wait_ge(S["f_p"], 2 * m + 2)
                    t_.matmul(psum[4 + q][0:P, :], idp, l_a2[b][0:P, c], start=False, stop=True)\
                        .then_inc(S["f_sum"], 1)

            by_pairs(pe, NB, f_block)


_MLP = [f"{n}{l}" for l in range(1, 5) for n in ("W", "b", "g", "be")]
_CONV = ["Wf", "bf", "Ws", "bs", "gamma", "beta"]


def kernel(**inputs):
    import numpy as np
    import concourse.bacc as bacc
    from concourse.bass_utils import run_bass_kernel_spmd

    nc = bacc.Bacc("TRN2", target_bir_lowering=False, num_devices=1)
    arrays, aps = {}, {}
    for name, value in inputs.items():
        a = np.ascontiguousarray(value)
        arrays[f"in_{name}"] = a
        aps[name] = nc.dram_tensor(f"in_{name}", a.shape, mybir.dt.from_np(a.dtype), kind="ExternalInput").ap()
    out = nc.dram_tensor("out", (N, D), F32, kind="ExternalOutput").ap()
    tables = [nc.dram_tensor(name, (NT, D), F32).ap() for name in ("y_tab", "x1_tab", "agg1_tab", "agg2_tab")]
    gnn_kernel(nc, aps["x"], aps["src"], aps["dst"], aps["edge_attr_2"], aps["edge_weight"],
               {k: aps[f"L0_gnn_{k}"] for k in _MLP},
               [{k: aps[f"L1_gnn_{k}{i}"] for k in _CONV} for i in (1, 2)],
               out, tables[0], tables[1], tables[2:])
    r = run_bass_kernel_spmd(nc, [arrays], core_ids=[0])
    return r.results[0]["out"]
```
